# Optimizing a Trainium2 kernel written in Bass

```python
import numpy as np
import jax
import jax.numpy as jnp

def _softmax(x, axis=-1):
    return jax.nn.softmax(x, axis=axis)

def _gelu(x):
    return jax.nn.gelu(x, approximate=True)

def _silu(x):
    return jax.nn.silu(x)

def _sigmoid(x):
    return jax.nn.sigmoid(x)

def _layernorm(x, axis=-1, eps=1e-05):
    m = jnp.mean(x, axis=axis, keepdims=True)
    v = jnp.var(x, axis=axis, keepdims=True)
    return (x - m) / jnp.sqrt(v + eps)

def _scatter_add(tgt, idx, src, axis=0):
    return tgt.at[idx].add(src)

def _segment_sum(src, seg, n):
    return jax.ops.segment_sum(src, seg, n)
kernel_name = 'mk_xattn_ffn_d2_seqx_r4_30d0ad'

def setup_inputs(seed: int=0):
    np.random.seed(seed)
    _w = jnp.asarray

    def _rec_inputs():
        import jax
        import jax.numpy as jnp
        _rk = jax.random.key(seed)
        x = -0.0002928 + 1 * jax.random.normal(jax.random.fold_in(_rk, 1), (4, 1024, 256), jnp.float32)
        _lenS = 1024 - jax.random.randint(jax.random.fold_in(_rk, 7), (4,), 0, max(1, 1024 // 4) + 1, jnp.int32)
        _lenS2 = 77 - jax.random.randint(jax.random.fold_in(_rk, 8), (4,), 0, max(1, 77 // 4) + 1, jnp.int32)
        _ctx_768P = jax.random.normal(jax.random.fold_in(_rk, 11), (4, 16, 192), jnp.float32)
        _ctx_768c = jax.random.dirichlet(jax.random.fold_in(_rk, 511), 0.3 * jnp.ones((16,), jnp.float32), (4, 77))
        _ctx_768t = jnp.einsum('bsk,bkd->bsd', _ctx_768c, _ctx_768P)
        _ctx_768t = _ctx_768t * jax.lax.rsqrt(jnp.mean(jnp.square(_ctx_768t)) + 1e-12) * 0.953939
        ctx_768 = -0.00055796 + 0.999787 * (_ctx_768t + 0.3 * jax.random.normal(jax.random.fold_in(_rk, 611), (4, 77, 192), jnp.float32))
        return (x, ctx_768)
    x, ctx_768 = _rec_inputs()

    def _L0_xattn_setup():
        import jax, jax.numpy as jnp
        import numpy as np
        HEADS = 16
        DIM_HEAD = 64
        key = jax.random.key(seed)
        ks = jax.random.split(key, 7)
        b, n, m = (2, 512, 256)
        query_dim, context_dim = (256, 192)
        inner = HEADS * DIM_HEAD
        s_q = 1.0 / np.sqrt(query_dim)
        s_c = 1.0 / np.sqrt(context_dim)
        s_i = 1.0 / np.sqrt(inner)
        return {'x': jax.random.normal(ks[0], (b, n, query_dim), jnp.float32), 'context': jax.random.normal(ks[1], (b, m, context_dim), jnp.float32), 'Wq': jax.random.normal(ks[2], (query_dim, inner), jnp.float32) * s_q, 'Wk': jax.random.normal(ks[3], (context_dim, inner), jnp.float32) * s_c, 'Wv': jax.random.normal(ks[4], (context_dim, inner), jnp.float32) * s_c, 'Wo': jax.random.normal(ks[5], (inner, query_dim), jnp.float32) * s_i, 'bo': jax.random.normal(ks[6], (query_dim,), jnp.float32) * 0.01}
    _L0_xattn_all = _L0_xattn_setup()
    _L0_xattn_in = {k: v for k, v in _L0_xattn_all.items() if k in ('Wq', 'Wk', 'Wv', 'Wo', 'bo')}
    del _L0_xattn_all

    def _L0_ffn_setup():
        import jax, jax.numpy as jnp
        import numpy as np
        D = 256
        H = 192
        E = 8
        K = 2
        NS = 2
        ROUTE_SCALE = 1.0

        def _gated_mlp(x, w1, w2):
            h = x @ w1.T
            y, g = jnp.split(h, 2, axis=-1)
            return y * jax.nn.silu(g) @ w2.T
        key = jax.random.key(seed)
        ks = jax.random.split(key, 6)
        s = 0.02
        return {'x': jax.random.normal(ks[0], (2, 256, D), jnp.float32), 'gate_w': jax.random.normal(ks[1], (E, D), jnp.float32) * s, 'W1': jax.random.normal(ks[2], (E, 2 * H, D), jnp.float32) * s, 'W2': jax.random.normal(ks[3], (E, D, H), jnp.float32) * s, 'Ws1': jax.random.normal(ks[4], (2 * NS * H, D), jnp.float32) * s, 'Ws2': jax.random.normal(ks[5], (D, NS * H), jnp.float32) * s}
    _L0_ffn_all = _L0_ffn_setup()
    _L0_ffn_in = {k: v for k, v in _L0_ffn_all.items() if k in ('gate_w', 'W1', 'W2', 'Ws1', 'Ws2')}
    del _L0_ffn_all

    def _L1_xattn_setup():
        import jax, jax.numpy as jnp
        import numpy as np
        QUERY_DIM, KV_DIM, EMBED_DIM, NUM_HEADS = (256, 192, 256, 16)
        HEAD_DIM = EMBED_DIM // NUM_HEADS
        SCALE = HEAD_DIM ** (-0.5)
        LN_EPS = 1e-05

        def _l2norm(x, eps=1e-12):
            n = jnp.sqrt(jnp.sum(x * x, axis=-1, keepdims=True))
            return x / jnp.maximum(n, eps)
        key = jax.random.key(seed)
        ks = jax.random.split(key, 12)
        B, Nq, Nk = (2, 512, 512)
        s = lambda d: 1.0 / np.sqrt(d)
        return {'query': jax.random.normal(ks[0], (B, Nq, QUERY_DIM), jnp.float32), 'key': jax.random.normal(ks[1], (B, Nk, KV_DIM), jnp.float32), 'value': jax.random.normal(ks[2], (B, Nk, KV_DIM), jnp.float32), 'Wq': jax.random.normal(ks[3], (QUERY_DIM, EMBED_DIM), jnp.float32) * s(QUERY_DIM), 'bq': jnp.zeros((EMBED_DIM,), jnp.float32), 'Wk': jax.random.normal(ks[4], (KV_DIM, EMBED_DIM), jnp.float32) * s(KV_DIM), 'bk': jnp.zeros((EMBED_DIM,), jnp.float32), 'Wv': jax.random.normal(ks[5], (KV_DIM, EMBED_DIM), jnp.float32) * s(KV_DIM), 'bv': jnp.zeros((EMBED_DIM,), jnp.float32), 'Wo': jax.random.normal(ks[6], (EMBED_DIM, EMBED_DIM), jnp.float32) * s(EMBED_DIM), 'bo': jnp.zeros((EMBED_DIM,), jnp.float32), 'ln_gamma': jnp.ones((EMBED_DIM,), jnp.float32), 'ln_beta': jnp.zeros((EMBED_DIM,), jnp.float32)}
    _L1_xattn_all = _L1_xattn_setup()
    _L1_xattn_in = {k: v for k, v in _L1_xattn_all.items() if k in ('Wq', 'bq', 'Wk', 'bk', 'Wv', 'bv', 'Wo', 'bo', 'ln_gamma', 'ln_beta')}
    del _L1_xattn_all

    def _L1_ffn_setup():
        import jax, jax.numpy as jnp
        import numpy as np
        FP8_MAX = 448.0

        def quant_fp8(x):
            amax = jnp.max(jnp.abs(x)).astype(jnp.float32)
            scale = jnp.minimum(FP8_MAX / jnp.maximum(amax, 1e-12), FP8_MAX)
            x_fp8 = jnp.clip(x * scale, -FP8_MAX, FP8_MAX).astype(jnp.float8_e4m3fn)
            return (x_fp8, 1.0 / scale)
        key = jax.random.key(seed)
        k1, k2, k3 = jax.random.split(key, 3)
        B, S, IN, OUT = (4, 2048, 256, 256)
        input = jax.random.normal(k1, (B, S, IN), dtype=jnp.float32)
        bound = 1.0 / np.sqrt(IN)
        weight = jax.random.uniform(k2, (OUT, IN), dtype=jnp.float32, minval=-bound, maxval=bound)
        bias = jax.random.uniform(k3, (OUT,), dtype=jnp.float32, minval=-bound, maxval=bound)
        return {'input': input, 'weight': weight, 'bias': bias}
    _L1_ffn_all = _L1_ffn_setup()
    _L1_ffn_in = {k: v for k, v in _L1_ffn_all.items() if k in ('weight', 'bias')}
    del _L1_ffn_all
    return {'x': x, 'ctx_768': ctx_768, 'L0_xattn_Wq': _L0_xattn_in['Wq'], 'L0_xattn_Wk': _L0_xattn_in['Wk'], 'L0_xattn_Wv': _L0_xattn_in['Wv'], 'L0_xattn_Wo': _L0_xattn_in['Wo'], 'L0_xattn_bo': _L0_xattn_in['bo'], 'L0_ffn_gate_w': _L0_ffn_in['gate_w'], 'L0_ffn_W1': _L0_ffn_in['W1'], 'L0_ffn_W2': _L0_ffn_in['W2'], 'L0_ffn_Ws1': _L0_ffn_in['Ws1'], 'L0_ffn_Ws2': _L0_ffn_in['Ws2'], 'L1_xattn_Wq': _L1_xattn_in['Wq'], 'L1_xattn_bq': _L1_xattn_in['bq'], 'L1_xattn_Wk': _L1_xattn_in['Wk'], 'L1_xattn_bk': _L1_xattn_in['bk'], 'L1_xattn_Wv': _L1_xattn_in['Wv'], 'L1_xattn_bv': _L1_xattn_in['bv'], 'L1_xattn_Wo': _L1_xattn_in['Wo'], 'L1_xattn_bo': _L1_xattn_in['bo'], 'L1_xattn_ln_gamma': _L1_xattn_in['ln_gamma'], 'L1_xattn_ln_beta': _L1_xattn_in['ln_beta'], 'L1_ffn_weight': _L1_ffn_in['weight'], 'L1_ffn_bias': _L1_ffn_in['bias']}

def reference(x, ctx_768, L0_xattn_Wq, L0_xattn_Wk, L0_xattn_Wv, L0_xattn_Wo, L0_xattn_bo, L0_ffn_gate_w, L0_ffn_W1, L0_ffn_W2, L0_ffn_Ws1, L0_ffn_Ws2, L1_xattn_Wq, L1_xattn_bq, L1_xattn_Wk, L1_xattn_bk, L1_xattn_Wv, L1_xattn_bv, L1_xattn_Wo, L1_xattn_bo, L1_xattn_ln_gamma, L1_xattn_ln_beta, L1_ffn_weight, L1_ffn_bias):
    import jax
    import jax.numpy as jnp

    def _L0_xattn_ref(x, context, Wq, Wk, Wv, Wo, bo):
        import jax, jax.numpy as jnp
        import numpy as np
        HEADS = 16
        DIM_HEAD = 64
        b, n, _ = x.shape
        h, d = (HEADS, DIM_HEAD)
        scale = d ** (-0.5)
        q = (x @ Wq).reshape(b, n, h, d).transpose(0, 2, 1, 3)
        k = (context @ Wk).reshape(b, -1, h, d).transpose(0, 2, 1, 3)
        v = (context @ Wv).reshape(b, -1, h, d).transpose(0, 2, 1, 3)
        sim = jnp.einsum('bhid,bhjd->bhij', q, k) * scale
        attn = jax.nn.softmax(sim, axis=-1)
        out = jnp.einsum('bhij,bhjd->bhid', attn, v)
        out = out.transpose(0, 2, 1, 3).reshape(b, n, h * d)
        return out @ Wo + bo

    def _L0_ffn_ref(x, gate_w, W1, W2, Ws1, Ws2):
        import jax, jax.numpy as jnp
        import numpy as np
        D = 256
        H = 192
        E = 8
        K = 2
        NS = 2
        ROUTE_SCALE = 1.0

        def _gated_mlp(x, w1, w2):
            h = x @ w1.T
            y, g = jnp.split(h, 2, axis=-1)
            return y * jax.nn.silu(g) @ w2.T
        x_shape = x.shape
        xf = x.reshape(-1, D)
        T = xf.shape[0]
        scores = jax.nn.softmax((xf @ gate_w.T).astype(jnp.float32), axis=-1)
        top_vals, top_idx = jax.lax.top_k(scores, K)
        weights = (top_vals * ROUTE_SCALE).astype(x.dtype)
        w_dense = jnp.zeros((T, E), x.dtype).at[jnp.arange(T)[:, None], top_idx].set(weights)
        h = jnp.einsum('td,ehd->teh', xf, W1)
        y, g = jnp.split(h, 2, axis=-1)
        eo = jnp.einsum('teh,edh->ted', y * jax.nn.silu(g), W2)
        z = jnp.einsum('te,ted->td', w_dense, eo)
        z = z + _gated_mlp(xf, Ws1, Ws2)
        return z.reshape(x_shape)

    def _L1_xattn_ref(query, key, value, Wq, bq, Wk, bk, Wv, bv, Wo, bo, ln_gamma, ln_beta):
        import jax, jax.numpy as jnp
        import numpy as np
        QUERY_DIM, KV_DIM, EMBED_DIM, NUM_HEADS = (256, 192, 256, 16)
        HEAD_DIM = EMBED_DIM // NUM_HEADS
        SCALE = HEAD_DIM ** (-0.5)
        LN_EPS = 1e-05

        def _l2norm(x, eps=1e-12):
            n = jnp.sqrt(jnp.sum(x * x, axis=-1, keepdims=True))
            return x / jnp.maximum(n, eps)
        B, Nq, _ = query.shape
        Nk = key.shape[1]
        Qp = query @ Wq + bq
        K = _l2norm(key @ Wk + bk)
        V = value @ Wv + bv
        Q = _l2norm(Qp)
        Q = Q.reshape(B, Nq, NUM_HEADS, HEAD_DIM).transpose(0, 2, 1, 3)
        K = K.reshape(B, Nk, NUM_HEADS, HEAD_DIM).transpose(0, 2, 1, 3)
        V = V.reshape(B, Nk, NUM_HEADS, HEAD_DIM).transpose(0, 2, 1, 3)
        scores = jnp.einsum('bhqd,bhkd->bhqk', Q, K) * SCALE
        attn = jax.nn.softmax(scores, axis=-1)
        out = jnp.einsum('bhqk,bhkd->bhqd', attn, V)
        out = out.transpose(0, 2, 1, 3).reshape(B, Nq, EMBED_DIM)
        out = out @ Wo + bo
        x = out + Qp
        mu = jnp.mean(x, axis=-1, keepdims=True)
        var = jnp.mean((x - mu) ** 2, axis=-1, keepdims=True)
        return (x - mu) / jnp.sqrt(var + LN_EPS) * ln_gamma + ln_beta

    def _L1_ffn_ref(input, weight, bias):
        import jax, jax.numpy as jnp
        import numpy as np
        FP8_MAX = 448.0

        def quant_fp8(x):
            amax = jnp.max(jnp.abs(x)).astype(jnp.float32)
            scale = jnp.minimum(FP8_MAX / jnp.maximum(amax, 1e-12), FP8_MAX)
            x_fp8 = jnp.clip(x * scale, -FP8_MAX, FP8_MAX).astype(jnp.float8_e4m3fn)
            return (x_fp8, 1.0 / scale)
        prev_shape = input.shape
        x2d = input.reshape(-1, weight.shape[1])
        w_fp8, w_scale = quant_fp8(weight)
        x_fp8, x_scale = quant_fp8(x2d)
        acc = jnp.matmul(x_fp8.astype(jnp.float32), w_fp8.astype(jnp.float32).T)
        out2d = (acc * (x_scale * w_scale) + bias).astype(jnp.bfloat16)
        out = out2d.reshape(*prev_shape[:-1], weight.shape[0]).astype(input.dtype)
        return out
    x = x + _L0_xattn_ref(_layernorm(x, axis=-1), ctx_768, L0_xattn_Wq, L0_xattn_Wk, L0_xattn_Wv, L0_xattn_Wo, L0_xattn_bo)
    x = x + _L0_ffn_ref(_layernorm(x, axis=-1), L0_ffn_gate_w, L0_ffn_W1, L0_ffn_W2, L0_ffn_Ws1, L0_ffn_Ws2)
    x = x + _L1_xattn_ref(_layernorm(x, axis=-1), ctx_768, ctx_768, L1_xattn_Wq, L1_xattn_bq, L1_xattn_Wk, L1_xattn_bk, L1_xattn_Wv, L1_xattn_bv, L1_xattn_Wo, L1_xattn_bo, L1_xattn_ln_gamma, L1_xattn_ln_beta)
    x = x + _L1_ffn_ref(_layernorm(x, axis=-1), L1_ffn_weight, L1_ffn_bias)
    return x

_drawn_inputs = setup_inputs


def setup_inputs(seed=0):
    import zlib

    import numpy as np

    out = dict(_drawn_inputs(seed))
    spreads = {'L1_xattn_bq': (0.0, 0.652),
     'L1_xattn_bk': (0.0, 2.0),
     'L1_xattn_bv': (0.0, 0.6),
     'L1_xattn_bo': (0.0, 0.622),
     'L1_xattn_ln_gamma': (1.0, 0.568),
     'L1_xattn_ln_beta': (0.0, 0.543)}
    factors = {'L0_xattn_bo': 5.606,
     'L0_ffn_gate_w': 8.0,
     'L0_ffn_W1': 8.0,
     'L0_ffn_W2': 8.0,
     'L0_ffn_Ws1': 2.972,
     'L0_ffn_Ws2': 2.987,
     'L1_xattn_Wk': 64.0,
     'L1_ffn_bias': 8.0}
    for name, (base, spread) in spreads.items():
        noise = np.random.default_rng([zlib.crc32(name.encode()), seed]).standard_normal(out[name].shape)
        drawn = base * np.exp(spread * noise) if base else spread * noise
        out[name] = jnp.asarray(drawn.astype(out[name].dtype))
    for name, factor in factors.items():
        out[name] = (out[name] * factor).astype(out[name].dtype)
    return out
```

```python
from contextlib import ExitStack

import concourse.bass as bass
from concourse import mybir

ALU = mybir.AluOpType
ACT = mybir.ActivationFunctionType
AX_X = mybir.AxisListType.X
F32 = mybir.dt.float32
F32R = mybir.dt.float32r
BF16 = mybir.dt.bfloat16
I32 = mybir.dt.int32
ds = bass.ds

P = 128
D = 256
DC = D // P
B, N = 4, 1024
T = B * N
TB = 512
TJ = TB // P
NBLK = T // TB
BPB = N // TB
KEYS = 77
CTX = 192
CC, CP = 2, 96
CK = B * KEYS
HEADS = 16
LN_EPS = 1e-5

HI_LO_PASSES = ((0, 0), (0, 1), (1, 0))


def f32(ap):
    return ap.bitcast(F32)


def layer_norm_stats(dve, x_tile, stats, mean_var, ready_sem):
    for j in range(TJ):
        dve.bn_stats(stats[:, j, :], x_tile(j))
    dve.drain()
    for j in range(TJ):
        last = dve.bn_aggr(mean_var[:, j, :], stats[:, j, :])
    last.then_inc(ready_sem, 1)


def inverse_std(gp, g, rstd, var, eps_sem, eps_count, ready_sem):
    gp.tensor_tensor(rstd[:, :], var, g["eps"][:, :], ALU.add).then_inc(eps_sem, 1)
    gp.wait_ge(eps_sem, eps_count)
    gp.tensor_tensor(rstd[:, :], rstd[:, :], g["minus_half"][:, :], ALU.pow).then_inc(ready_sem, 1)


H0, DH0 = HEADS, 64
INNER0 = H0 * DH0
PAIRS = INNER0 // P
HK = H0 * KEYS
PAIR_COLS = 2 * KEYS
KCH = -(-HK // P)
LAST_ROWS = HK - (KCH - 1) * P
BANK_HEADS = (6, 6, 4)
BANK_HEAD0 = (0, 6, 12)
TR_GROUPS = ((0, 4), (4, 4), (8, 2))
VZ_STEP = PAIR_COLS + P
U_TERMS = [[p for p in range(PAIRS) if PAIR_COLS * p < P * (c + 1) and PAIR_COLS * (p + 1) > P * c]
           for c in range(KCH)]
M_GROUPS = [(dc, p0, np) for dc in range(DC) for p0, np in ((0, 3), (3, 3), (6, 2))]
PREP_USES = len(M_GROUPS) + KCH // 2
TILES = BPB * TJ


def attention0_weights(nc, g, w, ctx):
    sb = lambda name, shape, dt: ctx.enter_context(nc.sbuf_tensor(name, shape, dt))
    g["wqT"] = [sb(f"wqT{i}", [P, PAIRS, D], F32R) for i in range(2)]
    g["wo"] = [sb(f"wo{i}", [P, PAIRS, D], F32R) for i in range(2)]
    g["kT"] = sb("kT", [P, PAIRS, CK], F32)
    g["vT"] = sb("vT", [P, PAIRS, CK], F32)
    g["kbd"] = [sb(f"kbd{i}", [P, PAIRS, PAIR_COLS], F32R) for i in range(2)]
    g["vz"] = [sb(f"vz{i}", [P, PAIRS * VZ_STEP], F32R) for i in range(2)]
    g["bo0"] = sb("bo0", [P, D], F32)
    with ExitStack() as tmp:
        t = lambda name, shape, dt: tmp.enter_context(nc.sbuf_tensor(name, shape, dt))
        sem = lambda name: tmp.enter_context(nc.semaphore(name))
        ctxs = t("ctxs", [KEYS, B, CTX], F32)
        ctxT = [t(f"ctxT{i}", [CP, CC, CK], F32R) for i in range(2)]
        wqs = t("wqs", [P, DC, INNER0], F32)
        wos = t("wos", [P, PAIRS, D], F32)
        wks = t("wks", [CP, CC, INNER0], F32)
        wvs = t("wvs", [CP, CC, INNER0], F32)
        wk = [t(f"wk{i}", [CP, CC, INNER0], F32R) for i in range(2)]
        wv = [t(f"wv{i}", [CP, CC, INNER0], F32R) for i in range(2)]
        bank = [tmp.enter_context(nc.psum_tensor(f"w0_bank{i}", [P, 512], F32)) for i in range(8)]
        ctx_in, wq_in, wo_in, wk_in, wv_in, bo_in, x_in = (
            sem(n) for n in ("ctx_in", "wq_in", "wo_in", "wk_in", "wv_in", "bo_in", "x_in"))
        ident_zero, ident_done = sem("ident_zero"), sem("ident_done")
        w_hi, bank_mm, bank_hi, bank_lo, w_lo = (
            sem(n) for n in ("w_hi", "bank_mm", "bank_hi", "bank_lo", "w_lo"))
        k_out, v_out = sem("k_out"), sem("v_out")
        K_USE, V_USE = 6, 6 + PAIRS

        with nc.Block() as block:
            @block.sync
            def _(sp):
                sp.dma_start(ctxs[:, :, :], w["ctx_768"].rearrange("b k c -> k b c")).then_inc(ctx_in, 16)
                for dst, src, s in ((wks, w["L0_xattn_Wk"], wk_in), (wvs, w["L0_xattn_Wv"], wv_in)):
                    sp.dma_start(dst[:, :, :], src.rearrange("(c p) n -> p c n", p=CP)).then_inc(s, 16)
                sp.dma_start(wqs[:, :, :], w["L0_xattn_Wq"].rearrange("(c p) n -> p c n", p=P)).then_inc(wq_in, 16)
                sp.dma_start(wos[:, :, :], w["L0_xattn_Wo"].rearrange("(c p) n -> p c n", p=P)).then_inc(wo_in, 16)
                sp.dma_start(g["bo0"][:, :], w["L0_xattn_bo"].partition_broadcast(P)).then_inc(bo_in, 16)
                sp.dma_start(g["x"][:, :, :, :], w["x"].rearrange("b (n p j) d -> p (b n) j d", p=P, j=TJ)).then_inc(x_in, 16)
                sp.wait_ge(bo_in, 16)
                sp.wait_ge(x_in, 16)

            @block.gpsimd
            def _(gp):
                gp.memset(g["ident"][:, :], 0.0).then_inc(ident_zero, 1)
                gp.wait_ge(ident_zero, 1)
                gp.affine_select(out=g["ident"][:, :], in_=g["ident"][:, :], compare_op=ALU.not_equal, fill=1.0,
                                 base=0, pattern=[[-1, P]], channel_multiplier=1).then_inc(ident_done, 1)
                gp.memset(g["minus_half"][:, :], -0.5)
                gp.memset(g["half"][:, :], 0.5)
                gp.memset(g["eps"][:, :], LN_EPS)
                for i in range(2):
                    gp.memset(f32(g["kbd"][i][:, :, :]), 0.0)
                    gp.memset(f32(g["vz"][i][:, :]), 0.0)

            @block.scalar
            def _(act):
                act.wait_ge(wk_in, 16)
                act.activation(wk[0][:, :, :], wks[:, :, :], ACT.Copy).then_inc(w_hi, 1)
                act.wait_ge(wv_in, 16)
                act.activation(wv[0][:, :, :], wvs[:, :, :], ACT.Copy).then_inc(w_hi, 1)
                for c in range(CC):
                    act.wait_ge(bank_mm, c + 1)
                    act.activation(ctxT[0][:, c, :], bank[c][0:CP, 0:CK], ACT.Copy).then_inc(bank_hi, 1)
                for u in range(2, K_USE):
                    act.wait_ge(bank_mm, u + 1)
                    act.activation(g["wqT"][0][:, 2 * (u - 2):2 * (u - 1), :], bank[u][:, :].rearrange("p (a d) -> p a d", a=2),
                                   ACT.Copy, scale=DH0 ** -0.5).then_inc(bank_hi, 1)
                act.wait_ge(wo_in, 16)
                act.activation(g["wo"][0][:, :, :], wos[:, :, :], ACT.Copy).then_inc(w_hi, 1)
                for p in range(PAIRS):
                    act.wait_ge(bank_mm, K_USE + p + 1)
                    act.activation(g["kT"][:, p, :], bank[(K_USE + p) % 8][:, 0:CK], ACT.Copy).then_inc(k_out, 1)

            @block.vector
            def _(dve):
                dve.wait_ge(w_hi, 1)
                dve.tensor_tensor(wk[1][:, :, :], wks[:, :, :], f32(wk[0][:, :, :]), ALU.subtract).then_inc(w_lo, 1)
                dve.wait_ge(w_hi, 2)
                dve.tensor_tensor(wv[1][:, :, :], wvs[:, :, :], f32(wv[0][:, :, :]), ALU.subtract).then_inc(w_lo, 1)
                for c in range(CC):
                    dve.wait_ge(bank_hi, c + 1)
                    dve.tensor_tensor(ctxT[1][:, c, :], bank[c][0:CP, 0:CK], f32(ctxT[0][:, c, :]),
                                      ALU.subtract).then_inc(bank_lo, 1)
                for u in range(2, K_USE):
                    dve.wait_ge(bank_hi, u + 1)
                    pair2 = slice(2 * (u - 2), 2 * (u - 1))
                    dve.scalar_tensor_tensor(g["wqT"][1][:, pair2, :], bank[u][:, :].rearrange("p (a d) -> p a d", a=2),
                                             DH0 ** -0.5, f32(g["wqT"][0][:, pair2, :]), ALU.mult, ALU.subtract).then_inc(bank_lo, 1)
                dve.wait_ge(w_hi, 3)
                dve.tensor_tensor(g["wo"][1][:, :, :], wos[:, :, :], f32(g["wo"][0][:, :, :]), ALU.subtract)
                for p in range(PAIRS):
                    dve.wait_ge(bank_mm, V_USE + p + 1)
                    dve.tensor_copy(g["vT"][:, p, :], bank[(V_USE + p) % 8][:, 0:CK]).then_inc(v_out, 1)

            @block.tensor
            def _(pe):
                pe.wait_ge(ident_done, 1)
                pe.wait_ge(ctx_in, 16)
                for c in range(CC):
                    for b in range(B):
                        last = pe.transpose(bank[c][0:CP, b * KEYS:(b + 1) * KEYS], ctxs[:, b, c * CP:(c + 1) * CP],
                                            g["ident"][0:KEYS, 0:KEYS])
                    last.then_inc(bank_mm, 1)
                pe.wait_ge(wq_in, 16)
                for u in range(2, K_USE):
                    for a in range(2):
                        for dc in range(DC):
                            pair = 2 * (u - 2) + a
                            last = pe.transpose(bank[u][:, a * D + dc * P:a * D + (dc + 1) * P],
                                                wqs[:, dc, pair * P:(pair + 1) * P], g["ident"][:, :])
                    last.then_inc(bank_mm, 1)
                pe.wait_ge(w_lo, 2)
                pe.wait_ge(bank_lo, CC)
                for first_use, weight in ((K_USE, wk), (V_USE, wv)):
                    for p in range(PAIRS):
                        u = first_use + p
                        if u >= V_USE:
                            pe.wait_ge(k_out, u - 8 - K_USE + 1)
                        elif u >= 8:
                            pe.wait_ge(bank_lo, u - 8 + 1)
                        for n, (i, k) in enumerate(HI_LO_PASSES):
                            for c in range(CC):
                                last = pe.matmul(bank[u % 8][:, 0:CK], weight[i][:, c, p * P:(p + 1) * P], ctxT[k][:, c, :],
                                                 start=(n == 0 and c == 0), stop=(n == 2 and c == CC - 1))
                        last.then_inc(bank_mm, 1)


def transpose_uses0():
    order = [("x", 0, dc) for dc in range(DC)]
    for t in range(-2, TILES):
        if 0 <= t + 1 < TILES:
            order += [("p", t + 1, gr) for gr in range(len(TR_GROUPS))]
        if t == 1:
            order += [("x", 1, dc) for dc in range(DC)]
    return {use: n for n, use in enumerate(order)}


def attention0(nc, g):
    with ExitStack() as ctx:
        sb = lambda name, shape, dt: ctx.enter_context(nc.sbuf_tensor(name, shape, dt))
        sem = lambda name: ctx.enter_context(nc.semaphore(name))
        m = [sb(f"m{i}", [P, DC, HK], F32R) for i in range(2)]
        u = [sb(f"u{i}", [P, KCH, D], F32R) for i in range(2)]
        xn = sb("xn0", [P, TJ, D], F32)
        xnT = [[sb(f"xnT0_{blk}_{i}", [P, DC, TB], F32R) for i in range(2)] for blk in range(BPB)]
        stats, mean_var, rstd = sb("stats0", [P, TJ, 6], F32), sb("mean_var0", [P, TJ, 2], F32), sb("rstd0", [P, TJ], F32)
        prob = [sb(f"prob{s}", [P, HK], F32) for s in range(2)]
        probT = [[sb(f"probT{s}_{i}", [P, KCH, P], F32R) for i in range(2)] for s in range(2)]
        neg_max = [sb(f"neg_max{s}", [P, H0], F32) for s in range(2)]
        row_sum, row_inv = sb("row_sum", [P, H0], F32), [sb(f"row_inv{s}", [P, H0], F32) for s in range(2)]
        score = [[ctx.enter_context(nc.psum_tensor(f"score{s}_{k}", [P, 512], F32)) for k in range(3)] for s in range(2)]
        tr = ctx.enter_context(nc.psum_tensor("tr0", [P, 512], F32))
        acc = ctx.enter_context(nc.psum_tensor("acc0", [P, 512], F32))
        prep_bank = [score[n // 3 % 2][n % 3] for n in range(PREP_USES)]
        (bd_hi, bd_lo, prep_mm, prep_hi, prep_lo, mv_ready, eps_done, rstd_ready, xn_ready, bo_added,
         tr_mm, tr_hi, tr_lo, score_mm, max_ready, exp_done, sum_done, inv_ready, prob_ready, out_mm, out_added) = (
            sem(n + "0") for n in (
                "bd_hi", "bd_lo", "prep_mm", "prep_hi", "prep_lo", "mv_ready", "eps_done", "rstd_ready",
                "xn_ready", "bo_added", "tr_mm", "tr_hi", "tr_lo", "score_mm", "max_ready", "exp_done", "sum_done",
                "inv_ready", "prob_ready", "out_mm", "out_added"))
        USE = transpose_uses0()
        NB = len(BANK_HEADS)
        TB_BANKS = TILES * NB

        def heads(k):
            return slice(BANK_HEAD0[k], BANK_HEAD0[k] + BANK_HEADS[k])

        def cols(k):
            return slice(BANK_HEAD0[k] * KEYS, (BANK_HEAD0[k] + BANK_HEADS[k]) * KEYS)

        def probs_of(t, k):
            return prob[t % 2][:, cols(k)].rearrange("p (h k) -> p h k", k=KEYS)

        def scores_of(t, k):
            return score[t % 2][k][:, 0:BANK_HEADS[k] * KEYS].rearrange("p (h k) -> p h k", k=KEYS)

        def diagonal(i, half):
            r = slice(half * DH0, (half + 1) * DH0)
            k = g["kbd"][i][r, :, half * KEYS:(half + 1) * KEYS]
            v = g["vz"][i][r, :].rearrange("q (p w) -> q p w", w=VZ_STEP)[:, :, half * KEYS:(half + 1) * KEYS]
            return r, k, v

        with nc.Block() as block:
            @block.gpsimd
            def _(gp):
                with gp.Fori(0, B) as it:
                    def normalize(t):
                        for k in range(NB):
                            gp.wait_ge(inv_ready, it * TB_BANKS + t * NB + k + 1)
                            pr = probs_of(t, k)
                            gp.tensor_tensor(pr, pr, row_inv[t % 2][:, heads(k)].unsqueeze(2).to_broadcast([P, BANK_HEADS[k], KEYS]),
                                             ALU.mult).then_inc(prob_ready, 1)

                    def block_rstd(blk):
                        gp.wait_ge(mv_ready, it * BPB + blk + 1)
                        inverse_std(gp, g, rstd, mean_var[:, :, 1], eps_done, it * BPB + blk + 1, rstd_ready)

                    def add_bo(blk):
                        gp.wait_ge(xn_ready, it * BPB + blk + 1)
                        xb = g["x"][:, ds(it * BPB + blk, 1), :, :].rearrange("p a j d -> p (a j) d")
                        gp.tensor_tensor(xb, xb, g["bo0"][:, :].unsqueeze(1).to_broadcast([P, TJ, D]), ALU.add).then_inc(bo_added, 1)

                    block_rstd(0)
                    add_bo(0)
                    for t in range(-2, TILES):
                        if t + 2 < TILES:
                            normalize(t + 2)
                        if t == 0:
                            block_rstd(1)
                        if t == 1:
                            add_bo(1)

            @block.scalar
            def _(act):
                with act.Fori(0, B) as it:
                    for kind, src in enumerate((g["kT"], g["vT"])):
                        for half in range(2):
                            r, *dst = diagonal(0, half)
                            act.activation(dst[kind], src[r, :, ds(it * KEYS, KEYS)], ACT.Copy).then_inc(bd_hi, 1)

                    def split_x(blk):
                        for dc in range(DC):
                            act.wait_ge(tr_mm, it * len(USE) + USE["x", blk, dc] + 1)
                            act.activation(xnT[blk][0][:, dc, :], tr[:, :], ACT.Copy).then_inc(tr_hi, 1)

                    def split_p(t, gr):
                        c0, n = TR_GROUPS[gr]
                        act.wait_ge(tr_mm, it * len(USE) + USE["p", t, gr] + 1)
                        if t >= 2:
                            act.wait_ge(out_mm, it * TILES + t - 1)
                        act.activation(probT[t % 2][0][:, c0:c0 + n, :], tr[:, 0:n * P].rearrange("p (c q) -> p c q", q=P),
                                       ACT.Copy).then_inc(tr_hi, 1)

                    def exps(t, k):
                        act.wait_ge(max_ready, it * TB_BANKS + t * NB + k + 1)
                        if t >= 2 and k == 0:
                            act.wait_ge(tr_mm, it * len(USE) + USE["p", t - 2, 2] + 1)
                        for n, h in enumerate(range(BANK_HEAD0[k], BANK_HEAD0[k] + BANK_HEADS[k])):
                            last = act.activation(prob[t % 2][:, h * KEYS:(h + 1) * KEYS],
                                                  score[t % 2][k][:, n * KEYS:(n + 1) * KEYS], ACT.Exp,
                                                  bias=neg_max[t % 2][:, h:h + 1])
                        last.then_inc(exp_done, 1)

                    split_x(0)
                    for n in range(PREP_USES):
                        act.wait_ge(prep_mm, it * PREP_USES + n + 1)
                        if n < len(M_GROUPS):
                            dc, p0, np = M_GROUPS[n]
                            act.activation(m[0][:, dc, p0 * PAIR_COLS:(p0 + np) * PAIR_COLS], prep_bank[n][:, 0:np * PAIR_COLS],
                                           ACT.Copy).then_inc(prep_hi, 1)
                        else:
                            c = 2 * (n - len(M_GROUPS))
                            act.activation(u[0][:, c:c + 2, :], prep_bank[n][:, :].rearrange("p (c d) -> p c d", d=D),
                                           ACT.Copy).then_inc(prep_hi, 1)
                    for t in range(-2, TILES):
                        tr_t, ex_t = 0 <= t + 1, t + 2 < TILES
                        if tr_t and t + 1 < TILES:
                            split_p(t + 1, 0)
                            split_p(t + 1, 1)
                        if ex_t:
                            exps(t + 2, 0)
                        if tr_t and t + 1 < TILES:
                            split_p(t + 1, 2)
                        if ex_t:
                            exps(t + 2, 1)
                            exps(t + 2, 2)
                        if t == 1:
                            split_x(1)
                    act.wait_ge(out_mm, it * TILES + TILES)

            @block.vector
            def _(dve):
                with dve.Fori(0, B) as it:
                    def x_tile(blk):
                        return lambda j: g["x"][:, ds(it * BPB + blk, 1), j, :].rearrange("p a d -> p (a d)")

                    def stats_of(blk):
                        layer_norm_stats(dve, x_tile(blk), stats, mean_var, mv_ready)

                    def norm_of(blk):
                        dve.wait_ge(rstd_ready, it * BPB + blk + 1)
                        for j in range(TJ):
                            last = dve.tensor_scalar(xn[:, j, :], x_tile(blk)(j), mean_var[:, j, 0:1], rstd[:, j:j + 1],
                                                     ALU.subtract, ALU.mult)
                        last.then_inc(xn_ready, 1)

                    def split_x(blk):
                        for dc in range(DC):
                            dve.wait_ge(tr_hi, it * len(USE) + USE["x", blk, dc] + 1)
                            dve.tensor_tensor(xnT[blk][1][:, dc, :], tr[:, :], f32(xnT[blk][0][:, dc, :]),
                                              ALU.subtract).then_inc(tr_lo, 1)

                    def split_p(t, gr):
                        c0, n = TR_GROUPS[gr]
                        dve.wait_ge(tr_hi, it * len(USE) + USE["p", t, gr] + 1)
                        dve.tensor_tensor(probT[t % 2][1][:, c0:c0 + n, :], tr[:, 0:n * P].rearrange("p (c q) -> p c q", q=P),
                                          f32(probT[t % 2][0][:, c0:c0 + n, :]), ALU.subtract).then_inc(tr_lo, 1)

                    def maxima(t, k):
                        dve.wait_ge(score_mm, it * TB_BANKS + t * NB + k + 1)
                        dve.tensor_reduce(neg_max[t % 2][:, heads(k)], scores_of(t, k), AX_X, ALU.max, negate=True).then_inc(max_ready, 1)

                    def sums(t, k):
                        dve.wait_ge(exp_done, it * TB_BANKS + t * NB + k + 1)
                        dve.tensor_reduce(row_sum[:, heads(k)], probs_of(t, k), AX_X, ALU.add).then_inc(sum_done, 1)
                        dve.wait_ge(sum_done, it * TB_BANKS + t * NB + k + 1)
                        dve.reciprocal(row_inv[t % 2][:, heads(k)], row_sum[:, heads(k)]).then_inc(inv_ready, 1)

                    stats_of(0)
                    for kind, src in enumerate((g["kT"], g["vT"])):
                        for half in range(2):
                            r, *hi = diagonal(0, half)
                            r, *lo = diagonal(1, half)
                            dve.wait_ge(bd_hi, it * 4 + kind * 2 + half + 1)
                            dve.tensor_tensor(lo[kind], src[r, :, ds(it * KEYS, KEYS)], f32(hi[kind]), ALU.subtract).then_inc(bd_lo, 1)
                    norm_of(0)
                    split_x(0)
                    for n in range(PREP_USES):
                        dve.wait_ge(prep_hi, it * PREP_USES + n + 1)
                        if n < len(M_GROUPS):
                            dc, p0, np = M_GROUPS[n]
                            c = slice(p0 * PAIR_COLS, (p0 + np) * PAIR_COLS)
                            dve.tensor_tensor(m[1][:, dc, c], prep_bank[n][:, 0:np * PAIR_COLS], f32(m[0][:, dc, c]),
                                              ALU.subtract).then_inc(prep_lo, 1)
                        else:
                            c = 2 * (n - len(M_GROUPS))
                            dve.tensor_tensor(u[1][:, c:c + 2, :], prep_bank[n][:, :].rearrange("p (c d) -> p c d", d=D),
                                              f32(u[0][:, c:c + 2, :]), ALU.subtract).then_inc(prep_lo, 1)
                    for t in range(-2, TILES):
                        tr_t, ex_t = 0 <= t + 1 < TILES, t + 2 < TILES
                        if tr_t:
                            split_p(t + 1, 0)
                        if ex_t:
                            maxima(t + 2, 0)
                        if tr_t:
                            split_p(t + 1, 1)
                        if ex_t:
                            maxima(t + 2, 1)
                        if tr_t:
                            split_p(t + 1, 2)
                        if ex_t:
                            maxima(t + 2, 2)
                            for k in range(NB):
                                sums(t + 2, k)
                        if t >= 0:
                            blk, j = divmod(t, TJ)
                            dve.wait_ge(out_mm, it * TILES + t + 1)
                            if j == 0:
                                dve.wait_ge(bo_added, it * BPB + blk + 1)
                            dve.tensor_tensor(x_tile(blk)(j), acc[:, 0:D], x_tile(blk)(j), ALU.add).then_inc(out_added, 1)
                        if t == 0:
                            stats_of(1)
                            norm_of(1)
                        if t == 1:
                            split_x(1)

            @block.tensor
            def _(pe):
                with pe.Fori(0, B) as it:
                    def transpose_x(blk):
                        pe.wait_ge(xn_ready, it * BPB + blk + 1)
                        for dc in range(DC):
                            n = USE["x", blk, dc]
                            if n:
                                pe.wait_ge(tr_lo, it * len(USE) + n)
                            for j in range(TJ):
                                last = pe.transpose(tr[:, j * P:(j + 1) * P], xn[:, j, dc * P:(dc + 1) * P], g["ident"][:, :])
                            last.then_inc(tr_mm, 1)

                    def transpose_p(t, gr):
                        c0, nch = TR_GROUPS[gr]
                        pe.wait_ge(prob_ready, it * TB_BANKS + t * NB + (2, 3, 3)[gr])
                        pe.wait_ge(tr_lo, it * len(USE) + USE["p", t, gr])
                        for c in range(c0, c0 + nch):
                            w = min(P, HK - c * P)
                            last = pe.transpose(tr[0:w, (c - c0) * P:(c - c0 + 1) * P], prob[t % 2][:, c * P:c * P + w], g["ident"][:, :])
                        last.then_inc(tr_mm, 1)

                    def scores(t, k):
                        blk, j = divmod(t, TJ)
                        if t >= 2:
                            pe.wait_ge(exp_done, it * TB_BANKS + (t - 2) * NB + k + 1)
                        for n, (i, w) in enumerate(HI_LO_PASSES):
                            for dc in range(DC):
                                last = pe.matmul(score[t % 2][k][:, 0:BANK_HEADS[k] * KEYS], xnT[blk][i][:, dc, j * P:(j + 1) * P],
                                                 m[w][:, dc, cols(k)], start=(n == 0 and dc == 0), stop=(n == 2 and dc == DC - 1))
                        last.then_inc(score_mm, 1)

                    transpose_x(0)
                    pe.wait_ge(bd_lo, it * 4 + 4)
                    for n in range(PREP_USES):
                        if n >= 6:
                            pe.wait_ge(prep_lo, it * PREP_USES + n - 5)
                        if n < len(M_GROUPS):
                            dc, p0, np = M_GROUPS[n]
                            for p in range(p0, p0 + np):
                                for q, (i, k) in enumerate(HI_LO_PASSES):
                                    last = pe.matmul(prep_bank[n][:, (p - p0) * PAIR_COLS:(p - p0 + 1) * PAIR_COLS],
                                                     g["wqT"][i][:, p, dc * P:(dc + 1) * P], g["kbd"][k][:, p, :], start=(q == 0), stop=(q == 2))
                        else:
                            for a in range(2):
                                c = 2 * (n - len(M_GROUPS)) + a
                                terms = [(p, i, k) for p in U_TERMS[c] for i, k in HI_LO_PASSES]
                                for q, (p, i, k) in enumerate(terms):
                                    last = pe.matmul(prep_bank[n][:, a * D:(a + 1) * D], g["vz"][i][:, P * (c + p):P * (c + p + 1)],
                                                     g["wo"][k][:, p, :], start=(q == 0), stop=(q == len(terms) - 1))
                        last.then_inc(prep_mm, 1)
                    pe.wait_ge(prep_lo, it * PREP_USES + PREP_USES)
                    pe.wait_ge(tr_lo, it * len(USE) + USE["x", 0, DC - 1] + 1)
                    for t in range(-2, TILES):
                        for k in range(NB):
                            if 0 <= t + 1 < TILES:
                                transpose_p(t + 1, k)
                            if t + 2 < TILES:
                                if t + 2 == TJ and k == 0:
                                    pe.wait_ge(tr_lo, it * len(USE) + USE["x", 1, DC - 1] + 1)
                                scores(t + 2, k)
                        if t >= 0:
                            if t == TILES - 1:
                                pe.wait_ge(tr_lo, it * len(USE) + len(USE))
                            if t >= 1:
                                pe.wait_ge(out_added, it * TILES + t)
                            for c in range(KCH):
                                rows = min(P, HK - c * P)
                                for q, (i, k) in enumerate(HI_LO_PASSES):
                                    last = pe.matmul(acc[:, 0:D], probT[t % 2][i][0:rows, c, :], u[k][0:rows, c, :],
                                                     start=(c == 0 and q == 0), stop=(c == KCH - 1 and q == 2))
                            last.then_inc(out_mm, 1)
                        if t == 1:
                            transpose_x(1)
                    pe.wait_ge(out_added, it * TILES + TILES)


E, H2 = 8, 192
NS = 2
TOP_K = 2
ROUTED = E * H2 // P
SHARED = NS * H2 // P
HCH = ROUTED + SHARED
XPOSE4 = 4


def experts_weights(nc, g, w, ctx):
    sb = lambda name, shape, dt: ctx.enter_context(nc.sbuf_tensor(name, shape, dt))
    g["w1T"] = [sb(f"w1T{i}", [P, DC, 2, HCH, P], F32R) for i in range(2)]
    g["w2T"] = [sb(f"w2T{i}", [P, HCH, D], F32R) for i in range(2)]
    g["gateT"] = [sb(f"gateT{i}", [P, DC, E], F32R) for i in range(2)]
    g["before"] = sb("before", [P, E, E], F32)
    with ExitStack() as tmp:
        t = lambda name, shape, dt: tmp.enter_context(nc.sbuf_tensor(name, shape, dt))
        sem = lambda name: tmp.enter_context(nc.semaphore(name))
        w1s = t("w1s", [P, 2, HCH, D], F32)
        w2s = t("w2s", [P, DC, HCH * P], F32)
        gates = t("gates", [E, D], F32)
        bank = [tmp.enter_context(nc.psum_tensor(f"w1_bank{i}", [P, 512], F32)) for i in range(8)]
        gate_in, y_in, g_in, w2_in = sem("gate_in"), sem("y_in"), sem("g_in"), sem("w2_in")
        ones_done = sem("ones_done")
        bank_mm, bank_hi, bank_lo = sem("bank_mm1"), sem("bank_hi1"), sem("bank_lo1")
        w1_uses = [("w1", yg, dc, c) for yg in range(2) for c in range(0, HCH, XPOSE4) for dc in range(DC)]
        uses = [("gate",)] + w1_uses + [("w2", c) for c in range(0, HCH, 2)]

        def moved(use, n, i):
            b = bank[n % 8]
            if use[0] == "gate":
                return b[:, 0:DC * E].rearrange("p (c e) -> p c e", e=E), g["gateT"][i][:, :, :]
            if use[0] == "w1":
                _, yg, dc, c = use
                k = min(XPOSE4, HCH - c)
                return b[:, 0:k * P].rearrange("p (c h) -> p c h", h=P), g["w1T"][i][:, dc, yg, c:c + k, :]
            c = use[1]
            k = min(2, HCH - c)
            return b[:, 0:k * D].rearrange("p (c d) -> p c d", d=D), g["w2T"][i][:, c:c + k, :]

        with nc.Block() as block:
            @block.sync
            def _(sp):
                sp.dma_start(gates[:, :], w["L0_ffn_gate_w"]).then_inc(gate_in, 16)
                w1 = w["L0_ffn_W1"].rearrange("(q e) (s r) d -> s e r q d", e=2, s=2)
                ws1 = w["L0_ffn_Ws1"].rearrange("(s c p) d -> s p c d", s=2, p=P)
                half = P // 2
                for yg, s in ((0, y_in), (1, g_in)):
                    sp.dma_start(w1s[:, yg, 0:ROUTED:3, :], w1[yg, 0, 0:P]).then_inc(s, 16)
                    sp.dma_start(w1s[0:half, yg, 1:ROUTED:3, :], w1[yg, 0, P:H2]).then_inc(s, 16)
                    sp.dma_start(w1s[half:P, yg, 1:ROUTED:3, :], w1[yg, 1, 0:half]).then_inc(s, 16)
                    sp.dma_start(w1s[:, yg, 2:ROUTED:3, :], w1[yg, 1, half:H2]).then_inc(s, 16)
                    sp.dma_start(w1s[:, yg, ROUTED:HCH, :], ws1[yg]).then_inc(s, 16)
                w2s_routed = w2s[:, :, 0:E * H2].rearrange("p c (e h) -> p c e h", h=H2)
                for dc in range(DC):
                    sp.dma_start(w2s_routed[:, dc, :, :], w["L0_ffn_W2"][:, dc * P:(dc + 1) * P, :].rearrange("e p h -> p e h")).then_inc(w2_in, 16)
                sp.dma_start(w2s[:, :, E * H2:], w["L0_ffn_Ws2"].rearrange("(c p) h -> p c h", p=P)).then_inc(w2_in, 16)

            @block.gpsimd
            def _(gp):
                gp.memset(g["before"][:, :, :], 1.0).then_inc(ones_done, 1)
                gp.wait_ge(ones_done, 1)
                gp.affine_select(out=g["before"][:, :, :], in_=g["before"][:, :, :], compare_op=ALU.is_gt, fill=0.0,
                                 base=0, pattern=[[1, E], [-1, E]], channel_multiplier=0)

            @block.tensor
            def _(pe):
                for n, use in enumerate(uses):
                    b = bank[n % 8]
                    if n >= 8:
                        pe.wait_ge(bank_lo, n - 7)
                    if use[0] == "gate":
                        pe.wait_ge(gate_in, 16)
                        for dc in range(DC):
                            last = pe.transpose(b[:, dc * E:(dc + 1) * E], gates[:, dc * P:(dc + 1) * P], g["ident"][0:E, 0:E])
                    elif use[0] == "w1":
                        _, yg, dc, c0 = use
                        pe.wait_ge((y_in, g_in)[yg], 5 * 16)
                        for c in range(c0, min(c0 + XPOSE4, HCH)):
                            last = pe.transpose(b[:, (c - c0) * P:(c - c0 + 1) * P], w1s[:, yg, c, dc * P:(dc + 1) * P], g["ident"][:, :])
                    else:
                        pe.wait_ge(w2_in, 3 * 16)
                        for c in range(use[1], min(use[1] + 2, HCH)):
                            for dc in range(DC):
                                at = (c - use[1]) * D + dc * P
                                last = pe.transpose(b[:, at:at + P], w2s[:, dc, c * P:(c + 1) * P], g["ident"][:, :])
                    last.then_inc(bank_mm, 1)

            @block.scalar
            def _(act):
                for n, use in enumerate(uses):
                    src, hi = moved(use, n, 0)
                    act.wait_ge(bank_mm, n + 1)
                    act.activation(hi, src, ACT.Copy).then_inc(bank_hi, 1)

            @block.vector
            def _(dve):
                for n, use in enumerate(uses):
                    src, hi = moved(use, n, 0)
                    _, lo = moved(use, n, 1)
                    dve.wait_ge(bank_hi, n + 1)
                    dve.tensor_tensor(lo, src, f32(hi), ALU.subtract).then_inc(bank_lo, 1)


def experts(nc, g, scratch):
    with ExitStack() as ctx:
        sb = lambda name, shape, dt: ctx.enter_context(nc.sbuf_tensor(name, shape, dt))
        pb = lambda name: ctx.enter_context(nc.psum_tensor(name, [P, 512], F32))
        xn = sb("xn1", [P, TJ, D], F32)
        xnT = [[sb(f"xnT1_{s}_{i}", [P, DC, TB], F32R) for i in range(2)] for s in range(2)]
        stats, mean_var, rstd = sb("stats1", [P, TJ, 6], F32), sb("mean_var1", [P, TJ, 2], F32), sb("rstd1", [P, TJ], F32)
        logit, expv, route = (sb(n, [P, TJ, E], F32) for n in ("logit", "expv", "route"))
        gmax, gsum, ginv = (sb(n, [P, TJ], F32) for n in ("gmax", "gsum", "ginv"))
        above, tie = sb("above", [P, TJ, E, E], F32), sb("tie", [P, TJ, E, E], F32)
        rank, weight = sb("rank", [P, TJ, E], F32), sb("weight", [P, TJ, E], F32)
        weightT = sb("weightT", [E, TB], F32)
        weight_all = sb("weight_all", [P, ROUTED, TB], F32)
        gated = [sb(f"gated{s}", [P, TB], F32) for s in range(2)]
        hid = [sb(f"hid{s}", [P, TB], F32) for s in range(3)]
        hidT = [[sb(f"hidT{s}_{i}", [P, TB], F32R) for i in range(2)] for s in range(3)]
        py, pg = [pb(f"py{s}") for s in range(2)], [pb(f"pg{s}") for s in range(2)]
        acc = [pb(f"acc1_{s}") for s in range(2)]
        tr, pgate = pb("tr1"), pb("pgate")
        names = ("mv_ready", "eps_done", "rstd_ready", "xn_ready", "tr_mm", "tr_hi", "tr_lo", "gate_mm", "gmax_done", "logit_ready",
                 "expv_ready", "gsum_done", "ginv_done", "route_done", "above_done", "tie_done", "tied_done", "count_done", "rank_done",
                 "weight_ready", "wT_mm", "wT_ready", "wT_out", "w_all_in", "up_mm", "silu_done", "silu_weighted", "hid_done", "hid_hi",
                 "hid_lo", "down_mm", "acc_free")
        s = {n: ctx.enter_context(nc.semaphore(n + "1")) for n in names}

        PE_STEPS = (5, 7, 9, 13)
        ACT_STEPS = (6, 8, 11, 14)
        DVE_STEPS = (2, 4, 6, 8, 10, 12)

        def pe_next(pe, n, par, part):
            if part < DC:
                if part == 0:
                    pe.wait_ge(s["xn_ready"], n + 1)
                    pe.wait_ge(s["wT_ready"], n + 1)
                pe.wait_ge(s["tr_lo"], DC * n + part + 1)
                for j in range(TJ):
                    last = pe.transpose(tr[:, j * P:(j + 1) * P], xn[:, j, part * P:(part + 1) * P], g["ident"][:, :])
                last.then_inc(s["tr_mm"], 1)
            elif part == 2:
                pe.wait_ge(s["tr_lo"], DC * n + DC + 1)
                for j in range(TJ):
                    for q, (i, k) in enumerate(HI_LO_PASSES):
                        for dc in range(DC):
                            last = pe.matmul(pgate[:, j * E:(j + 1) * E], xnT[par][i][:, dc, j * P:(j + 1) * P], g["gateT"][k][:, dc, :],
                                             start=(q == 0 and dc == 0), stop=(q == 2 and dc == DC - 1))
                last.then_inc(s["gate_mm"], 1)
            else:
                pe.wait_ge(s["weight_ready"], n + 1)
                for j in range(TJ):
                    last = pe.transpose(tr[0:E, j * P:(j + 1) * P], weight[:, j, :], g["ident"][:, :])
                last.then_inc(s["wT_mm"], 1)

        def pe_block(pe, n, par, nxt):
            def up(c):
                if c >= 2:
                    pe.wait_ge(s["hid_done"], HCH * n + c - 1)
                for yg, out in ((0, py), (1, pg)):
                    for q, (i, k) in enumerate(HI_LO_PASSES):
                        for dc in range(DC):
                            last = pe.matmul(out[c % 2][:, :], g["w1T"][i][:, dc, yg, c, :], xnT[par][k][:, dc, :],
                                             start=(q == 0 and dc == 0), stop=(q == 2 and dc == DC - 1))
                last.then_inc(s["up_mm"], 1)

            def down(c):
                pe.wait_ge(s["hid_lo"], HCH * n + c + 1)
                if c == 0:
                    pe.wait_ge(s["acc_free"], n + 1)
                for j in range(TJ):
                    for q, (i, k) in enumerate(HI_LO_PASSES):
                        last = pe.matmul(acc[j // 2][:, (j % 2) * D:(j % 2 + 1) * D], hidT[c % 3][i][:, j * P:(j + 1) * P], g["w2T"][k][:, c, :],
                                         start=(c == 0 and q == 0 and j % 2 == 0), stop=(c == HCH - 1 and q == 2), skip_group_check=True)
                last.then_inc(s["down_mm"], 1)

            for c in range(HCH + 2):
                if c < HCH:
                    up(c)
                if c >= 2:
                    down(c - 2)
                if nxt and c in PE_STEPS:
                    pe_next(pe, n + 1, 1 - par, PE_STEPS.index(c))

        def act_next(act, n, par, part):
            if part < DC:
                act.wait_ge(s["tr_mm"], DC * n + part + 1)
                act.activation(xnT[par][0][:, part, :], tr[:, :], ACT.Copy).then_inc(s["tr_hi"], 1)
            elif part == 2:
                act.wait_ge(s["logit_ready"], n + 1)
                act.activation(expv[:, :, :], logit[:, :, :], ACT.Exp).then_inc(s["expv_ready"], 1)
            else:
                act.wait_ge(s["wT_mm"], n + 1)
                act.activation(weightT[:, :], tr[0:E, :], ACT.Copy).then_inc(s["wT_ready"], 1)

        def act_block(act, n, par, nxt):
            for c in range(HCH + 1):
                if c < HCH:
                    act.wait_ge(s["up_mm"], HCH * n + c + 1)
                    act.activation(gated[c % 2][:, :], pg[c % 2][:, :], ACT.Silu).then_inc(s["silu_done"], 1)
                if c >= 1:
                    act.wait_ge(s["hid_done"], HCH * n + c)
                    act.activation(hidT[(c - 1) % 3][0][:, :], hid[(c - 1) % 3][:, :], ACT.Copy).then_inc(s["hid_hi"], 1)
                if nxt and c in ACT_STEPS:
                    act_next(act, n + 1, 1 - par, ACT_STEPS.index(c))

        def gp_next(gp, n):
            gp.wait_ge(s["mv_ready"], n + 1)
            inverse_std(gp, g, rstd, mean_var[:, :, 1], s["eps_done"], n + 1, s["rstd_ready"])

        def gp_block(gp, n, nxt):
            gp.wait_ge(s["w_all_in"], 4 * 16 * (n + 1))
            for c in range(ROUTED):
                gp.wait_ge(s["silu_done"], HCH * n + c + 1)
                gp.tensor_tensor(gated[c % 2][:, :], gated[c % 2][:, :], weight_all[:, c, :], ALU.mult).then_inc(s["silu_weighted"], 1)
                if nxt and c == 3:
                    gp_next(gp, n + 1)

        def x_tile(n):
            return lambda j: g["x"][:, ds(n, 1), j, :].rearrange("p a d -> p (a d)")

        def dve_next(dve, n, par, part):
            if part == 0:
                layer_norm_stats(dve, x_tile(n), stats, mean_var, s["mv_ready"])
            elif part == 1:
                dve.wait_ge(s["rstd_ready"], n + 1)
                for j in range(TJ):
                    last = dve.tensor_scalar(xn[:, j, :], x_tile(n)(j), mean_var[:, j, 0:1], rstd[:, j:j + 1], ALU.subtract, ALU.mult)
                last.then_inc(s["xn_ready"], 1)
            elif part < 2 + DC:
                dc = part - 2
                dve.wait_ge(s["tr_hi"], DC * n + dc + 1)
                dve.tensor_tensor(xnT[par][1][:, dc, :], tr[:, :], f32(xnT[par][0][:, dc, :]), ALU.subtract).then_inc(s["tr_lo"], 1)
            elif part == 2 + DC:
                dve.wait_ge(s["gate_mm"], n + 1)
                logits = pgate[:, 0:TJ * E].rearrange("p (j e) -> p j e", e=E)
                dve.tensor_reduce(gmax[:, :], logits, AX_X, ALU.max).then_inc(s["gmax_done"], 1)
                dve.wait_ge(s["gmax_done"], n + 1)
                dve.tensor_tensor(logit[:, :, :], logits, gmax[:, :].unsqueeze(2).to_broadcast([P, TJ, E]),
                                  ALU.subtract).then_inc(s["logit_ready"], 1)
            else:
                dve.wait_ge(s["expv_ready"], n + 1)
                dve.tensor_reduce(gsum[:, :], expv[:, :, :], AX_X, ALU.add).then_inc(s["gsum_done"], 1)
                dve.wait_ge(s["gsum_done"], n + 1)
                dve.reciprocal(ginv[:, :], gsum[:, :]).then_inc(s["ginv_done"], 1)
                dve.wait_ge(s["ginv_done"], n + 1)
                dve.tensor_tensor(route[:, :, :], expv[:, :, :], ginv[:, :].unsqueeze(2).to_broadcast([P, TJ, E]),
                                  ALU.mult).then_inc(s["route_done"], 1)
                dve.wait_ge(s["route_done"], n + 1)
                other = route[:, :, :].unsqueeze(2).to_broadcast([P, TJ, E, E])
                own = route[:, :, :].unsqueeze(3).to_broadcast([P, TJ, E, E])
                dve.tensor_tensor(above[:, :, :, :], other, own, ALU.is_gt).then_inc(s["above_done"], 1)
                dve.tensor_tensor(tie[:, :, :, :], other, own, ALU.is_equal).then_inc(s["tie_done"], 1)
                dve.wait_ge(s["tie_done"], n + 1)
                dve.tensor_tensor(tie[:, :, :, :], tie[:, :, :, :], g["before"][:, :, :].unsqueeze(1).to_broadcast([P, TJ, E, E]),
                                  ALU.mult).then_inc(s["tied_done"], 1)
                dve.wait_ge(s["tied_done"], n + 1)
                dve.tensor_tensor(above[:, :, :, :], above[:, :, :, :], tie[:, :, :, :], ALU.add).then_inc(s["count_done"], 1)
                dve.wait_ge(s["count_done"], n + 1)
                dve.tensor_reduce(rank[:, :, :], above[:, :, :, :], AX_X, ALU.add).then_inc(s["rank_done"], 1)
                dve.wait_ge(s["rank_done"], n + 1)
                dve.scalar_tensor_tensor(weight[:, :, :], rank[:, :, :], float(TOP_K), route[:, :, :], ALU.is_lt, ALU.mult).then_inc(s["weight_ready"], 1)

        def dve_block(dve, n, par, nxt):
            for c in range(HCH + 1):
                if c < HCH:
                    if c < ROUTED:
                        dve.wait_ge(s["silu_weighted"], ROUTED * n + c + 1)
                    else:
                        dve.wait_ge(s["silu_done"], HCH * n + c + 1)
                    dve.tensor_tensor(hid[c % 3][:, :], py[c % 2][:, :], gated[c % 2][:, :], ALU.mult).then_inc(s["hid_done"], 1)
                if c >= 1:
                    dve.wait_ge(s["hid_hi"], HCH * n + c)
                    dve.tensor_tensor(hidT[(c - 1) % 3][1][:, :], hid[(c - 1) % 3][:, :], f32(hidT[(c - 1) % 3][0][:, :]),
                                      ALU.subtract).then_inc(s["hid_lo"], 1)
                if nxt and c in DVE_STEPS:
                    dve_next(dve, n + 1, 1 - par, DVE_STEPS.index(c))
            dve.wait_ge(s["down_mm"], HCH * (n + 1))
            for a in range(2):
                xa = g["x"][:, ds(n, 1), 2 * a:2 * a + 2, :].rearrange("p a j d -> p (a j d)")
                last = dve.tensor_tensor(xa, acc[a][:, :], xa, ALU.add)
            last.then_inc(s["acc_free"], 1)

        def sp_next(sp, n, first):
            transposed, written, used = (v if isinstance(v, int) else sp.to_reg(v) for v in (n + 2, 16 * (n + 1), ROUTED * n))
            sp.wait_ge(s["wT_ready"], transposed)
            sp.dma_start(scratch, weightT[:, :]).then_inc(s["wT_out"], 16)
            sp.wait_ge(s["wT_out"], written)
            if not first:
                sp.wait_ge(s["silu_weighted"], used)
            row, half = scratch.rearrange("(q e) t -> e q t", e=2), P // 2
            for dst, e in ((weight_all[:, 0:ROUTED:3, :], 0), (weight_all[0:half, 1:ROUTED:3, :], 0),
                           (weight_all[half:P, 1:ROUTED:3, :], 1), (weight_all[:, 2:ROUTED:3, :], 1)):
                sp.dma_start(dst, row[e].partition_broadcast(dst.shape[0])).then_inc(s["w_all_in"], 16)

        LOOPS = NBLK // 2 - 1

        with nc.Block() as block:
            @block.sync
            def _(sp):
                sp_next(sp, 0, True)
                with sp.Fori(0, LOOPS) as it:
                    for a in range(2):
                        sp_next(sp, 2 * it + a + 1, False)
                sp_next(sp, NBLK - 1, False)

            @block.gpsimd
            def _(gp):
                gp_next(gp, 0)
                with gp.Fori(0, LOOPS) as it:
                    for a in range(2):
                        gp_block(gp, 2 * it + a, True)
                gp_block(gp, NBLK - 2, True)
                gp_block(gp, NBLK - 1, False)

            @block.scalar
            def _(act):
                for part in range(len(ACT_STEPS)):
                    act_next(act, 0, 0, part)
                with act.Fori(0, LOOPS) as it:
                    for a in range(2):
                        act_block(act, 2 * it + a, a, True)
                act_block(act, NBLK - 2, 0, True)
                act_block(act, NBLK - 1, 1, False)

            @block.vector
            def _(dve):
                dve.sem_inc(s["acc_free"], 1)
                dve.sem_inc(s["tr_lo"], 1)
                dve.sem_inc(s["wT_ready"], 1)
                for part in range(len(DVE_STEPS)):
                    dve_next(dve, 0, 0, part)
                with dve.Fori(0, LOOPS) as it:
                    for a in range(2):
                        dve_block(dve, 2 * it + a, a, True)
                dve_block(dve, NBLK - 2, 0, True)
                dve_block(dve, NBLK - 1, 1, False)

            @block.tensor
            def _(pe):
                for part in range(len(PE_STEPS)):
                    pe_next(pe, 0, 0, part)
                with pe.Fori(0, LOOPS) as it:
                    for a in range(2):
                        pe_block(pe, 2 * it + a, a, True)
                pe_block(pe, NBLK - 2, 0, True)
                pe_block(pe, NBLK - 1, 1, False)


H3 = HEADS
DH3 = D // H3
HH = H3 // DC
HALF = HH * KEYS
C3 = -(-HALF // P)
SLOT = DH3 + 2
C3_HEADS = [(P * c // KEYS, min(HH, -(-P * (c + 1) // KEYS))) for c in range(C3)]
CMAX = max(b - a for a, b in C3_HEADS)
NORM_EPS = 1e-12


def attention1_weights(nc, g, w, ctx):
    sb = lambda name, shape, dt: ctx.enter_context(nc.sbuf_tensor(name, shape, dt))
    g["wq1"] = [sb(f"wq1_{i}", [P, DC, D], F32R) for i in range(2)]
    g["wo1"] = [sb(f"wo1_{i}", [P, DC, D], F32R) for i in range(2)]
    g["k1T"] = [sb(f"k1T_{i}", [P, DC, CK], F32R) for i in range(2)]
    g["vbd"] = [sb(f"vbd{i}", [P, B, DC, C3, CMAX, SLOT], F32R) for i in range(2)]
    g["head_rows"] = sb("head_rows", [P, HH, KEYS], F32)
    g["bq1"], g["bo1"], g["gamma"], g["beta"] = (sb(n, [P, D], F32) for n in ("bq1", "bo1", "gamma", "beta"))
    with ExitStack() as tmp:
        t = lambda name, shape, dt: tmp.enter_context(nc.sbuf_tensor(name, shape, dt))
        sem = lambda name: tmp.enter_context(nc.semaphore(name + "3w"))
        ctxs = t("ctxs1", [KEYS, B, CTX], F32)
        ctxT = [t(f"ctxT1_{i}", [CP, CC, CK], F32R) for i in range(2)]
        wqs, wos = t("wq1s", [P, DC, D], F32), t("wo1s", [P, DC, D], F32)
        wks, wvs = t("wk1s", [CP, CC, D], F32), t("wv1s", [CP, CC, D], F32)
        wk, wv = ([t(f"{n}_{i}", [CP, CC, D], F32R) for i in range(2)] for n in ("wk1", "wv1"))
        bk, bv = t("bk1", [P, D], F32), t("bv1", [P, D], F32)
        k, ksq, v = (t(n, [KEYS, B, D], F32) for n in ("k1", "k1sq", "v1"))
        vh = [t(f"v1_{i}", [KEYS, B, D], F32R) for i in range(2)]
        knorm, kinv = t("knorm", [KEYS, B], F32), t("kinv", [KEYS, B], F32)
        spread_f = t("spread_f", [KEYS, C3 * P], F32)
        spread = t("spread", [KEYS, C3 * P], F32R)
        row_head = t("row_head", [P, C3, HH], F32)
        bank = [tmp.enter_context(nc.psum_tensor(f"w3_bank{i}", [P, 512], F32)) for i in range(8)]
        ctx_in, wk_in, wv_in, wq_in, wo_in, bias_in, row_in = (
            sem(n) for n in ("ctx_in", "wk_in", "wv_in", "wq_in", "wo_in", "bias_in", "row_in"))
        fill, shaped, w_hi, w_lo, mm, hi, lo, k_out, sq_out, norm_out, norm_pow, norm_max, inv_out, kn_out, v_out, vh_hi, vh_lo, v_zero, spread_out, vbd_out = (
            sem(n) for n in ("fill", "shaped", "w_hi", "w_lo", "mm", "hi", "lo", "k_out", "sq_out", "norm_out", "norm_pow", "norm_max",
                             "inv_out", "kn_out", "v_out", "vh_hi", "vh_lo", "v_zero", "spread_out", "vbd_out"))
        SPREAD = [(b, c) for b in range(B) for c in range(C3)]

        def ones_where(gp, tile, pattern_base_cm, n):
            for m, (base, cm, pattern) in enumerate(pattern_base_cm):
                gp.wait_ge(fill if m == 0 else shaped, 4 if m == 0 else n + m)
                gp.affine_select(out=tile, in_=tile, compare_op=ALU.is_ge, fill=0.0, base=base, pattern=pattern,
                                 channel_multiplier=cm).then_inc(shaped, 1)
            return n + len(pattern_base_cm)

        with nc.Block() as block:
            @block.sync
            def _(sp):
                sp.dma_start(ctxs[:, :, :], w["ctx_768"].rearrange("b k c -> k b c")).then_inc(ctx_in, 16)
                for dst, src, p, s in ((wks, w["L1_xattn_Wk"], CP, wk_in), (wvs, w["L1_xattn_Wv"], CP, wv_in),
                                       (wqs, w["L1_xattn_Wq"], P, wq_in), (wos, w["L1_xattn_Wo"], P, wo_in)):
                    sp.dma_start(dst[:, :, :], src.rearrange("(c p) n -> p c n", p=p)).then_inc(s, 16)
                for dst, src in ((bk, w["L1_xattn_bk"]), (bv, w["L1_xattn_bv"])):
                    sp.dma_start(dst[:, :], src.partition_broadcast(P)).then_inc(bias_in, 16)
                rows = ((g["bq1"], w["L1_xattn_bq"]), (g["bo1"], w["L1_xattn_bo"]), (g["gamma"], w["L1_xattn_ln_gamma"]), (g["beta"], w["L1_xattn_ln_beta"]))
                for dst, src in rows:
                    sp.dma_start(dst[:, :], src.partition_broadcast(P)).then_inc(row_in, 16)
                sp.wait_ge(row_in, 16 * len(rows))

            @block.gpsimd
            def _(gp):
                gp.memset(g["head_rows"][:, :, :], 1.0).then_inc(fill, 1)
                gp.memset(row_head[:, :, :], 1.0).then_inc(fill, 1)
                gp.memset(spread_f[:, HALF:], 0.0).then_inc(fill, 1)
                gp.memset(spread_f[:, 0:HALF], 1.0).then_inc(fill, 1)
                n = ones_where(gp, g["head_rows"][:, :, :], ((0, 1, [[-DH3, HH], [0, KEYS]]), (DH3 - 1, -1, [[DH3, HH], [0, KEYS]])), 0)
                n = ones_where(gp, row_head[:, :, :], ((0, 1, [[P, C3], [-KEYS, HH]]), (KEYS - 1, -1, [[-P, C3], [KEYS, HH]])), n)
                n = ones_where(gp, spread_f[:, 0:HALF], ((0, 1, [[0, HH], [-1, KEYS]]), (0, -1, [[0, HH], [1, KEYS]])), n)
                for i in range(2):
                    gp.memset(f32(g["vbd"][i][:, :, :, :, :, :]), 0.0).then_inc(v_zero, 1)
                gp.wait_ge(norm_out, 1)
                gp.tensor_tensor(knorm[:, :], knorm[:, :], g["half"][0:KEYS, 0:B], ALU.pow).then_inc(norm_pow, 1)

            @block.scalar
            def _(act):
                for n, (dst, src, s) in enumerate(((wk, wks, wk_in), (wv, wvs, wv_in), (g["wq1"], wqs, wq_in), (g["wo1"], wos, wo_in))):
                    act.wait_ge(s, 16)
                    act.activation(dst[0][:, :, :], src[:, :, :], ACT.Copy).then_inc(w_hi, 1)
                for c in range(CC):
                    act.wait_ge(mm, c + 1)
                    act.activation(ctxT[0][:, c, :], bank[c][0:CP, 0:CK], ACT.Copy).then_inc(hi, 1)
                act.wait_ge(shaped, 6)
                act.activation(spread[:, :], spread_f[:, :], ACT.Copy).then_inc(spread_out, 1)
                act.wait_ge(v_out, 2)
                act.activation(vh[0][:, :, :], v[:, :, :], ACT.Copy).then_inc(vh_hi, 1)
                for f in range(DC):
                    act.wait_ge(mm, 7 + f)
                    act.activation(g["k1T"][0][:, f, :], bank[6 + f][:, 0:CK], ACT.Copy).then_inc(hi, 1)

            @block.vector
            def _(dve):
                for n, (dst, src) in enumerate(((wk, wks), (wv, wvs), (g["wq1"], wqs), (g["wo1"], wos))):
                    dve.wait_ge(w_hi, n + 1)
                    dve.tensor_tensor(dst[1][:, :, :], src[:, :, :], f32(dst[0][:, :, :]), ALU.subtract).then_inc(w_lo, 1)
                for c in range(CC):
                    dve.wait_ge(hi, c + 1)
                    dve.tensor_tensor(ctxT[1][:, c, :], bank[c][0:CP, 0:CK], f32(ctxT[0][:, c, :]), ALU.subtract).then_inc(lo, 1)
                dve.wait_ge(bias_in, 32)
                two = lambda ap: ap[0:KEYS, :].unsqueeze(1).to_broadcast([KEYS, 2, D])
                for n, (dst, bias, s) in enumerate(((k, bk, k_out), (k, bk, k_out), (v, bv, v_out), (v, bv, v_out))):
                    dve.wait_ge(mm, 2 + n + 1)
                    a = n % 2
                    dve.tensor_tensor(dst[:, 2 * a:2 * a + 2, :], bank[2 + n][0:KEYS, :].rearrange("p (b d) -> p b d", d=D), two(bias),
                                      ALU.add).then_inc(s, 1)
                dve.wait_ge(k_out, 2)
                dve.tensor_tensor(ksq[:, :, :], k[:, :, :], k[:, :, :], ALU.mult).then_inc(sq_out, 1)
                dve.wait_ge(sq_out, 1)
                dve.tensor_reduce(knorm[:, :], ksq[:, :, :], AX_X, ALU.add).then_inc(norm_out, 1)
                dve.wait_ge(norm_pow, 1)
                dve.tensor_scalar(knorm[:, :], knorm[:, :], NORM_EPS, None, ALU.max).then_inc(norm_max, 1)
                dve.wait_ge(norm_max, 1)
                dve.reciprocal(kinv[:, :], knorm[:, :]).then_inc(inv_out, 1)
                dve.wait_ge(inv_out, 1)
                dve.tensor_tensor(k[:, :, :], k[:, :, :], kinv[:, :].unsqueeze(2).to_broadcast([KEYS, B, D]), ALU.mult).then_inc(kn_out, 1)
                dve.wait_ge(vh_hi, 1)
                dve.tensor_tensor(vh[1][:, :, :], v[:, :, :], f32(vh[0][:, :, :]), ALU.subtract).then_inc(vh_lo, 1)
                for f in range(DC):
                    dve.wait_ge(hi, CC + f + 1)
                    dve.tensor_tensor(g["k1T"][1][:, f, :], bank[6 + f][:, 0:CK], f32(g["k1T"][0][:, f, :]), ALU.subtract).then_inc(lo, 1)
                dve.wait_ge(shaped, 6)
                dve.wait_ge(v_zero, 2)
                for c, (h0, h1) in enumerate(C3_HEADS):
                    dve.tensor_copy(g["vbd"][0][:, :, :, c, 0:h1 - h0, DH3],
                                    row_head[:, c, h0:h1].unsqueeze(1).unsqueeze(1).to_broadcast([P, B, DC, h1 - h0]))
                for n, (b, c) in enumerate(SPREAD):
                    h0, h1 = C3_HEADS[c]
                    dve.wait_ge(mm, 8 + n + 1)
                    for i in range(2):
                        src = bank[n % 8][:, i * D:(i + 1) * D].rearrange("p (f h d) -> p f h d", f=DC, d=DH3)[:, :, h0:h1, :]
                        keep = row_head[:, c, h0:h1].unsqueeze(1).unsqueeze(3).to_broadcast([P, DC, h1 - h0, DH3])
                        last = dve.tensor_tensor(g["vbd"][i][:, b, :, c, 0:h1 - h0, 0:DH3], src, keep, ALU.mult)
                    last.then_inc(vbd_out, 1)

            @block.tensor
            def _(pe):
                pe.wait_ge(ctx_in, 16)
                for c in range(CC):
                    for b in range(B):
                        last = pe.transpose(bank[c][0:CP, b * KEYS:(b + 1) * KEYS], ctxs[:, b, c * CP:(c + 1) * CP], g["ident"][0:KEYS, 0:KEYS])
                    last.then_inc(mm, 1)
                pe.wait_ge(lo, CC)
                for n, weight in enumerate((wk, wk, wv, wv)):
                    pe.wait_ge(w_lo, 1 + n // 2)
                    for a in range(2):
                        b = 2 * (n % 2) + a
                        for q, (i, j) in enumerate(HI_LO_PASSES):
                            for c in range(CC):
                                last = pe.matmul(bank[2 + n][0:KEYS, a * D:(a + 1) * D], ctxT[i][:, c, b * KEYS:(b + 1) * KEYS], weight[j][:, c, :],
                                                 start=(q == 0 and c == 0), stop=(q == 2 and c == CC - 1))
                    last.then_inc(mm, 1)
                pe.wait_ge(kn_out, 1)
                for f in range(DC):
                    for b in range(B):
                        last = pe.transpose(bank[6 + f][:, b * KEYS:(b + 1) * KEYS], k[:, b, f * P:(f + 1) * P], g["ident"][0:KEYS, 0:KEYS])
                    last.then_inc(mm, 1)
                pe.wait_ge(spread_out, 1)
                pe.wait_ge(vh_lo, 1)
                pe.wait_ge(lo, CC + DC)
                for n, (b, c) in enumerate(SPREAD):
                    if n >= 8:
                        pe.wait_ge(vbd_out, n - 7)
                    for i in range(2):
                        last = pe.matmul(bank[n % 8][:, i * D:(i + 1) * D], spread[:, c * P:(c + 1) * P], vh[i][:, b, :], start=True, stop=True)
                    last.then_inc(mm, 1)


def attention1(nc, g):
    with ExitStack() as ctx:
        sb = lambda name, shape, dt: ctx.enter_context(nc.sbuf_tensor(name, shape, dt))
        pb = lambda name: ctx.enter_context(nc.psum_tensor(name, [P, 512], F32))
        kbd = [sb(f"kbd1_{i}", [P, DC, HH, KEYS], F32R) for i in range(2)]
        xn = sb("xn3", [P, TJ, D], F32)
        xnT = [sb(f"xnT3_{i}", [P, DC, TB], F32R) for i in range(2)]
        stats, mean_var, rstd = sb("stats3", [P, TJ, 6], F32), sb("mean_var3", [P, TJ, 2], F32), sb("rstd3", [P, TJ], F32)
        qp, qres = [sb(f"qp{s}", [P, TJ, D], F32) for s in range(2)], [sb(f"qres{s}", [P, TJ, D], F32) for s in range(2)]
        qn, sq = sb("qn", [P, TJ, D], F32), sb("sq", [P, TJ, D], F32)
        qnorm, qinv = sb("qnorm", [P, TJ], F32), sb("qinv", [P, TJ], F32)
        qT = [[sb(f"qT{s}_{i}", [P, DC, TB], F32R) for i in range(2)] for s in range(2)]
        prob = [sb(f"prob3_{s}", [P, TB], F32) for s in range(3)]
        probT = [[sb(f"probT3_{s}_{i}", [P, TB], F32R) for i in range(2)] for s in range(3)]
        sums, o = sb("sums3", [P, TJ, H3], F32), sb("o3", [P, TJ, D], F32)
        oT = [sb(f"oT{i}", [P, DC, TB], F32R) for i in range(2)]
        y = sb("y3", [P, TJ, D], F32)
        score = [pb(f"score3_{s}") for s in range(2)]
        acc = [pb(f"acc3_{j}") for j in range(TJ)]
        tr, proj = pb("tr3"), pb("proj3")
        NC3 = DC * C3
        names = ("mv_ready", "eps_done", "rstd_ready", "xn_ready", "tr_mm", "tr_hi", "tr_lo", "proj_mm", "proj_out", "ssq_done", "root_done",
                 "norm_done", "qinv_done", "qn_ready", "qres_ready", "kbd_ready", "score_mm", "exp_done", "prob_hi", "prob_lo", "pv_mm",
                 "sums_done", "o_ready", "y_ready", "y_mv", "y_eps", "y_rstd", "yn_ready", "y_gamma", "y_beta", "x_ready", "x_seen", "f_mv", "f_eps", "f_rstd", "f_ready")
        s = {n: ctx.enter_context(nc.semaphore(n + "3")) for n in names}
        def place(n, back, front_uses, back_uses):
            if not back:
                return 0 if isinstance(n, int) and n == 0 else (front_uses + back_uses) * n - back_uses
            last = isinstance(n, int) and n == NBLK - 1
            return (front_uses + back_uses) * n + (front_uses if last else 2 * front_uses)

        def tr_use(n, kind, dc):
            return place(n, kind == 2, 2 * DC, DC) + (dc if kind == 2 else DC * kind + dc)

        def proj_use(n, kind, a):
            return place(n, kind == 1, 2, 2) + a

        two_tiles = lambda ap: ap[:, :].unsqueeze(1).to_broadcast([P, 2, D])
        four_tiles = lambda ap: ap[:, :].unsqueeze(1).to_broadcast([P, TJ, D])
        pair = lambda tile, a: tile[:, 2 * a:2 * a + 2, :]
        banked = lambda bank: bank[:, :].rearrange("p (j d) -> p j d", d=D)

        def x_tile(n):
            return lambda j: g["x"][:, ds(n, 1), j, :].rearrange("p a d -> p (a d)")

        def x_block(n):
            return g["x"][:, ds(n, 1), :, :].rearrange("p a j d -> p (a j) d")

        def pe_transpose(pe, n, kind, src):
            for dc in range(DC):
                use = tr_use(n, kind, dc)
                if not (isinstance(use, int) and use == 0):
                    pe.wait_ge(s["tr_lo"], use)
                for j in range(TJ):
                    last = pe.transpose(tr[:, j * P:(j + 1) * P], src[:, j, dc * P:(dc + 1) * P], g["ident"][:, :])
                last.then_inc(s["tr_mm"], 1)

        def pe_project(pe, n, kind, xT, weight):
            for a in range(2):
                use = proj_use(n, kind, a)
                if not (isinstance(use, int) and use == 0):
                    pe.wait_ge(s["proj_out"], use)
                for b in range(2):
                    j = 2 * a + b
                    for q, (i, k) in enumerate(HI_LO_PASSES):
                        for dc in range(DC):
                            last = pe.matmul(proj[:, b * D:(b + 1) * D], xT[i][:, dc, j * P:(j + 1) * P], weight[k][:, dc, :],
                                             start=(q == 0 and dc == 0), stop=(q == 2 and dc == DC - 1))
                last.then_inc(s["proj_mm"], 1)

        def pe_front(pe, n):
            pe.wait_ge(s["xn_ready"], n + 1)
            pe_transpose(pe, n, 0, xn)
            pe.wait_ge(s["tr_lo"], tr_use(n, 0, DC - 1) + 1)
            pe_project(pe, n, 0, xnT, g["wq1"])
            pe.wait_ge(s["qn_ready"], n + 1)
            pe_transpose(pe, n, 1, qn)

        def pe_main(pe, n, par, batch):
            pe.wait_ge(s["kbd_ready"], batch + 1)
            pe.wait_ge(s["tr_lo"], tr_use(n, 1, DC - 1) + 1)

            def scores(c):
                f, cc = divmod(c, C3)
                rows = min(P, HALF - cc * P)
                if c >= 2:
                    pe.wait_ge(s["exp_done"], NC3 * n + c - 1)
                for q, (i, k) in enumerate(HI_LO_PASSES):
                    keys = kbd[i][:, f, :, :].rearrange("p h k -> p (h k)")[:, cc * P:cc * P + rows]
                    last = pe.matmul(score[c % 2][0:rows, :], keys, qT[par][k][:, f, :], start=(q == 0), stop=(q == 2))
                last.then_inc(s["score_mm"], 1)

            def values(c):
                f, cc = divmod(c, C3)
                rows = min(P, HALF - cc * P)
                h0, h1 = C3_HEADS[cc]
                pe.wait_ge(s["prob_lo"], NC3 * n + c + 1)
                if c == 0:
                    pe.wait_ge(s["o_ready"], n + 1)
                for j in range(TJ):
                    out = acc[j][:, (f * HH + h0) * SLOT:(f * HH + h1) * SLOT]
                    for q, (i, k) in enumerate(HI_LO_PASSES):
                        v = g["vbd"][k][0:rows, ds(batch, 1), f, cc, 0:h1 - h0, :].rearrange("p a h d -> p (a h d)")
                        last = pe.matmul(out, probT[c % 3][i][0:rows, j * P:(j + 1) * P], v, start=(c == 0 and q == 0),
                                         stop=(c == NC3 - 1 and q == 2), skip_group_check=True)
                last.then_inc(s["pv_mm"], 1)

            for c in range(NC3 + 2):
                if c < NC3:
                    scores(c)
                if c >= 2:
                    values(c - 2)

        def pe_back(pe, n):
            pe.wait_ge(s["o_ready"], n + 2)
            pe_transpose(pe, n, 2, o)
            pe.wait_ge(s["tr_lo"], tr_use(n, 2, DC - 1) + 1)
            pe_project(pe, n, 1, oT, g["wo1"])

        def act_split(act, n, kind, dst):
            for dc in range(DC):
                act.wait_ge(s["tr_mm"], tr_use(n, kind, dc) + 1)
                act.activation(dst[0][:, dc, :], tr[:, :], ACT.Copy).then_inc(s["tr_hi"], 1)

        def act_front(act, n, par):
            act_split(act, n, 0, xnT)
            act.wait_ge(s["proj_out"], proj_use(n, 0, 1) + 1)
            for j in range(TJ):
                last = act.activation(sq[:, j, :], qp[par][:, j, :], ACT.Square, accum_out=qnorm[:, j:j + 1])
            last.then_inc(s["ssq_done"], 1)
            act_split(act, n, 1, qT[par])

        def act_main(act, n):
            for c in range(NC3 + 1):
                if c < NC3:
                    rows = min(P, HALF - c % C3 * P)
                    act.wait_ge(s["score_mm"], NC3 * n + c + 1)
                    act.activation(prob[c % 3][0:rows, :], score[c % 2][0:rows, :], ACT.Exp, scale=DH3 ** -0.5).then_inc(s["exp_done"], 1)
                if c >= 1:
                    rows = min(P, HALF - (c - 1) % C3 * P)
                    act.wait_ge(s["exp_done"], NC3 * n + c)
                    act.activation(probT[(c - 1) % 3][0][0:rows, :], prob[(c - 1) % 3][0:rows, :], ACT.Copy).then_inc(s["prob_hi"], 1)

        def dve_split(dve, n, kind, dst):
            for dc in range(DC):
                dve.wait_ge(s["tr_hi"], tr_use(n, kind, dc) + 1)
                dve.tensor_tensor(dst[1][:, dc, :], tr[:, :], f32(dst[0][:, dc, :]), ALU.subtract).then_inc(s["tr_lo"], 1)

        def dve_ln(dve, n):
            layer_norm_stats(dve, x_tile(n), stats, mean_var, s["mv_ready"])
            dve.wait_ge(s["rstd_ready"], n + 1)
            for j in range(TJ):
                last = dve.tensor_scalar(xn[:, j, :], x_tile(n)(j), mean_var[:, j, 0:1], rstd[:, j:j + 1], ALU.subtract, ALU.mult)
            last.then_inc(s["xn_ready"], 1)

        def dve_front(dve, n, par):
            dve_split(dve, n, 0, xnT)
            for a in range(2):
                dve.wait_ge(s["proj_mm"], proj_use(n, 0, a) + 1)
                dve.tensor_tensor(pair(qp[par], a), banked(proj), two_tiles(g["bq1"]), ALU.add).then_inc(s["proj_out"], 1)
            dve.wait_ge(s["root_done"], n + 1)
            dve.tensor_scalar(qnorm[:, :], qnorm[:, :], NORM_EPS, None, ALU.max).then_inc(s["norm_done"], 1)
            dve.wait_ge(s["norm_done"], n + 1)
            dve.reciprocal(qinv[:, :], qnorm[:, :]).then_inc(s["qinv_done"], 1)
            dve.wait_ge(s["qinv_done"], n + 1)
            for j in range(TJ):
                last = dve.tensor_scalar(qn[:, j, :], qp[par][:, j, :], qinv[:, j:j + 1], None, ALU.mult)
            last.then_inc(s["qn_ready"], 1)
            dve_split(dve, n, 1, qT[par])

        def dve_keys(dve, batch):
            for i in range(2):
                for f in range(DC):
                    keys = f32(g["k1T"][i][:, f, ds(batch * KEYS, KEYS)]).unsqueeze(1).to_broadcast([P, HH, KEYS])
                    last = dve.tensor_tensor(kbd[i][:, f, :, :], keys, g["head_rows"][:, :, :], ALU.mult)
            last.then_inc(s["kbd_ready"], 1)

        def dve_main(dve, n, nxt):
            for c in range(NC3):
                rows = min(P, HALF - c % C3 * P)
                dve.wait_ge(s["prob_hi"], NC3 * n + c + 1)
                dve.tensor_tensor(probT[c % 3][1][0:rows, :], prob[c % 3][0:rows, :], f32(probT[c % 3][0][0:rows, :]),
                                  ALU.subtract).then_inc(s["prob_lo"], 1)
                if nxt and c == 3:
                    dve_ln(dve, n + 1)
            dve.wait_ge(s["pv_mm"], NC3 * (n + 1))
            slots = [acc[j][:, 0:H3 * SLOT].rearrange("p (h d) -> p h d", d=SLOT) for j in range(TJ)]
            for j in range(TJ):
                last = dve.reciprocal(sums[:, j, :], slots[j][:, :, DH3])
            last.then_inc(s["sums_done"], 1)
            dve.wait_ge(s["sums_done"], n + 1)
            for j in range(TJ):
                last = dve.tensor_tensor(o[:, j, :].rearrange("p (h d) -> p h d", d=DH3), slots[j][:, :, 0:DH3],
                                         sums[:, j, :].unsqueeze(2).to_broadcast([P, H3, DH3]), ALU.mult)
            last.then_inc(s["o_ready"], 1)

        def dve_back(dve, n, par):
            dve_split(dve, n, 2, oT)
            dve.wait_ge(s["qres_ready"], n + 1)
            for a in range(2):
                dve.wait_ge(s["proj_mm"], proj_use(n, 1, a) + 1)
                dve.tensor_tensor(pair(y, a), banked(proj), pair(qres[par], a), ALU.add).then_inc(s["proj_out"], 1)
            dve.wait_ge(s["proj_out"], proj_use(n, 1, 1) + 1)
            layer_norm_stats(dve, lambda j: y[:, j, :], stats, mean_var, s["y_mv"])
            dve.wait_ge(s["y_rstd"], n + 1)
            for j in range(TJ):
                last = dve.tensor_scalar(y[:, j, :], y[:, j, :], mean_var[:, j, 0:1], rstd[:, j:j + 1], ALU.subtract, ALU.mult)
            last.then_inc(s["yn_ready"], 1)
            dve.wait_ge(s["x_ready"], n + 1)
            dve.sem_inc(s["x_seen"], 1)
            layer_norm_stats(dve, x_tile(n), stats, mean_var, s["f_mv"])
            dve.wait_ge(s["f_rstd"], n + 1)
            f_tile = lambda j: g["xf"][:, ds(n, 1), j, :].rearrange("p a d -> p (a d)")
            for j in range(TJ):
                last = dve.tensor_scalar(f_tile(j), x_tile(n)(j), mean_var[:, j, 0:1], rstd[:, j:j + 1], ALU.subtract, ALU.mult)
            last.then_inc(s["f_ready"], 1)
            dve.wait_ge(s["f_ready"], n + 1)
            dve.tensor_reduce(g["xf_max"][:, ds(n, 1)], g["xf"][:, ds(n, 1), :, :].rearrange("p a j d -> p a (j d)"), AX_X, ALU.max,
                              apply_absolute_value=True)

        def gp_ln(gp, n):
            gp.wait_ge(s["mv_ready"], n + 1)
            inverse_std(gp, g, rstd, mean_var[:, :, 1], s["eps_done"], n + 1, s["rstd_ready"])

        def gp_front(gp, n, par):
            gp.wait_ge(s["ssq_done"], n + 1)
            gp.tensor_tensor(qnorm[:, :], qnorm[:, :], g["half"][:, :], ALU.pow).then_inc(s["root_done"], 1)
            gp.tensor_tensor(qres[par][:, :, :], qp[par][:, :, :], four_tiles(g["bo1"]), ALU.add).then_inc(s["qres_ready"], 1)

        def gp_back(gp, n):
            gp.wait_ge(s["y_mv"], n + 1)
            inverse_std(gp, g, rstd, mean_var[:, :, 1], s["y_eps"], n + 1, s["y_rstd"])
            gp.wait_ge(s["yn_ready"], n + 1)
            gp.tensor_tensor(y[:, :, :], y[:, :, :], four_tiles(g["gamma"]), ALU.mult).then_inc(s["y_gamma"], 1)
            gp.wait_ge(s["y_gamma"], n + 1)
            gp.tensor_tensor(y[:, :, :], y[:, :, :], four_tiles(g["beta"]), ALU.add).then_inc(s["y_beta"], 1)
            gp.wait_ge(s["y_beta"], n + 1)
            gp.tensor_tensor(x_block(n), x_block(n), y[:, :, :], ALU.add).then_inc(s["x_ready"], 1)
            gp.wait_ge(s["f_mv"], n + 1)
            inverse_std(gp, g, rstd, mean_var[:, :, 1], s["f_eps"], n + 1, s["f_rstd"])

        LOOPS = B - 1

        def each_block(eng, body):
            with eng.Fori(0, LOOPS) as it:
                for a in range(BPB):
                    body(BPB * it + a, a, it, True)
            for a in range(BPB):
                body(NBLK - BPB + a, a, B - 1, a < BPB - 1)

        with nc.Block() as block:
            @block.gpsimd
            def _(gp):
                gp_ln(gp, 0)
                gp_front(gp, 0, 0)

                def body(n, par, batch, nxt):
                    if nxt:
                        gp_ln(gp, n + 1)
                        gp_front(gp, n + 1, 1 - par)
                    gp_back(gp, n)
                each_block(gp, body)

            @block.scalar
            def _(act):
                act_front(act, 0, 0)

                def body(n, par, batch, nxt):
                    act_main(act, n)
                    if nxt:
                        act_front(act, n + 1, 1 - par)
                    act_split(act, n, 2, oT)
                each_block(act, body)

            @block.vector
            def _(dve):
                dve.sem_inc(s["o_ready"], 1)
                dve_ln(dve, 0)
                dve_front(dve, 0, 0)

                def body(n, par, batch, nxt):
                    if par == 0:
                        dve_keys(dve, batch)
                    dve_main(dve, n, nxt)
                    if nxt:
                        dve_front(dve, n + 1, 1 - par)
                    dve_back(dve, n, par)
                each_block(dve, body)

            @block.tensor
            def _(pe):
                pe_front(pe, 0)

                def body(n, par, batch, nxt):
                    pe_main(pe, n, par, batch)
                    if nxt:
                        pe_front(pe, n + 1)
                    pe_back(pe, n)
                each_block(pe, body)


FP8_MAX = 448.0
AMAX_MIN = 1e-12
EXPONENT_BITS = 0x7F800000
FP8_MIN_NORMAL = 2.0 ** -6
ROUND_AT = 1.5 * 2.0 ** 20
QUANT_STEPS = 5


def quantize_step(dve, step, q, e, v, scale):
    if step == 0:
        return dve.tensor_scalar(q, v, scale, FP8_MAX, ALU.mult, ALU.min)
    if step == 1:
        return dve.tensor_scalar(e.bitcast(I32), q.bitcast(I32), EXPONENT_BITS, None, ALU.bitwise_and)
    if step == 2:
        return dve.tensor_scalar(e, e, FP8_MIN_NORMAL, ROUND_AT, ALU.max, ALU.mult)
    if step == 3:
        return dve.scalar_tensor_tensor(q, q, -FP8_MAX, e, ALU.max, ALU.add)
    return dve.tensor_tensor(q, q, e, ALU.subtract)


def quantized_ffn(nc, g, w, out):
    with ExitStack() as ctx:
        sb = lambda name, shape, dt: ctx.enter_context(nc.sbuf_tensor(name, shape, dt))
        pb = lambda name: ctx.enter_context(nc.psum_tensor(name, [P, 512], F32))
        ws, we, wq = (sb(n, [P, DC, D], F32) for n in ("ffn_ws", "ffn_we", "ffn_wq"))
        wqT = sb("ffn_wqT", [P, DC, D], BF16)
        bias = sb("ffn_bias", [P, D], F32)
        amax = sb("amax", [P, 2], F32)
        limit, scale_row = sb("limit", [2, 2], F32), sb("scale_row", [2, 2, P], F32)
        scales, dequant = sb("scales", [P, 4], F32), sb("dequant", [P, 1], F32)
        e, q = sb("ffn_e", [P, TJ, D], F32), [sb(f"ffn_q{s}", [P, TJ, D], F32) for s in range(2)]
        qT = [sb(f"ffn_qT{s}", [P, DC, TB], BF16) for s in range(2)]
        z = [sb(f"ffn_z{s}", [P, TJ, D], BF16) for s in range(2)]
        tr = [pb(f"ffn_tr{s}") for s in range(2)]
        acc = [pb(f"ffn_acc{s}") for s in range(4)]
        small = pb("ffn_small")
        names = ("w_in", "bias_in", "amax_done", "small_mm", "limit_done", "wq_step", "wq_mm",
                 "wqT_out", "q_step", "q_ready", "tr_mm", "qT_out", "mm", "z_out", "x_done", "stored")
        s = {n: ctx.enter_context(nc.semaphore(n + "4")) for n in names}

        with nc.Block() as block:
            @block.sync
            def _(sp):
                sp.dma_start(ws[:, :, :], w["L1_ffn_weight"].rearrange("(c p) d -> p c d", p=P)).then_inc(s["w_in"], 16)
                sp.dma_start(bias[:, :], w["L1_ffn_bias"].partition_broadcast(P)).then_inc(s["bias_in"], 16)
                out_blocks = out.rearrange("b (n p j) d -> p (b n) j d", p=P, j=TJ)
                for n in range(NBLK):
                    sp.wait_ge(s["x_done"], n + 1)
                    sp.dma_start(out_blocks[:, n, :, :], g["x"][:, n, :, :]).then_inc(s["stored"], 16)
                sp.wait_ge(s["stored"], 16 * NBLK)

            @block.vector
            def _(dve):
                dve.tensor_reduce(amax[:, 0:1], g["xf_max"][:, :], AX_X, ALU.max)
                dve.wait_ge(s["w_in"], 16)
                dve.tensor_reduce(amax[:, 1:2], ws[:, :, :].rearrange("p c d -> p (c d)"), AX_X, ALU.max,
                                  apply_absolute_value=True).then_inc(s["amax_done"], 1)
                dve.wait_ge(s["small_mm"], 1)
                dve.tensor_reduce(limit[:, 0:1], small[0:2, 0:P], AX_X, ALU.max).then_inc(s["limit_done"], 1)
                dve.wait_ge(s["limit_done"], 1)
                dve.tensor_scalar(limit[:, 0:1], limit[:, 0:1], AMAX_MIN, None, ALU.max).then_inc(s["limit_done"], 1)
                dve.wait_ge(s["limit_done"], 2)
                dve.reciprocal(limit[:, 0:1], limit[:, 0:1]).then_inc(s["limit_done"], 1)
                dve.wait_ge(s["limit_done"], 3)
                dve.tensor_scalar(limit[:, 0:1], limit[:, 0:1], FP8_MAX, FP8_MAX, ALU.mult, ALU.min).then_inc(s["limit_done"], 1)
                dve.wait_ge(s["limit_done"], 4)
                dve.reciprocal(limit[:, 1:2], limit[:, 0:1]).then_inc(s["limit_done"], 1)
                dve.wait_ge(s["limit_done"], 5)
                dve.tensor_copy(scale_row[:, :, :], limit[:, :].unsqueeze(2).to_broadcast([2, 2, P])).then_inc(s["limit_done"], 1)
                dve.wait_ge(s["small_mm"], 2)
                dve.tensor_copy(scales[:, :], small[:, P:P + 4]).then_inc(s["limit_done"], 1)
                dve.wait_ge(s["limit_done"], 7)
                dve.tensor_tensor(dequant[:, :], scales[:, 2:3], scales[:, 3:4], ALU.mult)
                for step in range(QUANT_STEPS):
                    if step:
                        dve.wait_ge(s["wq_step"], step)
                    quantize_step(dve, step, wq[:, :, :], we[:, :, :], ws[:, :, :], scales[:, 1:2]).then_inc(s["wq_step"], 1)
                dve.wait_ge(s["bias_in"], 16)

                dve.sem_inc(s["q_step"], 1)

                def quantize(n, par, first):
                    xf = g["xf"][:, ds(n, 1), :, :].rearrange("p a j d -> p (a j) d")
                    for step in range(QUANT_STEPS):
                        if step or not first:
                            dve.wait_ge(s["q_step"], (QUANT_STEPS) * n + step + 1)
                        if step == 0 and not first:
                            dve.wait_ge(s["tr_mm"], DC * n - DC)
                        last = quantize_step(dve, step, q[par][:, :, :], e[:, :, :], xf, scales[:, 0:1])
                        last.then_inc(s["q_step"], 1)

                def finish(n, par):
                    for a in range(2):
                        dve.wait_ge(s["mm"], 2 * n + a + 1)
                        for b in range(2):
                            j = 2 * a + b
                            last = dve.scalar_tensor_tensor(z[par][:, j, :], acc[2 * par + a][:, b * D:(b + 1) * D], dequant[:, 0:1], bias[:, :],
                                                            ALU.mult, ALU.add)
                        last.then_inc(s["z_out"], 1)

                for n in range(NBLK + 1):
                    if n < NBLK:
                        quantize(n, n % 2, n == 0)
                    if n >= 1:
                        if n >= 3:
                            dve.wait_ge(s["x_done"], n - 2)
                        finish(n - 1, (n - 1) % 2)

            @block.gpsimd
            def _(gp):
                for n in range(NBLK):
                    gp.wait_ge(s["z_out"], 2 * n + 2)
                    gp.tensor_tensor(g["x"][:, n, :, :], g["x"][:, n, :, :], z[n % 2][:, :, :], ALU.add).then_inc(s["x_done"], 1)

            @block.scalar
            def _(act):
                for c in range(DC):
                    act.wait_ge(s["wq_mm"], c + 1)
                    act.activation(wqT[:, c, :], tr[c][:, 0:D], ACT.Copy).then_inc(s["wqT_out"], 1)
                for n in range(NBLK):
                    if n >= 2:
                        act.wait_ge(s["mm"], 2 * n - 2)
                    for dc in range(DC):
                        act.wait_ge(s["tr_mm"], DC * n + dc + 1)
                        act.activation(qT[n % 2][:, dc, :], tr[dc][:, :], ACT.Copy).then_inc(s["qT_out"], 1)

            @block.tensor
            def _(pe):
                pe.wait_ge(s["amax_done"], 1)
                pe.transpose(small[0:2, 0:P], amax[:, :], g["ident"][:, :]).then_inc(s["small_mm"], 1)
                pe.wait_ge(s["limit_done"], 6)
                for i in range(2):
                    last = pe.transpose(small[:, P + 2 * i:P + 2 * i + 2], scale_row[:, i, :], g["ident"][0:2, 0:2])
                last.then_inc(s["small_mm"], 1)
                pe.wait_ge(s["wq_step"], QUANT_STEPS)
                for c in range(DC):
                    for r in range(DC):
                        last = pe.transpose(tr[c][:, r * P:(r + 1) * P], wq[:, r, c * P:(c + 1) * P], g["ident"][:, :])
                    last.then_inc(s["wq_mm"], 1)

                def transposes(n):
                    pe.wait_ge(s["q_step"], QUANT_STEPS * (n + 1) + 1)
                    for dc in range(DC):
                        if n == 0:
                            pe.wait_ge(s["wqT_out"], dc + 1)
                        else:
                            pe.wait_ge(s["qT_out"], DC * (n - 1) + dc + 1)
                        for j in range(TJ):
                            last = pe.transpose(tr[dc][:, j * P:(j + 1) * P], q[n % 2][:, j, dc * P:(dc + 1) * P], g["ident"][:, :])
                        last.then_inc(s["tr_mm"], 1)

                def products(n):
                    pe.wait_ge(s["qT_out"], DC * (n + 1))
                    if n >= 2:
                        pe.wait_ge(s["z_out"], 2 * n - 2)
                    for a in range(2):
                        for b in range(2):
                            j = 2 * a + b
                            for dc in range(DC):
                                last = pe.matmul(acc[2 * (n % 2) + a][:, b * D:(b + 1) * D], qT[n % 2][:, dc, j * P:(j + 1) * P], wqT[:, dc, :],
                                                 start=(dc == 0), stop=(dc == DC - 1))
                        last.then_inc(s["mm"], 1)

                for n in range(NBLK + 1):
                    if n < NBLK:
                        transposes(n)
                    if n >= 1:
                        products(n - 1)


def program(nc, w, out):
    with ExitStack() as ctx:
        g = {}
        sb = lambda name, shape, dt: ctx.enter_context(nc.sbuf_tensor(name, shape, dt))
        g["x"] = sb("x_res", [P, NBLK, TJ, D], F32)
        g["ident"] = sb("ident", [P, P], F32)
        g["minus_half"] = sb("minus_half", [P, TJ], F32)
        g["eps"] = sb("eps", [P, TJ], F32)
        g["half"] = sb("half", [P, TJ], F32)
        with ExitStack() as weights0:
            attention0_weights(nc, g, w, weights0)
            attention0(nc, g)
        weight_rows = nc.dram_tensor("weight_rows", (E, TB), F32, kind="Internal").ap()
        with ExitStack() as weights1:
            experts_weights(nc, g, w, weights1)
            experts(nc, g, weight_rows)
        g["xf"] = sb("xf", [P, NBLK, TJ, D], F32)
        g["xf_max"] = sb("xf_max", [P, NBLK], F32)
        with ExitStack() as weights3:
            attention1_weights(nc, g, w, weights3)
            attention1(nc, g)
        quantized_ffn(nc, g, w, out)


INPUTS = ['x', 'ctx_768', 'L0_xattn_Wq', 'L0_xattn_Wk', 'L0_xattn_Wv', 'L0_xattn_Wo', 'L0_xattn_bo', 'L0_ffn_gate_w',
          'L0_ffn_W1', 'L0_ffn_W2', 'L0_ffn_Ws1', 'L0_ffn_Ws2', 'L1_xattn_Wq', 'L1_xattn_bq', 'L1_xattn_Wk', 'L1_xattn_bk',
          'L1_xattn_Wv', 'L1_xattn_bv', 'L1_xattn_Wo', 'L1_xattn_bo', 'L1_xattn_ln_gamma', 'L1_xattn_ln_beta',
          'L1_ffn_weight', 'L1_ffn_bias']


def kernel(**inputs):
    import numpy as np
    import concourse.bacc as bacc
    from concourse.bass_utils import run_bass_kernel_spmd

    nc = bacc.Bacc("TRN2", target_bir_lowering=False, num_devices=1)
    arrays, views = {}, {}
    for name in INPUTS:
        a = np.ascontiguousarray(inputs[name])
        arrays["in_" + name] = a
        views[name] = nc.dram_tensor("in_" + name, a.shape, mybir.dt.from_np(a.dtype), kind="ExternalInput").ap()
    out = nc.dram_tensor("out", (B, N, D), F32, kind="ExternalOutput").ap()
    program(nc, views, out)
    r = run_bass_kernel_spmd(nc, [arrays], core_ids=[0])
    return r.results[0]["out"]
```

```python
from contextlib import ExitStack

import concourse.bass as bass
from concourse import mybir

ALU = mybir.AluOpType
ACT = mybir.ActivationFunctionType
AX_X = mybir.AxisListType.X
F32 = mybir.dt.float32
F32R = mybir.dt.float32r
BF16 = mybir.dt.bfloat16
I32 = mybir.dt.int32
ds = bass.ds

P = 128
D = 256
DC = D // P
B, N = 4, 1024
T = B * N
TB = 512
TJ = TB // P
NBLK = T // TB
BPB = N // TB
KEYS = 77
CTX = 192
CC, CP = 2, 96
CK = B * KEYS
HEADS = 16
LN_EPS = 1e-5

HI_LO_PASSES = ((0, 0), (0, 1), (1, 0))


def f32(ap):
    return ap.bitcast(F32)


def layer_norm_stats(dve, x_tile, stats, mean_var, ready_sem):
    for j in range(TJ):
        dve.bn_stats(stats[:, j, :], x_tile(j))
    dve.drain()
    for j in range(TJ):
        last = dve.bn_aggr(mean_var[:, j, :], stats[:, j, :])
    last.then_inc(ready_sem, 1)


def inverse_std(gp, g, rstd, var, eps_sem, eps_count, ready_sem):
    gp.tensor_tensor(rstd[:, :], var, g["eps"][:, :], ALU.add).then_inc(eps_sem, 1)
    gp.wait_ge(eps_sem, eps_count)
    gp.tensor_tensor(rstd[:, :], rstd[:, :], g["minus_half"][:, :], ALU.pow).then_inc(ready_sem, 1)


H0, DH0 = HEADS, 64
INNER0 = H0 * DH0
PAIRS = INNER0 // P
HK = H0 * KEYS
PAIR_COLS = 2 * KEYS
KCH = -(-HK // P)
LAST_ROWS = HK - (KCH - 1) * P
BANK_HEADS = (6, 6, 4)
BANK_HEAD0 = (0, 6, 12)
TR_GROUPS = ((0, 4), (4, 4), (8, 2))
VZ_STEP = PAIR_COLS + P
U_TERMS = [[p for p in range(PAIRS) if PAIR_COLS * p < P * (c + 1) and PAIR_COLS * (p + 1) > P * c]
           for c in range(KCH)]
M_GROUPS = [(dc, p0, np) for dc in range(DC) for p0, np in ((0, 3), (3, 3), (6, 2))]
PREP_USES = len(M_GROUPS) + KCH // 2
TILES = BPB * TJ


def attention0_weights(nc, g, w, ctx):
    sb = lambda name, shape, dt: ctx.enter_context(nc.sbuf_tensor(name, shape, dt))
    g["wqT"] = [sb(f"wqT{i}", [P, PAIRS, D], F32R) for i in range(2)]
    g["wo"] = [sb(f"wo{i}", [P, PAIRS, D], F32R) for i in range(2)]
    g["kT"] = sb("kT", [P, PAIRS, CK], F32)
    g["vT"] = sb("vT", [P, PAIRS, CK], F32)
    g["kbd"] = [sb(f"kbd{i}", [P, PAIRS, PAIR_COLS], F32R) for i in range(2)]
    g["vz"] = [sb(f"vz{i}", [P, PAIRS * VZ_STEP], F32R) for i in range(2)]
    g["bo0"] = sb("bo0", [P, D], F32)
    with ExitStack() as tmp:
        t = lambda name, shape, dt: tmp.enter_context(nc.sbuf_tensor(name, shape, dt))
        sem = lambda name: tmp.enter_context(nc.semaphore(name))
        ctxs = t("ctxs", [KEYS, B, CTX], F32)
        ctxT = [t(f"ctxT{i}", [CP, CC, CK], F32R) for i in range(2)]
        wqs = t("wqs", [P, DC, INNER0], F32)
        wos = t("wos", [P, PAIRS, D], F32)
        wks = t("wks", [CP, CC, INNER0], F32)
        wvs = t("wvs", [CP, CC, INNER0], F32)
        wk = [t(f"wk{i}", [CP, CC, INNER0], F32R) for i in range(2)]
        wv = [t(f"wv{i}", [CP, CC, INNER0], F32R) for i in range(2)]
        bank = [tmp.enter_context(nc.psum_tensor(f"w0_bank{i}", [P, 512], F32)) for i in range(8)]
        ctx_in, wq_in, wo_in, wk_in, wv_in, bo_in, x_in = (
            sem(n) for n in ("ctx_in", "wq_in", "wo_in", "wk_in", "wv_in", "bo_in", "x_in"))
        ident_zero, ident_done = sem("ident_zero"), sem("ident_done")
        w_hi, bank_mm, bank_hi, bank_lo, w_lo = (
            sem(n) for n in ("w_hi", "bank_mm", "bank_hi", "bank_lo", "w_lo"))
        k_out, v_out = sem("k_out"), sem("v_out")
        K_USE, V_USE = 6, 6 + PAIRS

        with nc.Block() as block:
            @block.sync
            def _(sp):
                sp.dma_start(ctxs[:, :, :], w["ctx_768"].rearrange("b k c -> k b c")).then_inc(ctx_in, 16)
                for dst, src, s in ((wks, w["L0_xattn_Wk"], wk_in), (wvs, w["L0_xattn_Wv"], wv_in)):
                    sp.dma_start(dst[:, :, :], src.rearrange("(c p) n -> p c n", p=CP)).then_inc(s, 16)
                sp.dma_start(wqs[:, :, :], w["L0_xattn_Wq"].rearrange("(c p) n -> p c n", p=P)).then_inc(wq_in, 16)
                sp.dma_start(wos[:, :, :], w["L0_xattn_Wo"].rearrange("(c p) n -> p c n", p=P)).then_inc(wo_in, 16)
                sp.dma_start(g["bo0"][:, :], w["L0_xattn_bo"].partition_broadcast(P)).then_inc(bo_in, 16)
                sp.dma_start(g["x"][:, :, :, :], w["x"].rearrange("b (n p j) d -> p (b n) j d", p=P, j=TJ)).then_inc(x_in, 16)
                sp.wait_ge(bo_in, 16)
                sp.wait_ge(x_in, 16)

            @block.gpsimd
            def _(gp):
                gp.memset(g["ident"][:, :], 0.0).then_inc(ident_zero, 1)
                gp.wait_ge(ident_zero, 1)
                gp.affine_select(out=g["ident"][:, :], in_=g["ident"][:, :], compare_op=ALU.not_equal, fill=1.0,
                                 base=0, pattern=[[-1, P]], channel_multiplier=1).then_inc(ident_done, 1)
                gp.memset(g["minus_half"][:, :], -0.5)
                gp.memset(g["half"][:, :], 0.5)
                gp.memset(g["eps"][:, :], LN_EPS)
                for i in range(2):
                    gp.memset(f32(g["kbd"][i][:, :, :]), 0.0)
                    gp.memset(f32(g["vz"][i][:, :]), 0.0)

            @block.scalar
            def _(act):
                act.wait_ge(wk_in, 16)
                act.activation(wk[0][:, :, :], wks[:, :, :], ACT.Copy).then_inc(w_hi, 1)
                act.wait_ge(wv_in, 16)
                act.activation(wv[0][:, :, :], wvs[:, :, :], ACT.Copy).then_inc(w_hi, 1)
                for c in range(CC):
                    act.wait_ge(bank_mm, c + 1)
                    act.activation(ctxT[0][:, c, :], bank[c][0:CP, 0:CK], ACT.Copy).then_inc(bank_hi, 1)
                for u in range(2, K_USE):
                    act.wait_ge(bank_mm, u + 1)
                    act.activation(g["wqT"][0][:, 2 * (u - 2):2 * (u - 1), :], bank[u][:, :].rearrange("p (a d) -> p a d", a=2),
                                   ACT.Copy, scale=DH0 ** -0.5).then_inc(bank_hi, 1)
                act.wait_ge(wo_in, 16)
                act.activation(g["wo"][0][:, :, :], wos[:, :, :], ACT.Copy).then_inc(w_hi, 1)
                for p in range(PAIRS):
                    act.wait_ge(bank_mm, K_USE + p + 1)
                    act.activation(g["kT"][:, p, :], bank[(K_USE + p) % 8][:, 0:CK], ACT.Copy).then_inc(k_out, 1)

            @block.vector
            def _(dve):
                dve.wait_ge(w_hi, 1)
                dve.tensor_tensor(wk[1][:, :, :], wks[:, :, :], f32(wk[0][:, :, :]), ALU.subtract).then_inc(w_lo, 1)
                dve.wait_ge(w_hi, 2)
                dve.tensor_tensor(wv[1][:, :, :], wvs[:, :, :], f32(wv[0][:, :, :]), ALU.subtract).then_inc(w_lo, 1)
                for c in range(CC):
                    dve.wait_ge(bank_hi, c + 1)
                    dve.tensor_tensor(ctxT[1][:, c, :], bank[c][0:CP, 0:CK], f32(ctxT[0][:, c, :]),
                                      ALU.subtract).then_inc(bank_lo, 1)
                for u in range(2, K_USE):
                    dve.wait_ge(bank_hi, u + 1)
                    pair2 = slice(2 * (u - 2), 2 * (u - 1))
                    dve.scalar_tensor_tensor(g["wqT"][1][:, pair2, :], bank[u][:, :].rearrange("p (a d) -> p a d", a=2),
                                             DH0 ** -0.5, f32(g["wqT"][0][:, pair2, :]), ALU.mult, ALU.subtract).then_inc(bank_lo, 1)
                dve.wait_ge(w_hi, 3)
                dve.tensor_tensor(g["wo"][1][:, :, :], wos[:, :, :], f32(g["wo"][0][:, :, :]), ALU.subtract)
                for p in range(PAIRS):
                    dve.wait_ge(bank_mm, V_USE + p + 1)
                    dve.tensor_copy(g["vT"][:, p, :], bank[(V_USE + p) % 8][:, 0:CK]).then_inc(v_out, 1)

            @block.tensor
            def _(pe):
                pe.wait_ge(ident_done, 1)
                pe.wait_ge(ctx_in, 16)
                for c in range(CC):
                    for b in range(B):
                        last = pe.transpose(bank[c][0:CP, b * KEYS:(b + 1) * KEYS], ctxs[:, b, c * CP:(c + 1) * CP],
                                            g["ident"][0:KEYS, 0:KEYS])
                    last.then_inc(bank_mm, 1)
                pe.wait_ge(wq_in, 16)
                for u in range(2, K_USE):
                    for a in range(2):
                        for dc in range(DC):
                            pair = 2 * (u - 2) + a
                            last = pe.transpose(bank[u][:, a * D + dc * P:a * D + (dc + 1) * P],
                                                wqs[:, dc, pair * P:(pair + 1) * P], g["ident"][:, :])
                    last.then_inc(bank_mm, 1)
                pe.wait_ge(w_lo, 2)
                pe.wait_ge(bank_lo, CC)
                for first_use, weight in ((K_USE, wk), (V_USE, wv)):
                    for p in range(PAIRS):
                        u = first_use + p
                        if u >= V_USE:
                            pe.wait_ge(k_out, u - 8 - K_USE + 1)
                        elif u >= 8:
                            pe.wait_ge(bank_lo, u - 8 + 1)
                        for n, (i, k) in enumerate(HI_LO_PASSES):
                            for c in range(CC):
                                last = pe.matmul(bank[u % 8][:, 0:CK], weight[i][:, c, p * P:(p + 1) * P], ctxT[k][:, c, :],
                                                 start=(n == 0 and c == 0), stop=(n == 2 and c == CC - 1))
                        last.then_inc(bank_mm, 1)


TR_BEGIN = [("x", 0, dc) for dc in range(DC)] + [("p", 0, gr) for gr in range(len(TR_GROUPS))]
TR_BATCH = [use for t in range(1, TILES) for use in
            [("p", t, gr) for gr in range(len(TR_GROUPS))] + ([("x", 1, dc) for dc in range(DC)] if t == 2 else [])] + TR_BEGIN


def transpose_use0(b, *use):
    if use in TR_BEGIN:
        if isinstance(b, int) and b == 0:
            return TR_BEGIN.index(use)
        return len(TR_BEGIN) + len(TR_BATCH) * (b - 1) + TR_BATCH.index(use)
    return len(TR_BEGIN) + len(TR_BATCH) * b + TR_BATCH.index(use)


def attention0(nc, g):
    with ExitStack() as ctx:
        sb = lambda name, shape, dt: ctx.enter_context(nc.sbuf_tensor(name, shape, dt))
        sem = lambda name: ctx.enter_context(nc.semaphore(name))
        m = [sb(f"m{i}", [P, DC, HK], F32R) for i in range(2)]
        u = [sb(f"u{i}", [P, KCH, D], F32R) for i in range(2)]
        xn = sb("xn0", [P, TJ, D], F32)
        xnT = [[sb(f"xnT0_{blk}_{i}", [P, DC, TB], F32R) for i in range(2)] for blk in range(BPB)]
        stats, mean_var, rstd = sb("stats0", [P, TJ, 6], F32), sb("mean_var0", [P, TJ, 2], F32), sb("rstd0", [P, TJ], F32)
        prob = [sb(f"prob{s}", [P, HK], F32) for s in range(2)]
        probT = [[sb(f"probT{s}_{i}", [P, KCH, P], F32R) for i in range(2)] for s in range(2)]
        neg_max = [sb(f"neg_max{s}", [P, H0], F32) for s in range(2)]
        row_sum, row_inv = sb("row_sum", [P, H0], F32), [sb(f"row_inv{s}", [P, H0], F32) for s in range(2)]
        score = [[ctx.enter_context(nc.psum_tensor(f"score{s}_{k}", [P, 512], F32)) for k in range(3)] for s in range(2)]
        tr = ctx.enter_context(nc.psum_tensor("tr0", [P, 512], F32))
        acc = ctx.enter_context(nc.psum_tensor("acc0", [P, 512], F32))
        prep_bank = [score[n // 3][n % 3] for n in range(len(M_GROUPS))] + [score[1][n % 3] for n in range(KCH // 2)]
        (bd_hi, bd_lo, prep_mm, prep_hi, prep_lo, mv_ready, eps_done, rstd_ready, xn_ready, bo_added,
         tr_mm, tr_hi, tr_lo, score_mm, max_ready, exp_done, sum_done, inv_ready, prob_ready, out_mm, out_added) = (
            sem(n + "0") for n in (
                "bd_hi", "bd_lo", "prep_mm", "prep_hi", "prep_lo", "mv_ready", "eps_done", "rstd_ready",
                "xn_ready", "bo_added", "tr_mm", "tr_hi", "tr_lo", "score_mm", "max_ready", "exp_done", "sum_done",
                "inv_ready", "prob_ready", "out_mm", "out_added"))
        NB = len(BANK_HEADS)
        TB_BANKS = TILES * NB

        def heads(k):
            return slice(BANK_HEAD0[k], BANK_HEAD0[k] + BANK_HEADS[k])

        def cols(k):
            return slice(BANK_HEAD0[k] * KEYS, (BANK_HEAD0[k] + BANK_HEADS[k]) * KEYS)

        def probs_of(t, k):
            return prob[t % 2][:, cols(k)].rearrange("p (h k) -> p h k", k=KEYS)

        def scores_of(t, k):
            return score[t % 2][k][:, 0:BANK_HEADS[k] * KEYS].rearrange("p (h k) -> p h k", k=KEYS)

        def diagonal(i, half):
            r = slice(half * DH0, (half + 1) * DH0)
            k = g["kbd"][i][r, :, half * KEYS:(half + 1) * KEYS]
            v = g["vz"][i][r, :].rearrange("q (p w) -> q p w", w=VZ_STEP)[:, :, half * KEYS:(half + 1) * KEYS]
            return r, k, v

        def first(b):
            return isinstance(b, int) and b == 0

        def each_batch(eng, begin, batch):
            begin(0)
            with eng.Fori(0, B - 1) as it:
                batch(it, True)
            batch(B - 1, False)

        def x_tile(b, blk):
            return lambda j: g["x"][:, ds(b * BPB + blk, 1), j, :].rearrange("p a d -> p (a d)")

        with nc.Block() as block:
            @block.gpsimd
            def _(gp):
                def normalize(b, t):
                    for k in range(NB):
                        gp.wait_ge(inv_ready, b * TB_BANKS + t * NB + k + 1)
                        pr = probs_of(t, k)
                        gp.tensor_tensor(pr, pr, row_inv[t % 2][:, heads(k)].unsqueeze(2).to_broadcast([P, BANK_HEADS[k], KEYS]),
                                         ALU.mult).then_inc(prob_ready, 1)

                def block_rstd(b, blk):
                    gp.wait_ge(mv_ready, b * BPB + blk + 1)
                    inverse_std(gp, g, rstd, mean_var[:, :, 1], eps_done, b * BPB + blk + 1, rstd_ready)

                def add_bo(b, blk):
                    gp.wait_ge(xn_ready, b * BPB + blk + 1)
                    xb = g["x"][:, ds(b * BPB + blk, 1), :, :].rearrange("p a j d -> p (a j) d")
                    gp.tensor_tensor(xb, xb, g["bo0"][:, :].unsqueeze(1).to_broadcast([P, TJ, D]), ALU.add).then_inc(bo_added, 1)

                def first_tiles(b):
                    normalize(b, 0)
                    block_rstd(b, 1)
                    normalize(b, 1)

                def begin(b):
                    block_rstd(b, 0)
                    add_bo(b, 0)
                    first_tiles(b)

                def batch(b, nxt):
                    for t in range(TILES - 2):
                        normalize(b, t + 2)
                        if t == 1:
                            add_bo(b, 1)
                        if nxt and t == 4:
                            block_rstd(b + 1, 0)
                    if nxt:
                        add_bo(b + 1, 0)
                        first_tiles(b + 1)
                each_batch(gp, begin, batch)

            @block.scalar
            def _(act):
                def diagonals(b, kind):
                    for half in range(2):
                        r, *dst = diagonal(0, half)
                        act.activation(dst[kind], (g["kT"], g["vT"])[kind][r, :, ds(b * KEYS, KEYS)], ACT.Copy).then_inc(bd_hi, 1)

                def split_x(b, blk, dc):
                    act.wait_ge(tr_mm, transpose_use0(b, "x", blk, dc) + 1)
                    act.activation(xnT[blk][0][:, dc, :], tr[:, :], ACT.Copy).then_inc(tr_hi, 1)

                def split_p(b, t, gr):
                    c0, n = TR_GROUPS[gr]
                    act.wait_ge(tr_mm, transpose_use0(b, "p", t, gr) + 1)
                    if t >= 2 or not first(b):
                        act.wait_ge(out_mm, b * TILES + t - 1)
                    act.activation(probT[t % 2][0][:, c0:c0 + n, :], tr[:, 0:n * P].rearrange("p (c q) -> p c q", q=P),
                                   ACT.Copy).then_inc(tr_hi, 1)

                def exps(b, t, k):
                    act.wait_ge(max_ready, b * TB_BANKS + t * NB + k + 1)
                    if k == 0 and t >= 2:
                        act.wait_ge(tr_mm, transpose_use0(b, "p", t - 2, 2) + 1)
                    elif k == 0 and not first(b):
                        act.wait_ge(tr_mm, transpose_use0(b - 1, "p", TILES + t - 2, 2) + 1)
                    for n, h in enumerate(range(BANK_HEAD0[k], BANK_HEAD0[k] + BANK_HEADS[k])):
                        last = act.activation(prob[t % 2][:, h * KEYS:(h + 1) * KEYS],
                                              score[t % 2][k][:, n * KEYS:(n + 1) * KEYS], ACT.Exp,
                                              bias=neg_max[t % 2][:, h:h + 1])
                    last.then_inc(exp_done, 1)

                def split_m(b, n):
                    act.wait_ge(prep_mm, b * PREP_USES + n + 1)
                    dc, p0, np = M_GROUPS[n]
                    act.activation(m[0][:, dc, p0 * PAIR_COLS:(p0 + np) * PAIR_COLS], prep_bank[n][:, 0:np * PAIR_COLS],
                                   ACT.Copy).then_inc(prep_hi, 1)

                def split_u(b):
                    for n in range(len(M_GROUPS), PREP_USES):
                        act.wait_ge(prep_mm, b * PREP_USES + n + 1)
                        c = 2 * (n - len(M_GROUPS))
                        act.activation(u[0][:, c:c + 2, :], prep_bank[n][:, :].rearrange("p (c d) -> p c d", d=D),
                                       ACT.Copy).then_inc(prep_hi, 1)

                def step(b, t, bs, ts):
                    split_p(b, t, 0)
                    split_p(b, t, 1)
                    exps(bs, ts, 0)
                    split_p(b, t, 2)
                    exps(bs, ts, 1)
                    exps(bs, ts, 2)

                def first_tiles(b):
                    for k in range(NB):
                        exps(b, 0, k)
                    split_u(b)
                    step(b, 0, b, 1)

                def begin(b):
                    for kind in range(2):
                        diagonals(b, kind)
                    for dc in range(DC):
                        split_x(b, 0, dc)
                    for n in range(len(M_GROUPS)):
                        split_m(b, n)
                    first_tiles(b)

                def batch(b, nxt):
                    for t in range(TILES - 2):
                        step(b, t + 1, b, t + 2)
                        if t == 1:
                            for dc in range(DC):
                                split_x(b, 1, dc)
                        if nxt and t in (2, 3):
                            diagonals(b + 1, t - 2)
                    for k in range(NB):
                        split_p(b, TILES - 1, k)
                        if nxt:
                            split_m(b + 1, k)
                    if nxt:
                        split_x(b + 1, 0, 0)
                        split_m(b + 1, 3)
                        split_m(b + 1, 4)
                        split_x(b + 1, 0, 1)
                        split_m(b + 1, 5)
                        first_tiles(b + 1)
                each_batch(act, begin, batch)

            @block.vector
            def _(dve):
                def diagonals(b, kind):
                    for half in range(2):
                        r, *hi = diagonal(0, half)
                        r, *lo = diagonal(1, half)
                        dve.wait_ge(bd_hi, b * 4 + kind * 2 + half + 1)
                        dve.tensor_tensor(lo[kind], (g["kT"], g["vT"])[kind][r, :, ds(b * KEYS, KEYS)], f32(hi[kind]),
                                          ALU.subtract).then_inc(bd_lo, 1)

                def stats_of(b, blk):
                    layer_norm_stats(dve, x_tile(b, blk), stats, mean_var, mv_ready)

                def norm_of(b, blk):
                    dve.wait_ge(rstd_ready, b * BPB + blk + 1)
                    for j in range(TJ):
                        last = dve.tensor_scalar(xn[:, j, :], x_tile(b, blk)(j), mean_var[:, j, 0:1], rstd[:, j:j + 1],
                                                 ALU.subtract, ALU.mult)
                    last.then_inc(xn_ready, 1)

                def split_x(b, blk, dc):
                    dve.wait_ge(tr_hi, transpose_use0(b, "x", blk, dc) + 1)
                    dve.tensor_tensor(xnT[blk][1][:, dc, :], tr[:, :], f32(xnT[blk][0][:, dc, :]), ALU.subtract).then_inc(tr_lo, 1)

                def split_p(b, t, gr):
                    c0, n = TR_GROUPS[gr]
                    dve.wait_ge(tr_hi, transpose_use0(b, "p", t, gr) + 1)
                    dve.tensor_tensor(probT[t % 2][1][:, c0:c0 + n, :], tr[:, 0:n * P].rearrange("p (c q) -> p c q", q=P),
                                      f32(probT[t % 2][0][:, c0:c0 + n, :]), ALU.subtract).then_inc(tr_lo, 1)

                def maxima(b, t, k):
                    dve.wait_ge(score_mm, b * TB_BANKS + t * NB + k + 1)
                    dve.tensor_reduce(neg_max[t % 2][:, heads(k)], scores_of(t, k), AX_X, ALU.max, negate=True).then_inc(max_ready, 1)

                def sums(b, t):
                    for k in range(NB):
                        dve.wait_ge(exp_done, b * TB_BANKS + t * NB + k + 1)
                        dve.tensor_reduce(row_sum[:, heads(k)], probs_of(t, k), AX_X, ALU.add).then_inc(sum_done, 1)
                        dve.wait_ge(sum_done, b * TB_BANKS + t * NB + k + 1)
                        dve.reciprocal(row_inv[t % 2][:, heads(k)], row_sum[:, heads(k)]).then_inc(inv_ready, 1)

                def split_m(b, n):
                    dve.wait_ge(prep_hi, b * PREP_USES + n + 1)
                    dc, p0, np = M_GROUPS[n]
                    c = slice(p0 * PAIR_COLS, (p0 + np) * PAIR_COLS)
                    dve.tensor_tensor(m[1][:, dc, c], prep_bank[n][:, 0:np * PAIR_COLS], f32(m[0][:, dc, c]),
                                      ALU.subtract).then_inc(prep_lo, 1)

                def split_u(b):
                    for n in range(len(M_GROUPS), PREP_USES):
                        dve.wait_ge(prep_hi, b * PREP_USES + n + 1)
                        c = 2 * (n - len(M_GROUPS))
                        dve.tensor_tensor(u[1][:, c:c + 2, :], prep_bank[n][:, :].rearrange("p (c d) -> p c d", d=D),
                                          f32(u[0][:, c:c + 2, :]), ALU.subtract).then_inc(prep_lo, 1)

                def add_out(b, t):
                    blk, j = divmod(t, TJ)
                    dve.wait_ge(out_mm, b * TILES + t + 1)
                    if j == 0:
                        dve.wait_ge(bo_added, b * BPB + blk + 1)
                    dve.tensor_tensor(x_tile(b, blk)(j), acc[:, 0:D], x_tile(b, blk)(j), ALU.add).then_inc(out_added, 1)

                def step(b, t, bs, ts):
                    for k in range(NB):
                        split_p(b, t, k)
                        maxima(bs, ts, k)

                def first_tiles(b, ended):
                    for k in range(NB):
                        maxima(b, 0, k)
                    if not first(b):
                        add_out(ended, TILES - 1)
                    sums(b, 0)
                    split_u(b)
                    stats_of(b, 1)
                    step(b, 0, b, 1)
                    sums(b, 1)

                def begin(b):
                    stats_of(b, 0)
                    for kind in range(2):
                        diagonals(b, kind)
                    norm_of(b, 0)
                    for dc in range(DC):
                        split_x(b, 0, dc)
                    for n in range(len(M_GROUPS)):
                        split_m(b, n)
                    first_tiles(b, None)

                def batch(b, nxt):
                    for t in range(TILES - 2):
                        step(b, t + 1, b, t + 2)
                        if t == 1:
                            split_x(b, 1, 0)
                        sums(b, t + 2)
                        add_out(b, t)
                        if t == 0:
                            norm_of(b, 1)
                        if t == 1:
                            split_x(b, 1, 1)
                        if nxt and t in (2, 3):
                            diagonals(b + 1, t - 2)
                        if nxt and t == 4:
                            stats_of(b + 1, 0)
                        if nxt and t == 5:
                            norm_of(b + 1, 0)
                    for k in range(NB):
                        split_p(b, TILES - 1, k)
                        if nxt:
                            split_m(b + 1, k)
                    if nxt:
                        split_x(b + 1, 0, 0)
                        split_m(b + 1, 3)
                        split_m(b + 1, 4)
                        split_x(b + 1, 0, 1)
                        split_m(b + 1, 5)
                        add_out(b, TILES - 2)
                        first_tiles(b + 1, b)
                    else:
                        add_out(b, TILES - 2)
                        add_out(b, TILES - 1)
                each_batch(dve, begin, batch)

            @block.tensor
            def _(pe):
                def free_tr(b, *use):
                    n = transpose_use0(b, *use)
                    if not first(n):
                        pe.wait_ge(tr_lo, n)

                def transpose_x(b, blk, dc):
                    if dc == 0:
                        pe.wait_ge(xn_ready, b * BPB + blk + 1)
                    free_tr(b, "x", blk, dc)
                    for j in range(TJ):
                        last = pe.transpose(tr[:, j * P:(j + 1) * P], xn[:, j, dc * P:(dc + 1) * P], g["ident"][:, :])
                    last.then_inc(tr_mm, 1)

                def transpose_p(b, t, gr):
                    c0, nch = TR_GROUPS[gr]
                    pe.wait_ge(prob_ready, b * TB_BANKS + t * NB + (2, 3, 3)[gr])
                    free_tr(b, "p", t, gr)
                    for c in range(c0, c0 + nch):
                        w = min(P, HK - c * P)
                        last = pe.transpose(tr[0:w, (c - c0) * P:(c - c0 + 1) * P], prob[t % 2][:, c * P:c * P + w], g["ident"][:, :])
                    last.then_inc(tr_mm, 1)

                def scores(b, t, k):
                    blk, j = divmod(t, TJ)
                    if t >= 2:
                        pe.wait_ge(exp_done, b * TB_BANKS + (t - 2) * NB + k + 1)
                    elif k == 0:
                        pe.wait_ge(prep_lo, b * PREP_USES + (len(M_GROUPS), PREP_USES)[t])
                    if j == 0 and k == 0:
                        pe.wait_ge(tr_lo, transpose_use0(b, "x", blk, DC - 1) + 1)
                    for n, (i, w) in enumerate(HI_LO_PASSES):
                        for dc in range(DC):
                            last = pe.matmul(score[t % 2][k][:, 0:BANK_HEADS[k] * KEYS], xnT[blk][i][:, dc, j * P:(j + 1) * P],
                                             m[w][:, dc, cols(k)], start=(n == 0 and dc == 0), stop=(n == 2 and dc == DC - 1))
                    last.then_inc(score_mm, 1)

                def merge_m(b, n):
                    if n == 0:
                        pe.wait_ge(bd_lo, b * 4 + 2)
                    if not first(b):
                        pe.wait_ge(exp_done, (b - 1) * TB_BANKS + (TILES - 2) * NB + n + 1)
                    dc, p0, np = M_GROUPS[n]
                    for p in range(p0, p0 + np):
                        for q, (i, k) in enumerate(HI_LO_PASSES):
                            last = pe.matmul(prep_bank[n][:, (p - p0) * PAIR_COLS:(p - p0 + 1) * PAIR_COLS],
                                             g["wqT"][i][:, p, dc * P:(dc + 1) * P], g["kbd"][k][:, p, :], start=(q == 0), stop=(q == 2))
                    last.then_inc(prep_mm, 1)

                def merge_u(b):
                    pe.wait_ge(bd_lo, b * 4 + 4)
                    for n in range(len(M_GROUPS), PREP_USES):
                        pe.wait_ge(prep_lo, b * PREP_USES + n - 2)
                        for a in range(2):
                            c = 2 * (n - len(M_GROUPS)) + a
                            terms = [(p, i, k) for p in U_TERMS[c] for i, k in HI_LO_PASSES]
                            for q, (p, i, k) in enumerate(terms):
                                last = pe.matmul(prep_bank[n][:, a * D:(a + 1) * D], g["vz"][i][:, P * (c + p):P * (c + p + 1)],
                                                 g["wo"][k][:, p, :], start=(q == 0), stop=(q == len(terms) - 1))
                        last.then_inc(prep_mm, 1)

                def outputs(b, t):
                    pe.wait_ge(tr_lo, transpose_use0(b, "p", t, len(TR_GROUPS) - 1) + 1)
                    if t >= 1 or not first(b):
                        pe.wait_ge(out_added, b * TILES + t)
                    for c in range(KCH):
                        rows = min(P, HK - c * P)
                        for q, (i, k) in enumerate(HI_LO_PASSES):
                            last = pe.matmul(acc[:, 0:D], probT[t % 2][i][0:rows, c, :], u[k][0:rows, c, :],
                                             start=(c == 0 and q == 0), stop=(c == KCH - 1 and q == 2))
                    last.then_inc(out_mm, 1)

                def step(b, t, bs, ts):
                    for k in range(NB):
                        transpose_p(b, t, k)
                        scores(bs, ts, k)

                def first_tiles(b, ended):
                    for k in range(NB):
                        scores(b, 0, k)
                    if not first(b):
                        outputs(ended, TILES - 1)
                    merge_u(b)
                    step(b, 0, b, 1)

                def begin(b):
                    for dc in range(DC):
                        transpose_x(b, 0, dc)
                    for n in range(len(M_GROUPS)):
                        merge_m(b, n)
                    first_tiles(b, None)

                def batch(b, nxt):
                    for t in range(TILES - 2):
                        step(b, t + 1, b, t + 2)
                        if t == 1:
                            transpose_x(b, 1, 0)
                        outputs(b, t)
                        if t == 1:
                            transpose_x(b, 1, 1)
                    for k in range(NB):
                        transpose_p(b, TILES - 1, k)
                        if nxt:
                            merge_m(b + 1, k)
                    if nxt:
                        transpose_x(b + 1, 0, 0)
                        merge_m(b + 1, 3)
                        merge_m(b + 1, 4)
                        transpose_x(b + 1, 0, 1)
                        merge_m(b + 1, 5)
                        outputs(b, TILES - 2)
                        first_tiles(b + 1, b)
                    else:
                        outputs(b, TILES - 2)
                        outputs(b, TILES - 1)
                each_batch(pe, begin, batch)


E, H2 = 8, 192
NS = 2
TOP_K = 2
ROUTED = E * H2 // P
SHARED = NS * H2 // P
HCH = SHARED + ROUTED
XPOSE4 = 4


def experts_weights(nc, g, w, ctx):
    sb = lambda name, shape, dt: ctx.enter_context(nc.sbuf_tensor(name, shape, dt))
    g["w1T"] = [sb(f"w1T{i}", [P, DC, 2, HCH, P], F32R) for i in range(2)]
    g["w2T"] = [sb(f"w2T{i}", [P, HCH, D], F32R) for i in range(2)]
    g["gateT"] = [sb(f"gateT{i}", [P, DC, E], F32R) for i in range(2)]
    g["before"] = sb("before", [P, E, E], F32)
    with ExitStack() as tmp:
        t = lambda name, shape, dt: tmp.enter_context(nc.sbuf_tensor(name, shape, dt))
        sem = lambda name: tmp.enter_context(nc.semaphore(name))
        w1s = t("w1s", [P, 2, HCH, D], F32)
        w2s = t("w2s", [P, DC, HCH * P], F32)
        gates = t("gates", [E, D], F32)
        bank = [tmp.enter_context(nc.psum_tensor(f"w1_bank{i}", [P, 512], F32)) for i in range(8)]
        gate_in, y_in, g_in, w2_in = sem("gate_in"), sem("y_in"), sem("g_in"), sem("w2_in")
        ones_done = sem("ones_done")
        bank_mm, bank_hi, bank_lo = sem("bank_mm1"), sem("bank_hi1"), sem("bank_lo1")
        w1_uses = [("w1", yg, dc, c) for yg in range(2) for c in range(0, HCH, XPOSE4) for dc in range(DC)]
        uses = [("gate",)] + w1_uses + [("w2", c) for c in range(0, HCH, 2)]

        def moved(use, n, i):
            b = bank[n % 8]
            if use[0] == "gate":
                return b[:, 0:DC * E].rearrange("p (c e) -> p c e", e=E), g["gateT"][i][:, :, :]
            if use[0] == "w1":
                _, yg, dc, c = use
                k = min(XPOSE4, HCH - c)
                return b[:, 0:k * P].rearrange("p (c h) -> p c h", h=P), g["w1T"][i][:, dc, yg, c:c + k, :]
            c = use[1]
            k = min(2, HCH - c)
            return b[:, 0:k * D].rearrange("p (c d) -> p c d", d=D), g["w2T"][i][:, c:c + k, :]

        with nc.Block() as block:
            @block.sync
            def _(sp):
                sp.dma_start(gates[:, :], w["L0_ffn_gate_w"]).then_inc(gate_in, 16)
                w1 = w["L0_ffn_W1"].rearrange("(q e) (s r) d -> s e r q d", e=2, s=2)
                ws1 = w["L0_ffn_Ws1"].rearrange("(s c p) d -> s p c d", s=2, p=P)
                half = P // 2
                for yg, s in ((0, y_in), (1, g_in)):
                    sp.dma_start(w1s[:, yg, SHARED::3, :], w1[yg, 0, 0:P]).then_inc(s, 16)
                    sp.dma_start(w1s[0:half, yg, SHARED + 1::3, :], w1[yg, 0, P:H2]).then_inc(s, 16)
                    sp.dma_start(w1s[half:P, yg, SHARED + 1::3, :], w1[yg, 1, 0:half]).then_inc(s, 16)
                    sp.dma_start(w1s[:, yg, SHARED + 2::3, :], w1[yg, 1, half:H2]).then_inc(s, 16)
                    sp.dma_start(w1s[:, yg, 0:SHARED, :], ws1[yg]).then_inc(s, 16)
                w2s_routed = w2s[:, :, SHARED * P:].rearrange("p c (e h) -> p c e h", h=H2)
                for dc in range(DC):
                    sp.dma_start(w2s_routed[:, dc, :, :], w["L0_ffn_W2"][:, dc * P:(dc + 1) * P, :].rearrange("e p h -> p e h")).then_inc(w2_in, 16)
                sp.dma_start(w2s[:, :, 0:SHARED * P], w["L0_ffn_Ws2"].rearrange("(c p) h -> p c h", p=P)).then_inc(w2_in, 16)

            @block.gpsimd
            def _(gp):
                gp.memset(g["before"][:, :, :], 1.0).then_inc(ones_done, 1)
                gp.wait_ge(ones_done, 1)
                gp.affine_select(out=g["before"][:, :, :], in_=g["before"][:, :, :], compare_op=ALU.is_gt, fill=0.0,
                                 base=0, pattern=[[1, E], [-1, E]], channel_multiplier=0)

            @block.tensor
            def _(pe):
                for n, use in enumerate(uses):
                    b = bank[n % 8]
                    if n >= 8:
                        pe.wait_ge(bank_lo, n - 7)
                    if use[0] == "gate":
                        pe.wait_ge(gate_in, 16)
                        for dc in range(DC):
                            last = pe.transpose(b[:, dc * E:(dc + 1) * E], gates[:, dc * P:(dc + 1) * P], g["ident"][0:E, 0:E])
                    elif use[0] == "w1":
                        _, yg, dc, c0 = use
                        pe.wait_ge((y_in, g_in)[yg], 5 * 16)
                        for c in range(c0, min(c0 + XPOSE4, HCH)):
                            last = pe.transpose(b[:, (c - c0) * P:(c - c0 + 1) * P], w1s[:, yg, c, dc * P:(dc + 1) * P], g["ident"][:, :])
                    else:
                        pe.wait_ge(w2_in, 3 * 16)
                        for c in range(use[1], min(use[1] + 2, HCH)):
                            for dc in range(DC):
                                at = (c - use[1]) * D + dc * P
                                last = pe.transpose(b[:, at:at + P], w2s[:, dc, c * P:(c + 1) * P], g["ident"][:, :])
                    last.then_inc(bank_mm, 1)

            @block.scalar
            def _(act):
                for n, use in enumerate(uses):
                    src, hi = moved(use, n, 0)
                    act.wait_ge(bank_mm, n + 1)
                    act.activation(hi, src, ACT.Copy).then_inc(bank_hi, 1)

            @block.vector
            def _(dve):
                for n, use in enumerate(uses):
                    src, hi = moved(use, n, 0)
                    _, lo = moved(use, n, 1)
                    dve.wait_ge(bank_hi, n + 1)
                    dve.tensor_tensor(lo, src, f32(hi), ALU.subtract).then_inc(bank_lo, 1)


def experts(nc, g, scratch):
    with ExitStack() as ctx:
        sb = lambda name, shape, dt: ctx.enter_context(nc.sbuf_tensor(name, shape, dt))
        pb = lambda name: ctx.enter_context(nc.psum_tensor(name, [P, 512], F32))
        xn = sb("xn1", [P, TJ, D], F32)
        xnT = [[sb(f"xnT1_{s}_{i}", [P, DC, TB], F32R) for i in range(2)] for s in range(2)]
        stats, mean_var, rstd = sb("stats1", [P, TJ, 6], F32), sb("mean_var1", [P, TJ, 2], F32), sb("rstd1", [P, TJ], F32)
        logit, expv, route = (sb(n, [P, TJ, E], F32) for n in ("logit", "expv", "route"))
        gmax, gsum, ginv = (sb(n, [P, TJ], F32) for n in ("gmax", "gsum", "ginv"))
        above, tie = sb("above", [P, TJ, E, E], F32), sb("tie", [P, TJ, E, E], F32)
        rank, weight = sb("rank", [P, TJ, E], F32), sb("weight", [P, TJ, E], F32)
        weightT = sb("weightT", [E, TB], F32)
        weight_all = sb("weight_all", [P, ROUTED, TB], F32)
        gated = [sb(f"gated{s}", [P, TB], F32) for s in range(2)]
        hid = [sb(f"hid{s}", [P, TB], F32) for s in range(3)]
        hidT = [[sb(f"hidT{s}_{i}", [P, TB], F32R) for i in range(2)] for s in range(3)]
        py, pg = [pb(f"py{s}") for s in range(2)], [pb(f"pg{s}") for s in range(2)]
        acc = [pb(f"acc1_{s}") for s in range(2)]
        tr, pgate = pb("tr1"), pb("pgate")
        names = ("mv_ready", "eps_done", "rstd_ready", "xn_ready", "tr_mm", "tr_hi", "tr_lo", "gate_mm", "gmax_done", "logit_ready",
                 "expv_ready", "gsum_done", "ginv_done", "route_done", "above_done", "tie_done", "tied_done", "count_done", "rank_done",
                 "weight_ready", "wT_mm", "wT_ready", "wT_out", "w_all_in", "up_mm", "silu_done", "silu_weighted", "hid_done", "hid_hi",
                 "hid_lo", "down_mm", "acc_free")
        s = {n: ctx.enter_context(nc.semaphore(n + "1")) for n in names}

        PE_STEPS = (5, 7, 9, 13)
        ACT_STEPS = (6, 8, 11, 14)
        DVE_STEPS = (2, 4, 6, 8, 10, 12)

        def pe_next(pe, n, par, part):
            if part < DC:
                if part == 0:
                    pe.wait_ge(s["xn_ready"], n + 1)
                    pe.wait_ge(s["wT_ready"], n + 1)
                pe.wait_ge(s["tr_lo"], DC * n + part + 1)
                for j in range(TJ):
                    last = pe.transpose(tr[:, j * P:(j + 1) * P], xn[:, j, part * P:(part + 1) * P], g["ident"][:, :])
                last.then_inc(s["tr_mm"], 1)
            elif part == 2:
                pe.wait_ge(s["tr_lo"], DC * n + DC + 1)
                for j in range(TJ):
                    for q, (i, k) in enumerate(HI_LO_PASSES):
                        for dc in range(DC):
                            last = pe.matmul(pgate[:, j * E:(j + 1) * E], xnT[par][i][:, dc, j * P:(j + 1) * P], g["gateT"][k][:, dc, :],
                                             start=(q == 0 and dc == 0), stop=(q == 2 and dc == DC - 1))
                last.then_inc(s["gate_mm"], 1)
            else:
                pe.wait_ge(s["weight_ready"], n + 1)
                for j in range(TJ):
                    last = pe.transpose(tr[0:E, j * P:(j + 1) * P], weight[:, j, :], g["ident"][:, :])
                last.then_inc(s["wT_mm"], 1)

        def pe_block(pe, n, par, nxt):
            def up(c):
                if c >= 2:
                    pe.wait_ge(s["hid_done"], HCH * n + c - 1)
                for yg, out in ((0, py), (1, pg)):
                    for q, (i, k) in enumerate(HI_LO_PASSES):
                        for dc in range(DC):
                            last = pe.matmul(out[c % 2][:, :], g["w1T"][i][:, dc, yg, c, :], xnT[par][k][:, dc, :],
                                             start=(q == 0 and dc == 0), stop=(q == 2 and dc == DC - 1))
                last.then_inc(s["up_mm"], 1)

            def down(c):
                pe.wait_ge(s["hid_lo"], HCH * n + c + 1)
                if c == 0:
                    pe.wait_ge(s["acc_free"], n + 1)
                for j in range(TJ):
                    for q, (i, k) in enumerate(HI_LO_PASSES):
                        last = pe.matmul(acc[j // 2][:, (j % 2) * D:(j % 2 + 1) * D], hidT[c % 3][i][:, j * P:(j + 1) * P], g["w2T"][k][:, c, :],
                                         start=(c == 0 and q == 0 and j % 2 == 0), stop=(c == HCH - 1 and q == 2), skip_group_check=True)
                last.then_inc(s["down_mm"], 1)

            for c in range(HCH + 2):
                if c < HCH:
                    up(c)
                if c >= 2:
                    down(c - 2)
                if nxt and c in PE_STEPS:
                    pe_next(pe, n + 1, 1 - par, PE_STEPS.index(c))

        def act_next(act, n, par, part):
            if part < DC:
                act.wait_ge(s["tr_mm"], DC * n + part + 1)
                act.activation(xnT[par][0][:, part, :], tr[:, :], ACT.Copy).then_inc(s["tr_hi"], 1)
            elif part == 2:
                act.wait_ge(s["logit_ready"], n + 1)
                act.activation(expv[:, :, :], logit[:, :, :], ACT.Exp).then_inc(s["expv_ready"], 1)
            else:
                act.wait_ge(s["wT_mm"], n + 1)
                act.activation(weightT[:, :], tr[0:E, :], ACT.Copy).then_inc(s["wT_ready"], 1)

        def act_block(act, n, par, nxt):
            for c in range(HCH + 1):
                if c < HCH:
                    act.wait_ge(s["up_mm"], HCH * n + c + 1)
                    act.activation(gated[c % 2][:, :], pg[c % 2][:, :], ACT.Silu).then_inc(s["silu_done"], 1)
                if c >= 1:
                    act.wait_ge(s["hid_done"], HCH * n + c)
                    act.activation(hidT[(c - 1) % 3][0][:, :], hid[(c - 1) % 3][:, :], ACT.Copy).then_inc(s["hid_hi"], 1)
                if nxt and c in ACT_STEPS:
                    act_next(act, n + 1, 1 - par, ACT_STEPS.index(c))

        def gp_next(gp, n):
            gp.wait_ge(s["mv_ready"], n + 1)
            inverse_std(gp, g, rstd, mean_var[:, :, 1], s["eps_done"], n + 1, s["rstd_ready"])

        def gp_block(gp, n, nxt):
            if nxt:
                gp_next(gp, n + 1)
            gp.wait_ge(s["w_all_in"], 4 * 16 * (n + 1))
            for c in range(SHARED, HCH):
                gp.wait_ge(s["silu_done"], HCH * n + c + 1)
                gp.tensor_tensor(gated[c % 2][:, :], gated[c % 2][:, :], weight_all[:, c - SHARED, :], ALU.mult).then_inc(s["silu_weighted"], 1)

        def x_tile(n):
            return lambda j: g["x"][:, ds(n, 1), j, :].rearrange("p a d -> p (a d)")

        def dve_next(dve, n, par, part):
            if part == 0:
                layer_norm_stats(dve, x_tile(n), stats, mean_var, s["mv_ready"])
            elif part == 1:
                dve.wait_ge(s["rstd_ready"], n + 1)
                for j in range(TJ):
                    last = dve.tensor_scalar(xn[:, j, :], x_tile(n)(j), mean_var[:, j, 0:1], rstd[:, j:j + 1], ALU.subtract, ALU.mult)
                last.then_inc(s["xn_ready"], 1)
            elif part < 2 + DC:
                dc = part - 2
                dve.wait_ge(s["tr_hi"], DC * n + dc + 1)
                dve.tensor_tensor(xnT[par][1][:, dc, :], tr[:, :], f32(xnT[par][0][:, dc, :]), ALU.subtract).then_inc(s["tr_lo"], 1)
            elif part == 2 + DC:
                dve.wait_ge(s["gate_mm"], n + 1)
                logits = pgate[:, 0:TJ * E].rearrange("p (j e) -> p j e", e=E)
                dve.tensor_reduce(gmax[:, :], logits, AX_X, ALU.max).then_inc(s["gmax_done"], 1)
                dve.wait_ge(s["gmax_done"], n + 1)
                dve.tensor_tensor(logit[:, :, :], logits, gmax[:, :].unsqueeze(2).to_broadcast([P, TJ, E]),
                                  ALU.subtract).then_inc(s["logit_ready"], 1)
            else:
                dve.wait_ge(s["expv_ready"], n + 1)
                dve.tensor_reduce(gsum[:, :], expv[:, :, :], AX_X, ALU.add).then_inc(s["gsum_done"], 1)
                dve.wait_ge(s["gsum_done"], n + 1)
                dve.reciprocal(ginv[:, :], gsum[:, :]).then_inc(s["ginv_done"], 1)
                dve.wait_ge(s["ginv_done"], n + 1)
                dve.tensor_tensor(route[:, :, :], expv[:, :, :], ginv[:, :].unsqueeze(2).to_broadcast([P, TJ, E]),
                                  ALU.mult).then_inc(s["route_done"], 1)
                dve.wait_ge(s["route_done"], n + 1)
                other = route[:, :, :].unsqueeze(2).to_broadcast([P, TJ, E, E])
                own = route[:, :, :].unsqueeze(3).to_broadcast([P, TJ, E, E])
                dve.tensor_tensor(above[:, :, :, :], other, own, ALU.is_gt).then_inc(s["above_done"], 1)
                dve.tensor_tensor(tie[:, :, :, :], other, own, ALU.is_equal).then_inc(s["tie_done"], 1)
                dve.wait_ge(s["tie_done"], n + 1)
                dve.tensor_tensor(tie[:, :, :, :], tie[:, :, :, :], g["before"][:, :, :].unsqueeze(1).to_broadcast([P, TJ, E, E]),
                                  ALU.mult).then_inc(s["tied_done"], 1)
                dve.wait_ge(s["tied_done"], n + 1)
                dve.tensor_tensor(above[:, :, :, :], above[:, :, :, :], tie[:, :, :, :], ALU.add).then_inc(s["count_done"], 1)
                dve.wait_ge(s["count_done"], n + 1)
                dve.tensor_reduce(rank[:, :, :], above[:, :, :, :], AX_X, ALU.add).then_inc(s["rank_done"], 1)
                dve.wait_ge(s["rank_done"], n + 1)
                dve.scalar_tensor_tensor(weight[:, :, :], rank[:, :, :], float(TOP_K), route[:, :, :], ALU.is_lt, ALU.mult).then_inc(s["weight_ready"], 1)

        def dve_block(dve, n, par, nxt):
            for c in range(HCH + 1):
                if c < HCH:
                    if c >= SHARED:
                        dve.wait_ge(s["silu_weighted"], ROUTED * n + c - SHARED + 1)
                    else:
                        dve.wait_ge(s["silu_done"], HCH * n + c + 1)
                    dve.tensor_tensor(hid[c % 3][:, :], py[c % 2][:, :], gated[c % 2][:, :], ALU.mult).then_inc(s["hid_done"], 1)
                if c >= 1:
                    dve.wait_ge(s["hid_hi"], HCH * n + c)
                    dve.tensor_tensor(hidT[(c - 1) % 3][1][:, :], hid[(c - 1) % 3][:, :], f32(hidT[(c - 1) % 3][0][:, :]),
                                      ALU.subtract).then_inc(s["hid_lo"], 1)
                if nxt and c in DVE_STEPS:
                    dve_next(dve, n + 1, 1 - par, DVE_STEPS.index(c))
            dve.wait_ge(s["down_mm"], HCH * (n + 1))
            for a in range(2):
                xa = g["x"][:, ds(n, 1), 2 * a:2 * a + 2, :].rearrange("p a j d -> p (a j d)")
                last = dve.tensor_tensor(xa, acc[a][:, :], xa, ALU.add)
            last.then_inc(s["acc_free"], 1)

        def sp_next(sp, n, first):
            transposed, written, used = (v if isinstance(v, int) else sp.to_reg(v) for v in (n + 2, 16 * (n + 1), ROUTED * n))
            sp.wait_ge(s["wT_ready"], transposed)
            sp.dma_start(scratch, weightT[:, :]).then_inc(s["wT_out"], 16)
            sp.wait_ge(s["wT_out"], written)
            if not first:
                sp.wait_ge(s["silu_weighted"], used)
            row, half = scratch.rearrange("(q e) t -> e q t", e=2), P // 2
            for dst, e in ((weight_all[:, 0:ROUTED:3, :], 0), (weight_all[0:half, 1:ROUTED:3, :], 0),
                           (weight_all[half:P, 1:ROUTED:3, :], 1), (weight_all[:, 2:ROUTED:3, :], 1)):
                sp.dma_start(dst, row[e].partition_broadcast(dst.shape[0])).then_inc(s["w_all_in"], 16)

        LOOPS = NBLK // 2 - 1

        with nc.Block() as block:
            @block.sync
            def _(sp):
                sp_next(sp, 0, True)
                with sp.Fori(0, LOOPS) as it:
                    for a in range(2):
                        sp_next(sp, 2 * it + a + 1, False)
                sp_next(sp, NBLK - 1, False)

            @block.gpsimd
            def _(gp):
                gp_next(gp, 0)
                with gp.Fori(0, LOOPS) as it:
                    for a in range(2):
                        gp_block(gp, 2 * it + a, True)
                gp_block(gp, NBLK - 2, True)
                gp_block(gp, NBLK - 1, False)

            @block.scalar
            def _(act):
                for part in range(len(ACT_STEPS)):
                    act_next(act, 0, 0, part)
                with act.Fori(0, LOOPS) as it:
                    for a in range(2):
                        act_block(act, 2 * it + a, a, True)
                act_block(act, NBLK - 2, 0, True)
                act_block(act, NBLK - 1, 1, False)

            @block.vector
            def _(dve):
                dve.sem_inc(s["acc_free"], 1)
                dve.sem_inc(s["tr_lo"], 1)
                dve.sem_inc(s["wT_ready"], 1)
                for part in range(len(DVE_STEPS)):
                    dve_next(dve, 0, 0, part)
                with dve.Fori(0, LOOPS) as it:
                    for a in range(2):
                        dve_block(dve, 2 * it + a, a, True)
                dve_block(dve, NBLK - 2, 0, True)
                dve_block(dve, NBLK - 1, 1, False)

            @block.tensor
            def _(pe):
                for part in range(len(PE_STEPS)):
                    pe_next(pe, 0, 0, part)
                with pe.Fori(0, LOOPS) as it:
                    for a in range(2):
                        pe_block(pe, 2 * it + a, a, True)
                pe_block(pe, NBLK - 2, 0, True)
                pe_block(pe, NBLK - 1, 1, False)


H3 = HEADS
DH3 = D // H3
HH = H3 // DC
HALF = HH * KEYS
C3 = -(-HALF // P)
SLOT = DH3 + 2
C3_HEADS = [(P * c // KEYS, min(HH, -(-P * (c + 1) // KEYS))) for c in range(C3)]
CMAX = max(b - a for a, b in C3_HEADS)
NORM_EPS = 1e-12
NC3 = DC * C3
PROB_BUFFERS = 4


def attention1_weights(nc, g, w, ctx):
    sb = lambda name, shape, dt: ctx.enter_context(nc.sbuf_tensor(name, shape, dt))
    g["wq1"] = [sb(f"wq1_{i}", [P, DC, D], F32R) for i in range(2)]
    g["wo1"] = [sb(f"wo1_{i}", [P, DC, D], F32R) for i in range(2)]
    g["k1T"] = [sb(f"k1T_{i}", [P, DC, CK], F32R) for i in range(2)]
    g["vbd"] = [sb(f"vbd{i}", [P, B, DC, C3, CMAX, SLOT], F32R) for i in range(2)]
    g["head_rows"] = sb("head_rows", [P, HH, KEYS], F32)
    g["bq1"], g["bo1"], g["gamma"], g["beta"] = (sb(n, [P, D], F32) for n in ("bq1", "bo1", "gamma", "beta"))
    with ExitStack() as tmp:
        t = lambda name, shape, dt: tmp.enter_context(nc.sbuf_tensor(name, shape, dt))
        sem = lambda name: tmp.enter_context(nc.semaphore(name + "3w"))
        ctxs = t("ctxs1", [KEYS, B, CTX], F32)
        ctxT = [t(f"ctxT1_{i}", [CP, CC, CK], F32R) for i in range(2)]
        wqs, wos = t("wq1s", [P, DC, D], F32), t("wo1s", [P, DC, D], F32)
        wks, wvs = t("wk1s", [CP, CC, D], F32), t("wv1s", [CP, CC, D], F32)
        wk, wv = ([t(f"{n}_{i}", [CP, CC, D], F32R) for i in range(2)] for n in ("wk1", "wv1"))
        bk, bv = t("bk1", [P, D], F32), t("bv1", [P, D], F32)
        k, ksq, v = (t(n, [KEYS, B, D], F32) for n in ("k1", "k1sq", "v1"))
        vh = [t(f"v1_{i}", [KEYS, B, D], F32R) for i in range(2)]
        knorm, kinv = t("knorm", [KEYS, B], F32), t("kinv", [KEYS, B], F32)
        spread_f = t("spread_f", [KEYS, C3 * P], F32)
        spread = t("spread", [KEYS, C3 * P], F32R)
        row_head = t("row_head", [P, C3, HH], F32)
        bank = [tmp.enter_context(nc.psum_tensor(f"w3_bank{i}", [P, 512], F32)) for i in range(8)]
        ctx_in, wk_in, wv_in, wq_in, wo_in, bias_in, row_in = (
            sem(n) for n in ("ctx_in", "wk_in", "wv_in", "wq_in", "wo_in", "bias_in", "row_in"))
        fill, shaped, w_hi, w_lo, mm, hi, lo, k_out, sq_out, norm_out, norm_pow, norm_max, inv_out, kn_out, v_out, vh_hi, vh_lo, v_zero, spread_out, vbd_out = (
            sem(n) for n in ("fill", "shaped", "w_hi", "w_lo", "mm", "hi", "lo", "k_out", "sq_out", "norm_out", "norm_pow", "norm_max",
                             "inv_out", "kn_out", "v_out", "vh_hi", "vh_lo", "v_zero", "spread_out", "vbd_out"))
        SPREAD = [(b, c) for b in range(B) for c in range(C3)]

        def ones_where(gp, tile, pattern_base_cm, n):
            for m, (base, cm, pattern) in enumerate(pattern_base_cm):
                gp.wait_ge(fill if m == 0 else shaped, 4 if m == 0 else n + m)
                gp.affine_select(out=tile, in_=tile, compare_op=ALU.is_ge, fill=0.0, base=base, pattern=pattern,
                                 channel_multiplier=cm).then_inc(shaped, 1)
            return n + len(pattern_base_cm)

        with nc.Block() as block:
            @block.sync
            def _(sp):
                sp.dma_start(ctxs[:, :, :], w["ctx_768"].rearrange("b k c -> k b c")).then_inc(ctx_in, 16)
                for dst, src, p, s in ((wks, w["L1_xattn_Wk"], CP, wk_in), (wvs, w["L1_xattn_Wv"], CP, wv_in),
                                       (wqs, w["L1_xattn_Wq"], P, wq_in), (wos, w["L1_xattn_Wo"], P, wo_in)):
                    sp.dma_start(dst[:, :, :], src.rearrange("(c p) n -> p c n", p=p)).then_inc(s, 16)
                for dst, src in ((bk, w["L1_xattn_bk"]), (bv, w["L1_xattn_bv"])):
                    sp.dma_start(dst[:, :], src.partition_broadcast(P)).then_inc(bias_in, 16)
                rows = ((g["bq1"], w["L1_xattn_bq"]), (g["bo1"], w["L1_xattn_bo"]), (g["gamma"], w["L1_xattn_ln_gamma"]), (g["beta"], w["L1_xattn_ln_beta"]))
                for dst, src in rows:
                    sp.dma_start(dst[:, :], src.partition_broadcast(P)).then_inc(row_in, 16)
                sp.wait_ge(row_in, 16 * len(rows))

            @block.gpsimd
            def _(gp):
                gp.memset(g["head_rows"][:, :, :], 1.0).then_inc(fill, 1)
                gp.memset(row_head[:, :, :], 1.0).then_inc(fill, 1)
                gp.memset(spread_f[:, HALF:], 0.0).then_inc(fill, 1)
                gp.memset(spread_f[:, 0:HALF], 1.0).then_inc(fill, 1)
                n = ones_where(gp, g["head_rows"][:, :, :], ((0, 1, [[-DH3, HH], [0, KEYS]]), (DH3 - 1, -1, [[DH3, HH], [0, KEYS]])), 0)
                n = ones_where(gp, row_head[:, :, :], ((0, 1, [[P, C3], [-KEYS, HH]]), (KEYS - 1, -1, [[-P, C3], [KEYS, HH]])), n)
                n = ones_where(gp, spread_f[:, 0:HALF], ((0, 1, [[0, HH], [-1, KEYS]]), (0, -1, [[0, HH], [1, KEYS]])), n)
                for i in range(2):
                    gp.memset(f32(g["vbd"][i][:, :, :, :, :, :]), 0.0).then_inc(v_zero, 1)
                gp.wait_ge(norm_out, 1)
                gp.tensor_tensor(knorm[:, :], knorm[:, :], g["half"][0:KEYS, 0:B], ALU.pow).then_inc(norm_pow, 1)

            @block.scalar
            def _(act):
                for n, (dst, src, s) in enumerate(((wk, wks, wk_in), (wv, wvs, wv_in), (g["wq1"], wqs, wq_in), (g["wo1"], wos, wo_in))):
                    act.wait_ge(s, 16)
                    act.activation(dst[0][:, :, :], src[:, :, :], ACT.Copy).then_inc(w_hi, 1)
                for c in range(CC):
                    act.wait_ge(mm, c + 1)
                    act.activation(ctxT[0][:, c, :], bank[c][0:CP, 0:CK], ACT.Copy).then_inc(hi, 1)
                act.wait_ge(shaped, 6)
                act.activation(spread[:, :], spread_f[:, :], ACT.Copy).then_inc(spread_out, 1)
                act.wait_ge(v_out, 2)
                act.activation(vh[0][:, :, :], v[:, :, :], ACT.Copy).then_inc(vh_hi, 1)
                for f in range(DC):
                    act.wait_ge(mm, 7 + f)
                    act.activation(g["k1T"][0][:, f, :], bank[6 + f][:, 0:CK], ACT.Copy).then_inc(hi, 1)

            @block.vector
            def _(dve):
                for n, (dst, src) in enumerate(((wk, wks), (wv, wvs), (g["wq1"], wqs), (g["wo1"], wos))):
                    dve.wait_ge(w_hi, n + 1)
                    dve.tensor_tensor(dst[1][:, :, :], src[:, :, :], f32(dst[0][:, :, :]), ALU.subtract).then_inc(w_lo, 1)
                for c in range(CC):
                    dve.wait_ge(hi, c + 1)
                    dve.tensor_tensor(ctxT[1][:, c, :], bank[c][0:CP, 0:CK], f32(ctxT[0][:, c, :]), ALU.subtract).then_inc(lo, 1)
                dve.wait_ge(bias_in, 32)
                two = lambda ap: ap[0:KEYS, :].unsqueeze(1).to_broadcast([KEYS, 2, D])
                for n, (dst, bias, s) in enumerate(((k, bk, k_out), (k, bk, k_out), (v, bv, v_out), (v, bv, v_out))):
                    dve.wait_ge(mm, 2 + n + 1)
                    a = n % 2
                    dve.tensor_tensor(dst[:, 2 * a:2 * a + 2, :], bank[2 + n][0:KEYS, :].rearrange("p (b d) -> p b d", d=D), two(bias),
                                      ALU.add).then_inc(s, 1)
                dve.wait_ge(k_out, 2)
                dve.tensor_tensor(ksq[:, :, :], k[:, :, :], k[:, :, :], ALU.mult).then_inc(sq_out, 1)
                dve.wait_ge(sq_out, 1)
                dve.tensor_reduce(knorm[:, :], ksq[:, :, :], AX_X, ALU.add).then_inc(norm_out, 1)
                dve.wait_ge(norm_pow, 1)
                dve.tensor_scalar(knorm[:, :], knorm[:, :], NORM_EPS, None, ALU.max).then_inc(norm_max, 1)
                dve.wait_ge(norm_max, 1)
                dve.reciprocal(kinv[:, :], knorm[:, :]).then_inc(inv_out, 1)
                dve.wait_ge(inv_out, 1)
                dve.tensor_tensor(k[:, :, :], k[:, :, :], kinv[:, :].unsqueeze(2).to_broadcast([KEYS, B, D]), ALU.mult).then_inc(kn_out, 1)
                dve.wait_ge(vh_hi, 1)
                dve.tensor_tensor(vh[1][:, :, :], v[:, :, :], f32(vh[0][:, :, :]), ALU.subtract).then_inc(vh_lo, 1)
                for f in range(DC):
                    dve.wait_ge(hi, CC + f + 1)
                    dve.tensor_tensor(g["k1T"][1][:, f, :], bank[6 + f][:, 0:CK], f32(g["k1T"][0][:, f, :]), ALU.subtract).then_inc(lo, 1)
                dve.wait_ge(shaped, 6)
                dve.wait_ge(v_zero, 2)
                for c, (h0, h1) in enumerate(C3_HEADS):
                    dve.tensor_copy(g["vbd"][0][:, :, :, c, 0:h1 - h0, DH3],
                                    row_head[:, c, h0:h1].unsqueeze(1).unsqueeze(1).to_broadcast([P, B, DC, h1 - h0]))
                for n, (b, c) in enumerate(SPREAD):
                    h0, h1 = C3_HEADS[c]
                    dve.wait_ge(mm, 8 + n + 1)
                    for i in range(2):
                        src = bank[n % 8][:, i * D:(i + 1) * D].rearrange("p (f h d) -> p f h d", f=DC, d=DH3)[:, :, h0:h1, :]
                        keep = row_head[:, c, h0:h1].unsqueeze(1).unsqueeze(3).to_broadcast([P, DC, h1 - h0, DH3])
                        last = dve.tensor_tensor(g["vbd"][i][:, b, :, c, 0:h1 - h0, 0:DH3], src, keep, ALU.mult)
                    last.then_inc(vbd_out, 1)

            @block.tensor
            def _(pe):
                pe.wait_ge(ctx_in, 16)
                for c in range(CC):
                    for b in range(B):
                        last = pe.transpose(bank[c][0:CP, b * KEYS:(b + 1) * KEYS], ctxs[:, b, c * CP:(c + 1) * CP], g["ident"][0:KEYS, 0:KEYS])
                    last.then_inc(mm, 1)
                pe.wait_ge(lo, CC)
                for n, weight in enumerate((wk, wk, wv, wv)):
                    pe.wait_ge(w_lo, 1 + n // 2)
                    for a in range(2):
                        b = 2 * (n % 2) + a
                        for q, (i, j) in enumerate(HI_LO_PASSES):
                            for c in range(CC):
                                last = pe.matmul(bank[2 + n][0:KEYS, a * D:(a + 1) * D], ctxT[i][:, c, b * KEYS:(b + 1) * KEYS], weight[j][:, c, :],
                                                 start=(q == 0 and c == 0), stop=(q == 2 and c == CC - 1))
                    last.then_inc(mm, 1)
                pe.wait_ge(kn_out, 1)
                for f in range(DC):
                    for b in range(B):
                        last = pe.transpose(bank[6 + f][:, b * KEYS:(b + 1) * KEYS], k[:, b, f * P:(f + 1) * P], g["ident"][0:KEYS, 0:KEYS])
                    last.then_inc(mm, 1)
                pe.wait_ge(spread_out, 1)
                pe.wait_ge(vh_lo, 1)
                pe.wait_ge(lo, CC + DC)
                for n, (b, c) in enumerate(SPREAD):
                    if n >= 8:
                        pe.wait_ge(vbd_out, n - 7)
                    for i in range(2):
                        last = pe.matmul(bank[n % 8][:, i * D:(i + 1) * D], spread[:, c * P:(c + 1) * P], vh[i][:, b, :], start=True, stop=True)
                    last.then_inc(mm, 1)


def attention1(nc, g):
    with ExitStack() as ctx:
        sb = lambda name, shape, dt: ctx.enter_context(nc.sbuf_tensor(name, shape, dt))
        pb = lambda name: ctx.enter_context(nc.psum_tensor(name, [P, 512], F32))
        kbd = [sb(f"kbd1_{i}", [P, DC, HH, KEYS], F32R) for i in range(2)]
        xn = sb("xn3", [P, TJ, D], F32)
        xnT = [sb(f"xnT3_{i}", [P, DC, TB], F32R) for i in range(2)]
        stats, mean_var, rstd = sb("stats3", [P, TJ, 6], F32), sb("mean_var3", [P, TJ, 2], F32), sb("rstd3", [P, TJ], F32)
        y_stats, y_mean_var, y_rstd = sb("stats_y", [P, TJ, 6], F32), sb("mean_var_y", [P, TJ, 2], F32), sb("rstd_y", [P, TJ], F32)
        qp, qres = [sb(f"qp{s}", [P, TJ, D], F32) for s in range(2)], [sb(f"qres{s}", [P, TJ, D], F32) for s in range(2)]
        qn, sq = sb("qn", [P, TJ, D], F32), sb("sq", [P, TJ, D], F32)
        qnorm, qinv = sb("qnorm", [P, TJ], F32), sb("qinv", [P, TJ], F32)
        qT = [[sb(f"qT{s}_{i}", [P, DC, TB], F32R) for i in range(2)] for s in range(2)]
        prob = [sb(f"prob3_{s}", [P, TB], F32) for s in range(PROB_BUFFERS)]
        probT = [[sb(f"probT3_{s}_{i}", [P, TB], F32R) for i in range(2)] for s in range(PROB_BUFFERS)]
        sums, o = sb("sums3", [P, TJ, H3], F32), sb("o3", [P, TJ, D], F32)
        oT = [sb(f"oT{i}", [P, DC, TB], F32R) for i in range(2)]
        y = sb("y3", [P, TJ, D], F32)
        score = [pb(f"score3_{s}") for s in range(2)]
        acc = [pb(f"acc3_{j}") for j in range(TJ)]
        tr, proj = pb("tr3"), pb("proj3")
        names = ("mv_ready", "eps_done", "rstd_ready", "xn_ready", "tr_mm", "tr_hi", "tr_lo", "proj_mm", "proj_out", "ssq_done", "root_done",
                 "norm_done", "qinv_done", "qn_ready", "qres_ready", "kbd_ready", "score_mm", "exp_done", "prob_hi", "prob_lo", "pv_mm",
                 "sums_done", "o_ready", "y_mv", "y_eps", "y_rstd", "y_gamma", "beta_added")
        s = {n: ctx.enter_context(nc.semaphore(n + "3")) for n in names}
        two_tiles = lambda ap: ap[:, :].unsqueeze(1).to_broadcast([P, 2, D])
        four_tiles = lambda ap: ap[:, :].unsqueeze(1).to_broadcast([P, TJ, D])
        pair = lambda tile, a: tile[:, 2 * a:2 * a + 2, :]
        banked = lambda bank: bank[:, :].rearrange("p (j d) -> p j d", d=D)

        def is_block(n, *blocks):
            return isinstance(n, int) and n in blocks

        def tr_use(n, kind, dc):
            if kind == 0:
                return (0 if is_block(n, 0) else 6 * n - 2) + dc
            if kind == 1:
                return (2 if is_block(n, 0) else 6 * n) + dc
            return 6 * n + (4 if is_block(n, NBLK - 1) else 8) + dc

        def proj_use(n, kind, a):
            if kind == 0:
                return (0 if is_block(n, 0) else 4 * n - 2) + a
            return 4 * n + (2 if is_block(n, NBLK - 1) else 4) + a

        def chunk(c):
            f, cc = divmod(c, C3)
            return f, cc, min(P, HALF - cc * P)

        def slot(par, c):
            return (NC3 * par + c) % PROB_BUFFERS

        def x_tile(n):
            return lambda j: g["x"][:, ds(n, 1), j, :].rearrange("p a d -> p (a d)")

        def x_block(n):
            return g["x"][:, ds(n, 1), :, :].rearrange("p a j d -> p (a j) d")

        def pe_transpose(pe, n, kind, dc, src):
            use = tr_use(n, kind, dc)
            if not is_block(use, 0):
                pe.wait_ge(s["tr_lo"], use)
            for j in range(TJ):
                last = pe.transpose(tr[:, j * P:(j + 1) * P], src[:, j, dc * P:(dc + 1) * P], g["ident"][:, :])
            last.then_inc(s["tr_mm"], 1)

        def pe_project(pe, n, kind, a, xT, weight):
            use = proj_use(n, kind, a)
            if not is_block(use, 0):
                pe.wait_ge(s["proj_out"], use)
            if a == 0:
                pe.wait_ge(s["tr_lo"], tr_use(n, 2 * kind, DC - 1) + 1)
            for b in range(2):
                j = 2 * a + b
                for q, (i, k) in enumerate(HI_LO_PASSES):
                    for dc in range(DC):
                        last = pe.matmul(proj[:, b * D:(b + 1) * D], xT[i][:, dc, j * P:(j + 1) * P], weight[k][:, dc, :],
                                         start=(q == 0 and dc == 0), stop=(q == 2 and dc == DC - 1))
            last.then_inc(s["proj_mm"], 1)

        def pe_front(pe, n, part):
            if part < 2:
                if part == 0:
                    pe.wait_ge(s["xn_ready"], n + 1)
                pe_transpose(pe, n, 0, part, xn)
            elif part < 4:
                pe_project(pe, n, 0, part - 2, xnT, g["wq1"])
            else:
                if part == 4:
                    pe.wait_ge(s["qn_ready"], n + 1)
                pe_transpose(pe, n, 1, part - 4, qn)

        def pe_back(pe, n, part):
            if part < 2:
                if part == 0:
                    pe.wait_ge(s["o_ready"], n + 2)
                pe_transpose(pe, n, 2, part, o)
            else:
                pe_project(pe, n, 1, part - 2, oT, g["wo1"])

        def pe_scores(pe, n, par, batch, c):
            f, cc, rows = chunk(c)
            if cc == 0:
                pe.wait_ge(s["kbd_ready"], DC * batch + f + 1)
                pe.wait_ge(s["tr_lo"], tr_use(n, 1, f) + 1)
            if c >= 2 or not is_block(n, 0):
                pe.wait_ge(s["exp_done"], NC3 * n + c - 1)
            for q, (i, k) in enumerate(HI_LO_PASSES):
                keys = kbd[i][:, f, :, :].rearrange("p h k -> p (h k)")[:, cc * P:cc * P + rows]
                last = pe.matmul(score[c % 2][0:rows, :], keys, qT[par][k][:, f, :], start=(q == 0), stop=(q == 2))
            last.then_inc(s["score_mm"], 1)

        def pe_values(pe, n, par, batch, c):
            f, cc, rows = chunk(c)
            h0, h1 = C3_HEADS[cc]
            pe.wait_ge(s["prob_lo"], NC3 * n + c + 1)
            if c == 0:
                pe.wait_ge(s["o_ready"], n + 1)
            for j in range(TJ):
                out = acc[j][:, (f * HH + h0) * SLOT:(f * HH + h1) * SLOT]
                for q, (i, k) in enumerate(HI_LO_PASSES):
                    v = g["vbd"][k][0:rows, ds(batch, 1), f, cc, 0:h1 - h0, :].rearrange("p a h d -> p (a h d)")
                    last = pe.matmul(out, probT[slot(par, c)][i][0:rows, j * P:(j + 1) * P], v, start=(c == 0 and q == 0),
                                     stop=(c == NC3 - 1 and q == 2), skip_group_check=True)
            last.then_inc(s["pv_mm"], 1)

        PE_FRONT = {2: 0, 3: 1, 4: 2, 5: 3, 7: 4, 8: 5}
        PE_BACK = {0: 0, 1: 1, 2: 2, 3: 3}

        def pe_block(pe, n, par, batch, next_batch, prv, nxt):
            for c in range(NC3):
                if c + 2 < NC3:
                    pe_scores(pe, n, par, batch, c + 2)
                elif nxt and c + 1 == NC3:
                    pe_scores(pe, n + 1, 1 - par, next_batch, 0)
                pe_values(pe, n, par, batch, c)
                if nxt and c + 1 == NC3:
                    pe_scores(pe, n + 1, 1 - par, next_batch, 1)
                if prv and c in PE_BACK:
                    pe_back(pe, n - 1, PE_BACK[c])
                if nxt and c in PE_FRONT:
                    pe_front(pe, n + 1, PE_FRONT[c])

        def act_split(act, n, kind, dc, dst):
            act.wait_ge(s["tr_mm"], tr_use(n, kind, dc) + 1)
            act.activation(dst[0][:, dc, :], tr[:, :], ACT.Copy).then_inc(s["tr_hi"], 1)

        def act_squares(act, n, par):
            act.wait_ge(s["proj_out"], proj_use(n, 0, 1) + 1)
            for j in range(TJ):
                last = act.activation(sq[:, j, :], qp[par][:, j, :], ACT.Square, accum_out=qnorm[:, j:j + 1])
            last.then_inc(s["ssq_done"], 1)

        def act_exp(act, n, par, c):
            rows = chunk(c)[2]
            act.wait_ge(s["score_mm"], NC3 * n + c + 1)
            if c >= PROB_BUFFERS or not is_block(n, 0):
                act.wait_ge(s["prob_lo"], NC3 * n + c - PROB_BUFFERS + 1)
            act.activation(prob[slot(par, c)][0:rows, :], score[c % 2][0:rows, :], ACT.Exp, scale=DH3 ** -0.5).then_inc(s["exp_done"], 1)

        def act_hi(act, n, par, c):
            rows = chunk(c)[2]
            act.wait_ge(s["exp_done"], NC3 * n + c + 1)
            if c >= PROB_BUFFERS or not is_block(n, 0):
                act.wait_ge(s["pv_mm"], NC3 * n + c - PROB_BUFFERS + 1)
            act.activation(probT[slot(par, c)][0][0:rows, :], prob[slot(par, c)][0:rows, :], ACT.Copy).then_inc(s["prob_hi"], 1)

        def act_block(act, n, par, batch, next_batch, prv, nxt):
            for c in range(NC3):
                if c + 1 < NC3:
                    act_exp(act, n, par, c + 1)
                act_hi(act, n, par, c)
                if prv and c in (1, 2):
                    act_split(act, n - 1, 2, c - 1, oT)
                if nxt and c in (3, 4):
                    act_split(act, n + 1, 0, c - 3, xnT)
                if nxt and c == 6:
                    act_squares(act, n + 1, 1 - par)
                if nxt and c in (8, 9):
                    act_split(act, n + 1, 1, c - 8, qT[1 - par])
            if nxt:
                act_exp(act, n + 1, 1 - par, 0)

        def dve_split(dve, n, kind, dc, dst):
            dve.wait_ge(s["tr_hi"], tr_use(n, kind, dc) + 1)
            dve.tensor_tensor(dst[1][:, dc, :], tr[:, :], f32(dst[0][:, dc, :]), ALU.subtract).then_inc(s["tr_lo"], 1)

        def dve_stats(dve, n):
            layer_norm_stats(dve, x_tile(n), stats, mean_var, s["mv_ready"])

        def dve_normalize(dve, n):
            dve.wait_ge(s["rstd_ready"], n + 1)
            for j in range(TJ):
                last = dve.tensor_scalar(xn[:, j, :], x_tile(n)(j), mean_var[:, j, 0:1], rstd[:, j:j + 1], ALU.subtract, ALU.mult)
            last.then_inc(s["xn_ready"], 1)

        def dve_queries(dve, n, par, a):
            dve.wait_ge(s["proj_mm"], proj_use(n, 0, a) + 1)
            dve.tensor_tensor(pair(qp[par], a), banked(proj), two_tiles(g["bq1"]), ALU.add).then_inc(s["proj_out"], 1)

        def dve_unit_queries(dve, n, par):
            dve.wait_ge(s["root_done"], n + 1)
            dve.tensor_scalar(qnorm[:, :], qnorm[:, :], NORM_EPS, None, ALU.max).then_inc(s["norm_done"], 1)
            dve.wait_ge(s["norm_done"], n + 1)
            dve.reciprocal(qinv[:, :], qnorm[:, :]).then_inc(s["qinv_done"], 1)
            dve.wait_ge(s["qinv_done"], n + 1)
            for j in range(TJ):
                last = dve.tensor_scalar(qn[:, j, :], qp[par][:, j, :], qinv[:, j:j + 1], None, ALU.mult)
            last.then_inc(s["qn_ready"], 1)

        def dve_keys(dve, batch, f):
            for i in range(2):
                keys = f32(g["k1T"][i][:, f, ds(batch * KEYS, KEYS)]).unsqueeze(1).to_broadcast([P, HH, KEYS])
                last = dve.tensor_tensor(kbd[i][:, f, :, :], keys, g["head_rows"][:, :, :], ALU.mult)
            last.then_inc(s["kbd_ready"], 1)

        def dve_outputs(dve, n):
            dve.wait_ge(s["pv_mm"], NC3 * (n + 1))
            slots = [acc[j][:, 0:H3 * SLOT].rearrange("p (h d) -> p h d", d=SLOT) for j in range(TJ)]
            for j in range(TJ):
                last = dve.reciprocal(sums[:, j, :], slots[j][:, :, DH3])
            last.then_inc(s["sums_done"], 1)
            dve.wait_ge(s["sums_done"], n + 1)
            for j in range(TJ):
                last = dve.tensor_tensor(o[:, j, :].rearrange("p (h d) -> p h d", d=DH3), slots[j][:, :, 0:DH3],
                                         sums[:, j, :].unsqueeze(2).to_broadcast([P, H3, DH3]), ALU.mult)
            last.then_inc(s["o_ready"], 1)

        def dve_residual(dve, n, par, a):
            if a == 0:
                dve.wait_ge(s["qres_ready"], n + 1)
            dve.wait_ge(s["proj_mm"], proj_use(n, 1, a) + 1)
            dve.tensor_tensor(pair(y, a), banked(proj), pair(qres[par], a), ALU.add).then_inc(s["proj_out"], 1)

        def dve_y_stats(dve, n):
            dve.wait_ge(s["proj_out"], proj_use(n, 1, 1) + 1)
            layer_norm_stats(dve, lambda j: y[:, j, :], y_stats, y_mean_var, s["y_mv"])

        def dve_gamma(dve, n):
            dve.wait_ge(s["y_rstd"], n + 1)
            for j in range(TJ):
                last = dve.scalar_tensor_tensor(y[:, j, :], y[:, j, :], y_mean_var[:, j, 0:1], g["gamma"][:, :], ALU.subtract, ALU.mult)
            last.then_inc(s["y_gamma"], 1)

        def dve_update(dve, n):
            dve.wait_ge(s["y_gamma"], n + 1)
            dve.wait_ge(s["beta_added"], n + 1)
            for j in range(TJ):
                last = dve.scalar_tensor_tensor(x_tile(n)(j), y[:, j, :], y_rstd[:, j:j + 1], x_tile(n)(j), ALU.mult, ALU.add)

        def dve_block(dve, n, par, batch, next_batch, prv, nxt):
            if prv:
                dve_outputs(dve, n - 1)
            for c in range(NC3):
                rows = chunk(c)[2]
                dve.wait_ge(s["prob_hi"], NC3 * n + c + 1)
                dve.tensor_tensor(probT[slot(par, c)][1][0:rows, :], prob[slot(par, c)][0:rows, :], f32(probT[slot(par, c)][0][0:rows, :]),
                                  ALU.subtract).then_inc(s["prob_lo"], 1)
                if c == 0 and par == 0:
                    dve_keys(dve, batch, 1)
                if nxt and c == 0:
                    dve_stats(dve, n + 1)
                if prv and c in (1, 2):
                    dve_split(dve, n - 1, 2, c - 1, oT)
                if nxt and c == 1:
                    dve_normalize(dve, n + 1)
                if nxt and c in (3, 4):
                    dve_split(dve, n + 1, 0, c - 3, xnT)
                if prv and c in (3, 4):
                    dve_residual(dve, n - 1, 1 - par, c - 3)
                if nxt and c in (5, 6):
                    dve_queries(dve, n + 1, 1 - par, c - 5)
                if nxt and par == 1 and c == 7:
                    dve_keys(dve, next_batch, 0)
                if prv and c == 5:
                    dve_y_stats(dve, n - 1)
                if prv and c == 6:
                    dve_gamma(dve, n - 1)
                if nxt and c == 7:
                    dve_unit_queries(dve, n + 1, 1 - par)
                if nxt and c in (8, 9):
                    dve_split(dve, n + 1, 1, c - 8, qT[1 - par])
                if prv and c == 8:
                    dve_update(dve, n - 1)

        def gp_ln(gp, n):
            gp.wait_ge(s["mv_ready"], n + 1)
            inverse_std(gp, g, rstd, mean_var[:, :, 1], s["eps_done"], n + 1, s["rstd_ready"])

        def gp_root(gp, n):
            gp.wait_ge(s["ssq_done"], n + 1)
            gp.tensor_tensor(qnorm[:, :], qnorm[:, :], g["half"][:, :], ALU.pow).then_inc(s["root_done"], 1)

        def gp_residual(gp, n, par):
            gp.tensor_tensor(qres[par][:, :, :], qp[par][:, :, :], four_tiles(g["bo1"]), ALU.add).then_inc(s["qres_ready"], 1)

        def gp_beta(gp, n):
            gp.wait_ge(s["xn_ready"], n + 1)
            gp.tensor_tensor(x_block(n), x_block(n), four_tiles(g["beta"]), ALU.add).then_inc(s["beta_added"], 1)

        def gp_y(gp, n):
            gp.wait_ge(s["y_mv"], n + 1)
            inverse_std(gp, g, y_rstd, y_mean_var[:, :, 1], s["y_eps"], n + 1, s["y_rstd"])

        def gp_block(gp, n, par, batch, next_batch, prv, nxt):
            if nxt:
                gp_ln(gp, n + 1)
            if prv:
                gp_beta(gp, n - 1)
                gp_y(gp, n - 1)
            if nxt:
                gp_root(gp, n + 1)
                gp_residual(gp, n + 1, 1 - par)

        LOOPS = NBLK // 2 - 1

        def each_block(eng, body):
            body(eng, 0, 0, 0, 0, False, True)
            with eng.Fori(0, LOOPS) as it:
                body(eng, 2 * it + 1, 1, it, it + 1, True, True)
                body(eng, 2 * it + 2, 0, it + 1, it + 1, True, True)
            body(eng, NBLK - 1, 1, B - 1, B - 1, True, False)

        with nc.Block() as block:
            @block.gpsimd
            def _(gp):
                gp_ln(gp, 0)
                gp_root(gp, 0)
                gp_residual(gp, 0, 0)
                each_block(gp, gp_block)
                gp_beta(gp, NBLK - 1)
                gp_y(gp, NBLK - 1)

            @block.scalar
            def _(act):
                for dc in range(DC):
                    act_split(act, 0, 0, dc, xnT)
                act_squares(act, 0, 0)
                for dc in range(DC):
                    act_split(act, 0, 1, dc, qT[0])
                act_exp(act, 0, 0, 0)
                each_block(act, act_block)
                for dc in range(DC):
                    act_split(act, NBLK - 1, 2, dc, oT)

            @block.vector
            def _(dve):
                dve.sem_inc(s["o_ready"], 1)
                dve_stats(dve, 0)
                dve_keys(dve, 0, 0)
                dve_normalize(dve, 0)
                for dc in range(DC):
                    dve_split(dve, 0, 0, dc, xnT)
                for a in range(2):
                    dve_queries(dve, 0, 0, a)
                dve_unit_queries(dve, 0, 0)
                for dc in range(DC):
                    dve_split(dve, 0, 1, dc, qT[0])
                each_block(dve, dve_block)
                dve_outputs(dve, NBLK - 1)
                for dc in range(DC):
                    dve_split(dve, NBLK - 1, 2, dc, oT)
                for a in range(2):
                    dve_residual(dve, NBLK - 1, 1, a)
                dve_y_stats(dve, NBLK - 1)
                dve_gamma(dve, NBLK - 1)
                dve_update(dve, NBLK - 1)

            @block.tensor
            def _(pe):
                for part in range(6):
                    pe_front(pe, 0, part)
                for c in range(2):
                    pe_scores(pe, 0, 0, 0, c)
                each_block(pe, pe_block)
                for part in range(4):
                    pe_back(pe, NBLK - 1, part)


FP8_MAX = 448.0
AMAX_MIN = 1e-12
EXPONENT_BITS = 0x7F800000
FP8_MIN_NORMAL = 2.0 ** -6
ROUND_AT = 1.5 * 2.0 ** 20
QUANT_STEPS = 5


def quantize_step(dve, step, q, e, v, scale):
    if step == 0:
        return dve.tensor_scalar(q, v, scale, FP8_MAX, ALU.mult, ALU.min)
    if step == 1:
        return dve.tensor_scalar(e.bitcast(I32), q.bitcast(I32), EXPONENT_BITS, None, ALU.bitwise_and)
    if step == 2:
        return dve.tensor_scalar(e, e, FP8_MIN_NORMAL, ROUND_AT, ALU.max, ALU.mult)
    if step == 3:
        return dve.scalar_tensor_tensor(q, q, -FP8_MAX, e, ALU.max, ALU.add)
    return dve.tensor_tensor(q, q, e, ALU.subtract)


def last_layer_norm(nc, g):
    with ExitStack() as ctx:
        sb = lambda name, shape, dt: ctx.enter_context(nc.sbuf_tensor(name, shape, dt))
        stats = sb("stats5", [P, TJ, 6], F32)
        mean_var, rstd, shift = ([sb(f"{n}5_{s}", shape, F32) for s in range(2)]
                                 for n, shape in (("mean_var", [P, TJ, 2]), ("rstd", [P, TJ]), ("shift", [P, TJ])))
        names = ("mv_ready", "eps_done", "rstd_ready", "shift_ready", "shift_seen", "xf_ready")
        s = {n: ctx.enter_context(nc.semaphore(n + "5")) for n in names}

        def x_tile(n):
            return lambda j: g["x"][:, ds(n, 1), j, :].rearrange("p a d -> p (a d)")

        def dve_stats(dve, n, par):
            layer_norm_stats(dve, x_tile(n), stats, mean_var[par], s["mv_ready"])

        def dve_shift(dve, n, par):
            dve.wait_ge(s["rstd_ready"], n + 1)
            dve.scalar_tensor_tensor(shift[par][:, :], mean_var[par][:, :, 0], -1.0, rstd[par][:, :], ALU.mult, ALU.mult).then_inc(s["shift_ready"], 1)

        def dve_max(dve, n):
            dve.wait_ge(s["xf_ready"], n + 1)
            dve.tensor_reduce(g["xf_max"][:, ds(n, 1)], g["xf"][:, ds(n, 1), :, :].rearrange("p a j d -> p a (j d)"), AX_X, ALU.max,
                              apply_absolute_value=True)

        with nc.Block() as block:
            @block.gpsimd
            def _(gp):
                with gp.Fori(0, NBLK // 2) as it:
                    for a in range(2):
                        n = 2 * it + a
                        gp.wait_ge(s["mv_ready"], n + 1)
                        inverse_std(gp, g, rstd[a], mean_var[a][:, :, 1], s["eps_done"], n + 1, s["rstd_ready"])

            @block.scalar
            def _(act):
                with act.Fori(0, NBLK // 2) as it:
                    for a in range(2):
                        n = 2 * it + a
                        act.wait_ge(s["shift_ready"], n + 1)
                        act.sem_inc(s["shift_seen"], 1)
                        for j in range(TJ):
                            last = act.activation(g["xf"][:, ds(n, 1), j, :].rearrange("p a d -> p (a d)"), x_tile(n)(j), ACT.Identity,
                                                  scale=rstd[a][:, j:j + 1], bias=shift[a][:, j:j + 1])
                        last.then_inc(s["xf_ready"], 1)

            @block.vector
            def _(dve):
                dve_stats(dve, 0, 0)

                def body(n, par, nxt):
                    dve_shift(dve, n, par)
                    if nxt:
                        dve_stats(dve, n + 1, 1 - par)
                    dve_max(dve, n)
                with dve.Fori(0, NBLK // 2 - 1) as it:
                    for a in range(2):
                        body(2 * it + a, a, True)
                body(NBLK - 2, 0, True)
                body(NBLK - 1, 1, False)


def quantized_ffn(nc, g, w, out):
    with ExitStack() as ctx:
        sb = lambda name, shape, dt: ctx.enter_context(nc.sbuf_tensor(name, shape, dt))
        pb = lambda name: ctx.enter_context(nc.psum_tensor(name, [P, 512], F32))
        ws, we, wq = (sb(n, [P, DC, D], F32) for n in ("ffn_ws", "ffn_we", "ffn_wq"))
        wqT = sb("ffn_wqT", [P, DC, D], BF16)
        bias = sb("ffn_bias", [P, D], F32)
        amax = sb("amax", [P, 2], F32)
        limit, scale_row = sb("limit", [2, 2], F32), sb("scale_row", [2, 2, P], F32)
        scales, dequant = sb("scales", [P, 4], F32), sb("dequant", [P, 1], F32)
        e, q = sb("ffn_e", [P, TJ, D], F32), [sb(f"ffn_q{s}", [P, TJ, D], F32) for s in range(2)]
        qT = [sb(f"ffn_qT{s}", [P, DC, TB], BF16) for s in range(2)]
        z = [sb(f"ffn_z{s}", [P, TJ, D], BF16) for s in range(2)]
        tr = [pb(f"ffn_tr{s}") for s in range(2)]
        acc = [pb(f"ffn_acc{s}") for s in range(4)]
        small = pb("ffn_small")
        names = ("w_in", "bias_in", "amax_done", "small_mm", "limit_done", "wq_step", "wq_mm",
                 "wqT_out", "q_step", "q_ready", "tr_mm", "qT_out", "mm", "z_out", "x_done", "stored")
        s = {n: ctx.enter_context(nc.semaphore(n + "4")) for n in names}

        with nc.Block() as block:
            @block.sync
            def _(sp):
                sp.dma_start(ws[:, :, :], w["L1_ffn_weight"].rearrange("(c p) d -> p c d", p=P)).then_inc(s["w_in"], 16)
                sp.dma_start(bias[:, :], w["L1_ffn_bias"].partition_broadcast(P)).then_inc(s["bias_in"], 16)
                out_blocks = out.rearrange("b (n p j) d -> p (b n) j d", p=P, j=TJ)
                for n in range(NBLK):
                    sp.wait_ge(s["x_done"], n + 1)
                    sp.dma_start(out_blocks[:, n, :, :], g["x"][:, n, :, :]).then_inc(s["stored"], 16)
                sp.wait_ge(s["stored"], 16 * NBLK)

            @block.vector
            def _(dve):
                dve.tensor_reduce(amax[:, 0:1], g["xf_max"][:, :], AX_X, ALU.max)
                dve.wait_ge(s["w_in"], 16)
                dve.tensor_reduce(amax[:, 1:2], ws[:, :, :].rearrange("p c d -> p (c d)"), AX_X, ALU.max,
                                  apply_absolute_value=True).then_inc(s["amax_done"], 1)
                dve.wait_ge(s["small_mm"], 1)
                dve.tensor_reduce(limit[:, 0:1], small[0:2, 0:P], AX_X, ALU.max).then_inc(s["limit_done"], 1)
                dve.wait_ge(s["limit_done"], 1)
                dve.tensor_scalar(limit[:, 0:1], limit[:, 0:1], AMAX_MIN, None, ALU.max).then_inc(s["limit_done"], 1)
                dve.wait_ge(s["limit_done"], 2)
                dve.reciprocal(limit[:, 0:1], limit[:, 0:1]).then_inc(s["limit_done"], 1)
                dve.wait_ge(s["limit_done"], 3)
                dve.tensor_scalar(limit[:, 0:1], limit[:, 0:1], FP8_MAX, FP8_MAX, ALU.mult, ALU.min).then_inc(s["limit_done"], 1)
                dve.wait_ge(s["limit_done"], 4)
                dve.reciprocal(limit[:, 1:2], limit[:, 0:1]).then_inc(s["limit_done"], 1)
                dve.wait_ge(s["limit_done"], 5)
                dve.tensor_copy(scale_row[:, :, :], limit[:, :].unsqueeze(2).to_broadcast([2, 2, P])).then_inc(s["limit_done"], 1)
                dve.wait_ge(s["small_mm"], 2)
                dve.tensor_copy(scales[:, :], small[:, P:P + 4]).then_inc(s["limit_done"], 1)
                dve.wait_ge(s["limit_done"], 7)
                dve.tensor_tensor(dequant[:, :], scales[:, 2:3], scales[:, 3:4], ALU.mult)
                for step in range(QUANT_STEPS):
                    if step:
                        dve.wait_ge(s["wq_step"], step)
                    quantize_step(dve, step, wq[:, :, :], we[:, :, :], ws[:, :, :], scales[:, 1:2]).then_inc(s["wq_step"], 1)
                dve.wait_ge(s["bias_in"], 16)

                dve.sem_inc(s["q_step"], 1)

                def quantize(n, par, first):
                    xf = g["xf"][:, ds(n, 1), :, :].rearrange("p a j d -> p (a j) d")
                    for step in range(QUANT_STEPS):
                        if step or not first:
                            dve.wait_ge(s["q_step"], (QUANT_STEPS) * n + step + 1)
                        if step == 0 and not first:
                            dve.wait_ge(s["tr_mm"], DC * n - DC)
                        last = quantize_step(dve, step, q[par][:, :, :], e[:, :, :], xf, scales[:, 0:1])
                        last.then_inc(s["q_step"], 1)

                def finish(n, par):
                    for a in range(2):
                        dve.wait_ge(s["mm"], 2 * n + a + 1)
                        for b in range(2):
                            j = 2 * a + b
                            last = dve.scalar_tensor_tensor(z[par][:, j, :], acc[2 * par + a][:, b * D:(b + 1) * D], dequant[:, 0:1], bias[:, :],
                                                            ALU.mult, ALU.add)
                        last.then_inc(s["z_out"], 1)

                for n in range(NBLK + 1):
                    if n < NBLK:
                        quantize(n, n % 2, n == 0)
                    if n >= 1:
                        if n >= 3:
                            dve.wait_ge(s["x_done"], n - 2)
                        finish(n - 1, (n - 1) % 2)

            @block.gpsimd
            def _(gp):
                for n in range(NBLK):
                    gp.wait_ge(s["z_out"], 2 * n + 2)
                    gp.tensor_tensor(g["x"][:, n, :, :], g["x"][:, n, :, :], z[n % 2][:, :, :], ALU.add).then_inc(s["x_done"], 1)

            @block.scalar
            def _(act):
                for c in range(DC):
                    act.wait_ge(s["wq_mm"], c + 1)
                    act.activation(wqT[:, c, :], tr[c][:, 0:D], ACT.Copy).then_inc(s["wqT_out"], 1)
                for n in range(NBLK):
                    if n >= 2:
                        act.wait_ge(s["mm"], 2 * n - 2)
                    for dc in range(DC):
                        act.wait_ge(s["tr_mm"], DC * n + dc + 1)
                        act.activation(qT[n % 2][:, dc, :], tr[dc][:, :], ACT.Copy).then_inc(s["qT_out"], 1)

            @block.tensor
            def _(pe):
                pe.wait_ge(s["amax_done"], 1)
                pe.transpose(small[0:2, 0:P], amax[:, :], g["ident"][:, :]).then_inc(s["small_mm"], 1)
                pe.wait_ge(s["limit_done"], 6)
                for i in range(2):
                    last = pe.transpose(small[:, P + 2 * i:P + 2 * i + 2], scale_row[:, i, :], g["ident"][0:2, 0:2])
                last.then_inc(s["small_mm"], 1)
                pe.wait_ge(s["wq_step"], QUANT_STEPS)
                for c in range(DC):
                    for r in range(DC):
                        last = pe.transpose(tr[c][:, r * P:(r + 1) * P], wq[:, r, c * P:(c + 1) * P], g["ident"][:, :])
                    last.then_inc(s["wq_mm"], 1)

                def transposes(n):
                    pe.wait_ge(s["q_step"], QUANT_STEPS * (n + 1) + 1)
                    for dc in range(DC):
                        if n == 0:
                            pe.wait_ge(s["wqT_out"], dc + 1)
                        else:
                            pe.wait_ge(s["qT_out"], DC * (n - 1) + dc + 1)
                        for j in range(TJ):
                            last = pe.transpose(tr[dc][:, j * P:(j + 1) * P], q[n % 2][:, j, dc * P:(dc + 1) * P], g["ident"][:, :])
                        last.then_inc(s["tr_mm"], 1)

                def products(n):
                    pe.wait_ge(s["qT_out"], DC * (n + 1))
                    if n >= 2:
                        pe.wait_ge(s["z_out"], 2 * n - 2)
                    for a in range(2):
                        for b in range(2):
                            j = 2 * a + b
                            for dc in range(DC):
                                last = pe.matmul(acc[2 * (n % 2) + a][:, b * D:(b + 1) * D], qT[n % 2][:, dc, j * P:(j + 1) * P], wqT[:, dc, :],
                                                 start=(dc == 0), stop=(dc == DC - 1))
                        last.then_inc(s["mm"], 1)

                for n in range(NBLK + 1):
                    if n < NBLK:
                        transposes(n)
                    if n >= 1:
                        products(n - 1)


def program(nc, w, out):
    with ExitStack() as ctx:
        g = {}
        sb = lambda name, shape, dt: ctx.enter_context(nc.sbuf_tensor(name, shape, dt))
        g["x"] = sb("x_res", [P, NBLK, TJ, D], F32)
        g["ident"] = sb("ident", [P, P], F32)
        g["minus_half"] = sb("minus_half", [P, TJ], F32)
        g["eps"] = sb("eps", [P, TJ], F32)
        g["half"] = sb("half", [P, TJ], F32)
        with ExitStack() as weights0:
            attention0_weights(nc, g, w, weights0)
            attention0(nc, g)
        weight_rows = nc.dram_tensor("weight_rows", (E, TB), F32, kind="Internal").ap()
        with ExitStack() as weights1:
            experts_weights(nc, g, w, weights1)
            experts(nc, g, weight_rows)
        with ExitStack() as weights3:
            attention1_weights(nc, g, w, weights3)
            attention1(nc, g)
        g["xf"] = sb("xf", [P, NBLK, TJ, D], F32)
        g["xf_max"] = sb("xf_max", [P, NBLK], F32)
        last_layer_norm(nc, g)
        quantized_ffn(nc, g, w, out)


INPUTS = ['x', 'ctx_768', 'L0_xattn_Wq', 'L0_xattn_Wk', 'L0_xattn_Wv', 'L0_xattn_Wo', 'L0_xattn_bo', 'L0_ffn_gate_w',
          'L0_ffn_W1', 'L0_ffn_W2', 'L0_ffn_Ws1', 'L0_ffn_Ws2', 'L1_xattn_Wq', 'L1_xattn_bq', 'L1_xattn_Wk', 'L1_xattn_bk',
          'L1_xattn_Wv', 'L1_xattn_bv', 'L1_xattn_Wo', 'L1_xattn_bo', 'L1_xattn_ln_gamma', 'L1_xattn_ln_beta',
          'L1_ffn_weight', 'L1_ffn_bias']


def kernel(**inputs):
    import numpy as np
    import concourse.bacc as bacc
    from concourse.bass_utils import run_bass_kernel_spmd

    nc = bacc.Bacc("TRN2", target_bir_lowering=False, num_devices=1)
    arrays, views = {}, {}
    for name in INPUTS:
        a = np.ascontiguousarray(inputs[name])
        arrays["in_" + name] = a
        views[name] = nc.dram_tensor("in_" + name, a.shape, mybir.dt.from_np(a.dtype), kind="ExternalInput").ap()
    out = nc.dram_tensor("out", (B, N, D), F32, kind="ExternalOutput").ap()
    program(nc, views, out)
    r = run_bass_kernel_spmd(nc, [arrays], core_ids=[0])
    return r.results[0]["out"]
```

```python
from contextlib import ExitStack

import concourse.bass as bass
from concourse import mybir

ALU = mybir.AluOpType
ACT = mybir.ActivationFunctionType
AX_X = mybir.AxisListType.X
F32 = mybir.dt.float32
F32R = mybir.dt.float32r
BF16 = mybir.dt.bfloat16
I32 = mybir.dt.int32
ds = bass.ds

P = 128
D = 256
DC = D // P
B, N = 4, 1024
T = B * N
TB = 512
TJ = TB // P
NBLK = T // TB
BPB = N // TB
KEYS = 77
CTX = 192
CC, CP = 2, 96
CK = B * KEYS
HEADS = 16
LN_EPS = 1e-5

HI_LO_PASSES = ((0, 0), (0, 1), (1, 0))


def f32(ap):
    return ap.bitcast(F32)


def layer_norm_stats(dve, x_tile, stats, mean_var, ready_sem):
    for j in range(TJ):
        dve.bn_stats(stats[:, j, :], x_tile(j))
    dve.drain()
    for j in range(TJ):
        last = dve.bn_aggr(mean_var[:, j, :], stats[:, j, :])
    last.then_inc(ready_sem, 1)


def inverse_std(gp, g, rstd, var, eps_sem, eps_count, ready_sem):
    gp.tensor_tensor(rstd[:, :], var, g["eps"][:, :], ALU.add).then_inc(eps_sem, 1)
    gp.wait_ge(eps_sem, eps_count)
    gp.tensor_tensor(rstd[:, :], rstd[:, :], g["minus_half"][:, :], ALU.pow).then_inc(ready_sem, 1)


FP8_MAX = 448.0
AMAX_MIN = 1e-12
EXPONENT_BITS = 0x7F800000
FP8_MIN_NORMAL = 2.0 ** -6
ROUND_AT = 1.5 * 2.0 ** 20


def ffn_scales(dve, limit, scale_row, amax, done):
    dve.tensor_reduce(limit[:, 0:1], amax, AX_X, ALU.max).then_inc(done, 1)
    dve.wait_ge(done, 1)
    dve.tensor_scalar(limit[:, 0:1], limit[:, 0:1], AMAX_MIN, None, ALU.max).then_inc(done, 1)
    dve.wait_ge(done, 2)
    dve.reciprocal(limit[:, 0:1], limit[:, 0:1]).then_inc(done, 1)
    dve.wait_ge(done, 3)
    dve.tensor_scalar(limit[:, 0:1], limit[:, 0:1], FP8_MAX, FP8_MAX, ALU.mult, ALU.min).then_inc(done, 1)
    dve.wait_ge(done, 4)
    dve.reciprocal(limit[:, 1:2], limit[:, 0:1]).then_inc(done, 1)
    dve.wait_ge(done, 5)
    dve.tensor_copy(scale_row[:, :, :], limit[:, :].unsqueeze(2).to_broadcast([1, 2, P])).then_inc(done, 1)


def ffn_scale_buffers(sb, name):
    return sb(name + "_amax", [P, 1], F32), sb(name + "_limit", [1, 2], F32), sb(name + "_scale_row", [1, 2, P], F32)


def ffn_transpose_amax(pe, g, small, amax, done):
    pe.transpose(small[0:1, 0:P], amax[:, :], g["ident"][:, :]).then_inc(done, 1)


def ffn_spread_scales(pe, g, small, scale_row, done):
    for i in range(2):
        last = pe.transpose(small[:, P + i:P + i + 1], scale_row[:, i, :], g["ident"][0:1, 0:1])
    last.then_inc(done, 1)


H0, DH0 = HEADS, 64
INNER0 = H0 * DH0
PAIRS = INNER0 // P
HK = H0 * KEYS
PAIR_COLS = 2 * KEYS
KCH = -(-HK // P)
OUT_PARTS = ((0, 1), (1, 3), (3, KCH))
BANK_HEADS = (6, 6, 4)
BANK_HEAD0 = (0, 6, 12)
TR_GROUPS = ((0, 4), (4, 4), (8, 2))
VZ_STEP = PAIR_COLS + P
U_TERMS = [[p for p in range(PAIRS) if PAIR_COLS * p < P * (c + 1) and PAIR_COLS * (p + 1) > P * c]
           for c in range(KCH)]
M_GROUPS = [(dc, p0, np) for dc in range(DC) for p0, np in ((0, 3), (3, 3), (6, 2))]
PREP_USES = len(M_GROUPS) + KCH // 2
TILES = BPB * TJ


def attention0_weights(nc, g, w, ctx):
    sb = lambda name, shape, dt: ctx.enter_context(nc.sbuf_tensor(name, shape, dt))
    g["wqT"] = [sb(f"wqT{i}", [P, PAIRS, D], F32R) for i in range(2)]
    g["wo"] = [sb(f"wo{i}", [P, PAIRS, D], F32R) for i in range(2)]
    g["kT"] = sb("kT", [P, PAIRS, CK], F32)
    g["vT"] = sb("vT", [P, PAIRS, CK], F32)
    g["kbd"] = [sb(f"kbd{i}", [P, PAIRS, PAIR_COLS], F32R) for i in range(2)]
    g["vz"] = [sb(f"vz{i}", [P, PAIRS * VZ_STEP], F32R) for i in range(2)]
    g["bo0"] = sb("bo0", [P, D], F32)
    with ExitStack() as tmp:
        t = lambda name, shape, dt: tmp.enter_context(nc.sbuf_tensor(name, shape, dt))
        sem = lambda name: tmp.enter_context(nc.semaphore(name))
        ctxs = t("ctxs", [KEYS, B, CTX], F32)
        ctxT = [t(f"ctxT{i}", [CP, CC, CK], F32R) for i in range(2)]
        wqs = t("wqs", [P, DC, INNER0], F32)
        wos = t("wos", [P, PAIRS, D], F32)
        wks = t("wks", [CP, CC, INNER0], F32)
        wvs = t("wvs", [CP, CC, INNER0], F32)
        wk = [t(f"wk{i}", [CP, CC, INNER0], F32R) for i in range(2)]
        wv = [t(f"wv{i}", [CP, CC, INNER0], F32R) for i in range(2)]
        bank = [tmp.enter_context(nc.psum_tensor(f"w0_bank{i}", [P, 512], F32)) for i in range(8)]
        ctx_in, wq_in, wo_in, wk_in, wv_in, bo_in, x_in = (
            sem(n) for n in ("ctx_in", "wq_in", "wo_in", "wk_in", "wv_in", "bo_in", "x_in"))
        ident_zero, ident_done = sem("ident_zero"), sem("ident_done")
        w_hi, bank_mm, bank_hi, bank_lo, w_lo = (
            sem(n) for n in ("w_hi", "bank_mm", "bank_hi", "bank_lo", "w_lo"))
        k_out, v_out = sem("k_out"), sem("v_out")
        K_USE, V_USE = 6, 6 + PAIRS

        with nc.Block() as block:
            @block.sync
            def _(sp):
                sp.dma_start(ctxs[:, :, :], w["ctx_768"].rearrange("b k c -> k b c")).then_inc(ctx_in, 16)
                for dst, src, s in ((wks, w["L0_xattn_Wk"], wk_in), (wvs, w["L0_xattn_Wv"], wv_in)):
                    sp.dma_start(dst[:, :, :], src.rearrange("(c p) n -> p c n", p=CP)).then_inc(s, 16)
                sp.dma_start(wqs[:, :, :], w["L0_xattn_Wq"].rearrange("(c p) n -> p c n", p=P)).then_inc(wq_in, 16)
                sp.dma_start(wos[:, :, :], w["L0_xattn_Wo"].rearrange("(c p) n -> p c n", p=P)).then_inc(wo_in, 16)
                sp.dma_start(g["bo0"][:, :], w["L0_xattn_bo"].partition_broadcast(P)).then_inc(bo_in, 16)
                sp.dma_start(g["x"][:, :, :, :], w["x"].rearrange("b (n p j) d -> p (b n) j d", p=P, j=TJ)).then_inc(x_in, 16)
                sp.wait_ge(bo_in, 16)
                sp.wait_ge(x_in, 16)

            @block.gpsimd
            def _(gp):
                gp.memset(g["ident"][:, :], 0.0).then_inc(ident_zero, 1)
                gp.wait_ge(ident_zero, 1)
                gp.affine_select(out=g["ident"][:, :], in_=g["ident"][:, :], compare_op=ALU.not_equal, fill=1.0,
                                 base=0, pattern=[[-1, P]], channel_multiplier=1).then_inc(ident_done, 1)
                gp.memset(g["minus_half"][:, :], -0.5)
                gp.memset(g["half"][:, :], 0.5)
                gp.memset(g["eps"][:, :], LN_EPS)
                for i in range(2):
                    gp.memset(f32(g["kbd"][i][:, :, :]), 0.0)
                    gp.memset(f32(g["vz"][i][:, :]), 0.0)

            @block.scalar
            def _(act):
                act.wait_ge(wk_in, 16)
                act.activation(wk[0][:, :, :], wks[:, :, :], ACT.Copy).then_inc(w_hi, 1)
                act.wait_ge(wv_in, 16)
                act.activation(wv[0][:, :, :], wvs[:, :, :], ACT.Copy).then_inc(w_hi, 1)
                for c in range(CC):
                    act.wait_ge(bank_mm, c + 1)
                    act.activation(ctxT[0][:, c, :], bank[c][0:CP, 0:CK], ACT.Copy).then_inc(bank_hi, 1)
                for u in range(2, K_USE):
                    act.wait_ge(bank_mm, u + 1)
                    act.activation(g["wqT"][0][:, 2 * (u - 2):2 * (u - 1), :], bank[u][:, :].rearrange("p (a d) -> p a d", a=2),
                                   ACT.Copy, scale=DH0 ** -0.5).then_inc(bank_hi, 1)
                act.wait_ge(wo_in, 16)
                act.activation(g["wo"][0][:, :, :], wos[:, :, :], ACT.Copy).then_inc(w_hi, 1)
                for p in range(PAIRS):
                    act.wait_ge(bank_mm, K_USE + p + 1)
                    act.activation(g["kT"][:, p, :], bank[(K_USE + p) % 8][:, 0:CK], ACT.Copy).then_inc(k_out, 1)

            @block.vector
            def _(dve):
                dve.wait_ge(w_hi, 1)
                dve.tensor_tensor(wk[1][:, :, :], wks[:, :, :], f32(wk[0][:, :, :]), ALU.subtract).then_inc(w_lo, 1)
                dve.wait_ge(w_hi, 2)
                dve.tensor_tensor(wv[1][:, :, :], wvs[:, :, :], f32(wv[0][:, :, :]), ALU.subtract).then_inc(w_lo, 1)
                for c in range(CC):
                    dve.wait_ge(bank_hi, c + 1)
                    dve.tensor_tensor(ctxT[1][:, c, :], bank[c][0:CP, 0:CK], f32(ctxT[0][:, c, :]),
                                      ALU.subtract).then_inc(bank_lo, 1)
                for u in range(2, K_USE):
                    dve.wait_ge(bank_hi, u + 1)
                    pair2 = slice(2 * (u - 2), 2 * (u - 1))
                    dve.scalar_tensor_tensor(g["wqT"][1][:, pair2, :], bank[u][:, :].rearrange("p (a d) -> p a d", a=2),
                                             DH0 ** -0.5, f32(g["wqT"][0][:, pair2, :]), ALU.mult, ALU.subtract).then_inc(bank_lo, 1)
                dve.wait_ge(w_hi, 3)
                dve.tensor_tensor(g["wo"][1][:, :, :], wos[:, :, :], f32(g["wo"][0][:, :, :]), ALU.subtract)
                for p in range(PAIRS):
                    dve.wait_ge(bank_mm, V_USE + p + 1)
                    dve.tensor_copy(g["vT"][:, p, :], bank[(V_USE + p) % 8][:, 0:CK]).then_inc(v_out, 1)

            @block.tensor
            def _(pe):
                pe.wait_ge(ident_done, 1)
                pe.wait_ge(ctx_in, 16)
                for c in range(CC):
                    for b in range(B):
                        last = pe.transpose(bank[c][0:CP, b * KEYS:(b + 1) * KEYS], ctxs[:, b, c * CP:(c + 1) * CP],
                                            g["ident"][0:KEYS, 0:KEYS])
                    last.then_inc(bank_mm, 1)
                pe.wait_ge(wq_in, 16)
                for u in range(2, K_USE):
                    for a in range(2):
                        for dc in range(DC):
                            pair = 2 * (u - 2) + a
                            last = pe.transpose(bank[u][:, a * D + dc * P:a * D + (dc + 1) * P],
                                                wqs[:, dc, pair * P:(pair + 1) * P], g["ident"][:, :])
                    last.then_inc(bank_mm, 1)
                pe.wait_ge(w_lo, 2)
                pe.wait_ge(bank_lo, CC)
                for first_use, weight in ((K_USE, wk), (V_USE, wv)):
                    for p in range(PAIRS):
                        u = first_use + p
                        if u >= V_USE:
                            pe.wait_ge(k_out, u - 8 - K_USE + 1)
                        elif u >= 8:
                            pe.wait_ge(bank_lo, u - 8 + 1)
                        for n, (i, k) in enumerate(HI_LO_PASSES):
                            for c in range(CC):
                                last = pe.matmul(bank[u % 8][:, 0:CK], weight[i][:, c, p * P:(p + 1) * P], ctxT[k][:, c, :],
                                                 start=(n == 0 and c == 0), stop=(n == 2 and c == CC - 1))
                        last.then_inc(bank_mm, 1)


TR_BEGIN = [("x", 0, dc) for dc in range(DC)] + [("p", 0, gr) for gr in range(len(TR_GROUPS))]
TR_BATCH = [use for t in range(1, TILES) for use in
            [("p", t, gr) for gr in range(len(TR_GROUPS))] + ([("x", 1, dc) for dc in range(DC)] if t == 2 else [])] + TR_BEGIN


def transpose_use0(b, *use):
    if use in TR_BEGIN:
        if isinstance(b, int) and b == 0:
            return TR_BEGIN.index(use)
        return len(TR_BEGIN) + len(TR_BATCH) * (b - 1) + TR_BATCH.index(use)
    return len(TR_BEGIN) + len(TR_BATCH) * b + TR_BATCH.index(use)


def attention0(nc, g):
    with ExitStack() as ctx:
        sb = lambda name, shape, dt: ctx.enter_context(nc.sbuf_tensor(name, shape, dt))
        sem = lambda name: ctx.enter_context(nc.semaphore(name))
        m = [sb(f"m{i}", [P, DC, HK], F32R) for i in range(2)]
        u = [sb(f"u{i}", [P, KCH, D], F32R) for i in range(2)]
        xn = sb("xn0", [P, TJ, D], F32)
        xnT = [[sb(f"xnT0_{blk}_{i}", [P, DC, TB], F32R) for i in range(2)] for blk in range(BPB)]
        stats, mean_var, rstd = sb("stats0", [P, TJ, 6], F32), sb("mean_var0", [P, TJ, 2], F32), sb("rstd0", [P, TJ], F32)
        prob = [sb(f"prob{s}", [P, HK], F32) for s in range(2)]
        probT = [[sb(f"probT{s}_{i}", [P, KCH, P], F32R) for i in range(2)] for s in range(2)]
        neg_max = [sb(f"neg_max{s}", [P, H0], F32) for s in range(2)]
        row_sum, row_inv = sb("row_sum", [P, H0], F32), [sb(f"row_inv{s}", [P, H0], F32) for s in range(2)]
        score = [[ctx.enter_context(nc.psum_tensor(f"score{s}_{k}", [P, 512], F32)) for k in range(3)] for s in range(2)]
        tr = ctx.enter_context(nc.psum_tensor("tr0", [P, 512], F32))
        acc = ctx.enter_context(nc.psum_tensor("acc0", [P, 512], F32))
        prep_bank = [score[n // 3][n % 3] for n in range(len(M_GROUPS))] + [score[1][n % 3] for n in range(KCH // 2)]
        (bd_hi, bd_lo, prep_mm, prep_hi, prep_lo, mv_ready, eps_done, rstd_ready, xn_ready, bo_added,
         tr_mm, tr_hi, tr_lo, score_mm, max_ready, exp_done, sum_done, inv_ready, prob_ready, out_mm, out_added) = (
            sem(n + "0") for n in (
                "bd_hi", "bd_lo", "prep_mm", "prep_hi", "prep_lo", "mv_ready", "eps_done", "rstd_ready",
                "xn_ready", "bo_added", "tr_mm", "tr_hi", "tr_lo", "score_mm", "max_ready", "exp_done", "sum_done",
                "inv_ready", "prob_ready", "out_mm", "out_added"))
        NB = len(BANK_HEADS)
        TB_BANKS = TILES * NB

        def heads(k):
            return slice(BANK_HEAD0[k], BANK_HEAD0[k] + BANK_HEADS[k])

        def cols(k):
            return slice(BANK_HEAD0[k] * KEYS, (BANK_HEAD0[k] + BANK_HEADS[k]) * KEYS)

        def probs_of(t, k):
            return prob[t % 2][:, cols(k)].rearrange("p (h k) -> p h k", k=KEYS)

        def scores_of(t, k):
            return score[t % 2][k][:, 0:BANK_HEADS[k] * KEYS].rearrange("p (h k) -> p h k", k=KEYS)

        def diagonal(i, half):
            r = slice(half * DH0, (half + 1) * DH0)
            k = g["kbd"][i][r, :, half * KEYS:(half + 1) * KEYS]
            v = g["vz"][i][r, :].rearrange("q (p w) -> q p w", w=VZ_STEP)[:, :, half * KEYS:(half + 1) * KEYS]
            return r, k, v

        def first(b):
            return isinstance(b, int) and b == 0

        def each_batch(eng, begin, batch):
            begin(0)
            with eng.Fori(0, B - 1) as it:
                batch(it, True)
            batch(B - 1, False)

        def x_tile(b, blk):
            return lambda j: g["x"][:, ds(b * BPB + blk, 1), j, :].rearrange("p a d -> p (a d)")

        with nc.Block() as block:
            @block.gpsimd
            def _(gp):
                def normalize(b, t):
                    for k in range(NB):
                        gp.wait_ge(inv_ready, b * TB_BANKS + t * NB + k + 1)
                        pr = probs_of(t, k)
                        gp.tensor_tensor(pr, pr, row_inv[t % 2][:, heads(k)].unsqueeze(2).to_broadcast([P, BANK_HEADS[k], KEYS]),
                                         ALU.mult).then_inc(prob_ready, 1)

                def block_rstd(b, blk):
                    gp.wait_ge(mv_ready, b * BPB + blk + 1)
                    inverse_std(gp, g, rstd, mean_var[:, :, 1], eps_done, b * BPB + blk + 1, rstd_ready)

                def add_bo(b, blk):
                    gp.wait_ge(xn_ready, b * BPB + blk + 1)
                    xb = g["x"][:, ds(b * BPB + blk, 1), :, :].rearrange("p a j d -> p (a j) d")
                    gp.tensor_tensor(xb, xb, g["bo0"][:, :].unsqueeze(1).to_broadcast([P, TJ, D]), ALU.add).then_inc(bo_added, 1)

                def first_tiles(b):
                    normalize(b, 0)
                    block_rstd(b, 1)
                    normalize(b, 1)

                def begin(b):
                    block_rstd(b, 0)
                    add_bo(b, 0)
                    first_tiles(b)

                def batch(b, nxt):
                    for t in range(TILES - 2):
                        normalize(b, t + 2)
                        if t == 1:
                            add_bo(b, 1)
                        if nxt and t == 4:
                            block_rstd(b + 1, 0)
                    if nxt:
                        add_bo(b + 1, 0)
                        first_tiles(b + 1)
                each_batch(gp, begin, batch)

            @block.scalar
            def _(act):
                def diagonals(b, kind):
                    for half in range(2):
                        r, *dst = diagonal(0, half)
                        act.activation(dst[kind], (g["kT"], g["vT"])[kind][r, :, ds(b * KEYS, KEYS)], ACT.Copy).then_inc(bd_hi, 1)

                def split_x(b, blk, dc):
                    act.wait_ge(tr_mm, transpose_use0(b, "x", blk, dc) + 1)
                    act.activation(xnT[blk][0][:, dc, :], tr[:, :], ACT.Copy).then_inc(tr_hi, 1)

                def split_p(b, t, gr):
                    c0, n = TR_GROUPS[gr]
                    act.wait_ge(tr_mm, transpose_use0(b, "p", t, gr) + 1)
                    if t >= 2 or not first(b):
                        act.wait_ge(out_mm, b * TILES + t - 1)
                    act.activation(probT[t % 2][0][:, c0:c0 + n, :], tr[:, 0:n * P].rearrange("p (c q) -> p c q", q=P),
                                   ACT.Copy).then_inc(tr_hi, 1)

                def exps(b, t, k):
                    act.wait_ge(max_ready, b * TB_BANKS + t * NB + k + 1)
                    if k == 0 and t >= 2:
                        act.wait_ge(tr_mm, transpose_use0(b, "p", t - 2, 2) + 1)
                    elif k == 0 and not first(b):
                        act.wait_ge(tr_mm, transpose_use0(b - 1, "p", TILES + t - 2, 2) + 1)
                    for n, h in enumerate(range(BANK_HEAD0[k], BANK_HEAD0[k] + BANK_HEADS[k])):
                        last = act.activation(prob[t % 2][:, h * KEYS:(h + 1) * KEYS],
                                              score[t % 2][k][:, n * KEYS:(n + 1) * KEYS], ACT.Exp,
                                              bias=neg_max[t % 2][:, h:h + 1])
                    last.then_inc(exp_done, 1)

                def split_m(b, n):
                    act.wait_ge(prep_mm, b * PREP_USES + n + 1)
                    dc, p0, np = M_GROUPS[n]
                    act.activation(m[0][:, dc, p0 * PAIR_COLS:(p0 + np) * PAIR_COLS], prep_bank[n][:, 0:np * PAIR_COLS],
                                   ACT.Copy).then_inc(prep_hi, 1)

                def split_u(b):
                    for n in range(len(M_GROUPS), PREP_USES):
                        act.wait_ge(prep_mm, b * PREP_USES + n + 1)
                        c = 2 * (n - len(M_GROUPS))
                        act.activation(u[0][:, c:c + 2, :], prep_bank[n][:, :].rearrange("p (c d) -> p c d", d=D),
                                       ACT.Copy).then_inc(prep_hi, 1)

                def step(b, t, bs, ts):
                    split_p(b, t, 0)
                    split_p(b, t, 1)
                    exps(bs, ts, 0)
                    split_p(b, t, 2)
                    exps(bs, ts, 1)
                    exps(bs, ts, 2)

                def first_tiles(b):
                    for k in range(NB):
                        exps(b, 0, k)
                    split_u(b)
                    step(b, 0, b, 1)

                def begin(b):
                    for kind in range(2):
                        diagonals(b, kind)
                    for dc in range(DC):
                        split_x(b, 0, dc)
                    for n in range(len(M_GROUPS)):
                        split_m(b, n)
                    first_tiles(b)

                def batch(b, nxt):
                    for t in range(TILES - 2):
                        step(b, t + 1, b, t + 2)
                        if t == 1:
                            for dc in range(DC):
                                split_x(b, 1, dc)
                        if nxt and t in (2, 3):
                            diagonals(b + 1, t - 2)
                    for k in range(NB):
                        split_p(b, TILES - 1, k)
                        if nxt:
                            split_m(b + 1, k)
                    if nxt:
                        split_x(b + 1, 0, 0)
                        split_m(b + 1, 3)
                        split_m(b + 1, 4)
                        split_x(b + 1, 0, 1)
                        split_m(b + 1, 5)
                        first_tiles(b + 1)
                each_batch(act, begin, batch)

            @block.vector
            def _(dve):
                def diagonals(b, kind):
                    for half in range(2):
                        r, *hi = diagonal(0, half)
                        r, *lo = diagonal(1, half)
                        dve.wait_ge(bd_hi, b * 4 + kind * 2 + half + 1)
                        dve.tensor_tensor(lo[kind], (g["kT"], g["vT"])[kind][r, :, ds(b * KEYS, KEYS)], f32(hi[kind]),
                                          ALU.subtract).then_inc(bd_lo, 1)

                def stats_of(b, blk):
                    layer_norm_stats(dve, x_tile(b, blk), stats, mean_var, mv_ready)

                def norm_of(b, blk):
                    dve.wait_ge(rstd_ready, b * BPB + blk + 1)
                    for j in range(TJ):
                        last = dve.tensor_scalar(xn[:, j, :], x_tile(b, blk)(j), mean_var[:, j, 0:1], rstd[:, j:j + 1],
                                                 ALU.subtract, ALU.mult)
                    last.then_inc(xn_ready, 1)

                def split_x(b, blk, dc):
                    dve.wait_ge(tr_hi, transpose_use0(b, "x", blk, dc) + 1)
                    dve.tensor_tensor(xnT[blk][1][:, dc, :], tr[:, :], f32(xnT[blk][0][:, dc, :]), ALU.subtract).then_inc(tr_lo, 1)

                def split_p(b, t, gr):
                    c0, n = TR_GROUPS[gr]
                    dve.wait_ge(tr_hi, transpose_use0(b, "p", t, gr) + 1)
                    dve.tensor_tensor(probT[t % 2][1][:, c0:c0 + n, :], tr[:, 0:n * P].rearrange("p (c q) -> p c q", q=P),
                                      f32(probT[t % 2][0][:, c0:c0 + n, :]), ALU.subtract).then_inc(tr_lo, 1)

                def maxima(b, t, k):
                    dve.wait_ge(score_mm, b * TB_BANKS + t * NB + k + 1)
                    dve.tensor_reduce(neg_max[t % 2][:, heads(k)], scores_of(t, k), AX_X, ALU.max, negate=True).then_inc(max_ready, 1)

                def sums(b, t, banks=range(NB)):
                    for k in banks:
                        dve.wait_ge(exp_done, b * TB_BANKS + t * NB + k + 1)
                        dve.tensor_reduce(row_sum[:, heads(k)], probs_of(t, k), AX_X, ALU.add).then_inc(sum_done, 1)
                        dve.wait_ge(sum_done, b * TB_BANKS + t * NB + k + 1)
                        dve.reciprocal(row_inv[t % 2][:, heads(k)], row_sum[:, heads(k)]).then_inc(inv_ready, 1)

                def split_m(b, n):
                    dve.wait_ge(prep_hi, b * PREP_USES + n + 1)
                    dc, p0, np = M_GROUPS[n]
                    c = slice(p0 * PAIR_COLS, (p0 + np) * PAIR_COLS)
                    dve.tensor_tensor(m[1][:, dc, c], prep_bank[n][:, 0:np * PAIR_COLS], f32(m[0][:, dc, c]),
                                      ALU.subtract).then_inc(prep_lo, 1)

                def split_u(b):
                    for n in range(len(M_GROUPS), PREP_USES):
                        dve.wait_ge(prep_hi, b * PREP_USES + n + 1)
                        c = 2 * (n - len(M_GROUPS))
                        dve.tensor_tensor(u[1][:, c:c + 2, :], prep_bank[n][:, :].rearrange("p (c d) -> p c d", d=D),
                                          f32(u[0][:, c:c + 2, :]), ALU.subtract).then_inc(prep_lo, 1)

                def add_out(b, t):
                    blk, j = divmod(t, TJ)
                    dve.wait_ge(out_mm, b * TILES + t + 1)
                    if j == 0:
                        dve.wait_ge(bo_added, b * BPB + blk + 1)
                    dve.tensor_tensor(x_tile(b, blk)(j), acc[:, 0:D], x_tile(b, blk)(j), ALU.add).then_inc(out_added, 1)

                def step(b, t, bs, ts):
                    for k in range(NB):
                        split_p(b, t, k)
                        maxima(bs, ts, k)
                        if k == 1:
                            sums(bs, ts, range(1))

                def first_tiles(b, ended):
                    for k in range(NB):
                        maxima(b, 0, k)
                    if not first(b):
                        add_out(ended, TILES - 1)
                    sums(b, 0)
                    split_u(b)
                    stats_of(b, 1)
                    step(b, 0, b, 1)
                    sums(b, 1, range(1, NB))

                def begin(b):
                    stats_of(b, 0)
                    for kind in range(2):
                        diagonals(b, kind)
                    norm_of(b, 0)
                    for dc in range(DC):
                        split_x(b, 0, dc)
                    for n in range(len(M_GROUPS)):
                        split_m(b, n)
                    first_tiles(b, None)

                def batch(b, nxt):
                    for t in range(TILES - 2):
                        step(b, t + 1, b, t + 2)
                        if t == 1:
                            split_x(b, 1, 0)
                        sums(b, t + 2, range(1, NB))
                        add_out(b, t)
                        if t == 0:
                            norm_of(b, 1)
                        if t == 1:
                            split_x(b, 1, 1)
                        if nxt and t in (2, 3):
                            diagonals(b + 1, t - 2)
                        if nxt and t == 4:
                            stats_of(b + 1, 0)
                        if nxt and t == 5:
                            norm_of(b + 1, 0)
                    for k in range(NB):
                        split_p(b, TILES - 1, k)
                        if nxt:
                            split_m(b + 1, k)
                    if nxt:
                        split_x(b + 1, 0, 0)
                        split_m(b + 1, 3)
                        split_m(b + 1, 4)
                        split_x(b + 1, 0, 1)
                        split_m(b + 1, 5)
                        add_out(b, TILES - 2)
                        first_tiles(b + 1, b)
                    else:
                        add_out(b, TILES - 2)
                        add_out(b, TILES - 1)
                each_batch(dve, begin, batch)

            @block.tensor
            def _(pe):
                def free_tr(b, *use):
                    n = transpose_use0(b, *use)
                    if not first(n):
                        pe.wait_ge(tr_lo, n)

                def transpose_x(b, blk, dc):
                    if dc == 0:
                        pe.wait_ge(xn_ready, b * BPB + blk + 1)
                    free_tr(b, "x", blk, dc)
                    for j in range(TJ):
                        last = pe.transpose(tr[:, j * P:(j + 1) * P], xn[:, j, dc * P:(dc + 1) * P], g["ident"][:, :])
                    last.then_inc(tr_mm, 1)

                def transpose_p(b, t, gr):
                    c0, nch = TR_GROUPS[gr]
                    pe.wait_ge(prob_ready, b * TB_BANKS + t * NB + (2, 3, 3)[gr])
                    free_tr(b, "p", t, gr)
                    for c in range(c0, c0 + nch):
                        w = min(P, HK - c * P)
                        last = pe.transpose(tr[0:w, (c - c0) * P:(c - c0 + 1) * P], prob[t % 2][:, c * P:c * P + w], g["ident"][:, :])
                    last.then_inc(tr_mm, 1)

                def scores(b, t, k):
                    blk, j = divmod(t, TJ)
                    if t >= 2:
                        pe.wait_ge(exp_done, b * TB_BANKS + (t - 2) * NB + k + 1)
                    elif k == 0:
                        pe.wait_ge(prep_lo, b * PREP_USES + (len(M_GROUPS), PREP_USES)[t])
                    if j == 0 and k == 0:
                        pe.wait_ge(tr_lo, transpose_use0(b, "x", blk, DC - 1) + 1)
                    for n, (i, w) in enumerate(HI_LO_PASSES):
                        for dc in range(DC):
                            last = pe.matmul(score[t % 2][k][:, 0:BANK_HEADS[k] * KEYS], xnT[blk][i][:, dc, j * P:(j + 1) * P],
                                             m[w][:, dc, cols(k)], start=(n == 0 and dc == 0), stop=(n == 2 and dc == DC - 1))
                    last.then_inc(score_mm, 1)

                def merge_m(b, n):
                    if n == 0:
                        pe.wait_ge(bd_lo, b * 4 + 2)
                    if not first(b):
                        pe.wait_ge(exp_done, (b - 1) * TB_BANKS + (TILES - 2) * NB + n + 1)
                    dc, p0, np = M_GROUPS[n]
                    for p in range(p0, p0 + np):
                        for q, (i, k) in enumerate(HI_LO_PASSES):
                            last = pe.matmul(prep_bank[n][:, (p - p0) * PAIR_COLS:(p - p0 + 1) * PAIR_COLS],
                                             g["wqT"][i][:, p, dc * P:(dc + 1) * P], g["kbd"][k][:, p, :], start=(q == 0), stop=(q == 2))
                    last.then_inc(prep_mm, 1)

                def merge_u(b):
                    pe.wait_ge(bd_lo, b * 4 + 4)
                    for n in range(len(M_GROUPS), PREP_USES):
                        pe.wait_ge(prep_lo, b * PREP_USES + n - 2)
                        for a in range(2):
                            c = 2 * (n - len(M_GROUPS)) + a
                            terms = [(p, i, k) for p in U_TERMS[c] for i, k in HI_LO_PASSES]
                            for q, (p, i, k) in enumerate(terms):
                                last = pe.matmul(prep_bank[n][:, a * D:(a + 1) * D], g["vz"][i][:, P * (c + p):P * (c + p + 1)],
                                                 g["wo"][k][:, p, :], start=(q == 0), stop=(q == len(terms) - 1))
                        last.then_inc(prep_mm, 1)

                def outputs(b, t, chunks=range(KCH)):
                    if chunks[0] == 0:
                        pe.wait_ge(tr_lo, transpose_use0(b, "p", t, len(TR_GROUPS) - 1) + 1)
                        if t >= 1 or not first(b):
                            pe.wait_ge(out_added, b * TILES + t)
                    for c in chunks:
                        rows = min(P, HK - c * P)
                        for q, (i, k) in enumerate(HI_LO_PASSES):
                            last = pe.matmul(acc[:, 0:D], probT[t % 2][i][0:rows, c, :], u[k][0:rows, c, :],
                                             start=(c == 0 and q == 0), stop=(c == KCH - 1 and q == 2))
                    if chunks[-1] == KCH - 1:
                        last.then_inc(out_mm, 1)

                def step(b, t, bs, ts, outputs_part=None):
                    for k in range(NB):
                        transpose_p(b, t, k)
                        scores(bs, ts, k)
                        if outputs_part:
                            outputs_part(k)

                def first_tiles(b, ended):
                    for k in range(NB):
                        scores(b, 0, k)
                    if not first(b):
                        outputs(ended, TILES - 1)
                    merge_u(b)
                    step(b, 0, b, 1)

                def begin(b):
                    for dc in range(DC):
                        transpose_x(b, 0, dc)
                    for n in range(len(M_GROUPS)):
                        merge_m(b, n)
                    first_tiles(b, None)

                def batch(b, nxt):
                    for t in range(TILES - 2):
                        step(b, t + 1, b, t + 2, lambda k: outputs(b, t, range(*OUT_PARTS[k])))
                        if t == 1:
                            for dc in range(DC):
                                transpose_x(b, 1, dc)
                    for k in range(NB):
                        transpose_p(b, TILES - 1, k)
                        if nxt:
                            merge_m(b + 1, k)
                    if nxt:
                        transpose_x(b + 1, 0, 0)
                        merge_m(b + 1, 3)
                        merge_m(b + 1, 4)
                        transpose_x(b + 1, 0, 1)
                        merge_m(b + 1, 5)
                        outputs(b, TILES - 2)
                        first_tiles(b + 1, b)
                    else:
                        outputs(b, TILES - 2)
                        outputs(b, TILES - 1)
                each_batch(pe, begin, batch)


E, H2 = 8, 192
NS = 2
TOP_K = 2
ROUTED = E * H2 // P
SHARED = NS * H2 // P
HCH = SHARED + ROUTED
XPOSE4 = 4


def experts_weights(nc, g, w, ctx):
    sb = lambda name, shape, dt: ctx.enter_context(nc.sbuf_tensor(name, shape, dt))
    g["w1T"] = [sb(f"w1T{i}", [P, DC, 2, HCH, P], F32R) for i in range(2)]
    g["w2T"] = [sb(f"w2T{i}", [P, HCH, D], F32R) for i in range(2)]
    g["gateT"] = [sb(f"gateT{i}", [P, DC, E], F32R) for i in range(2)]
    g["before"] = sb("before", [P, E, E], F32)
    with ExitStack() as tmp:
        t = lambda name, shape, dt: tmp.enter_context(nc.sbuf_tensor(name, shape, dt))
        sem = lambda name: tmp.enter_context(nc.semaphore(name))
        w1s = t("w1s", [P, 2, HCH, D], F32)
        w2s = t("w2s", [P, DC, HCH * P], F32)
        gates = t("gates", [E, D], F32)
        fw, fe, fq = (t(n, [P, DC, D], F32) for n in ("ffn_w", "ffn_we", "ffn_wq"))
        amax, limit, scale_row = ffn_scale_buffers(t, "w")
        bank = [tmp.enter_context(nc.psum_tensor(f"w1_bank{i}", [P, 512], F32)) for i in range(8)]
        gate_in, y_in, g_in, w2_in = sem("gate_in"), sem("y_in"), sem("g_in"), sem("w2_in")
        ones_done = sem("ones_done")
        fw_in, fw_amax, fw_small, fw_limit, fq_step, fqT_mm, fqT_out = (
            sem(n) for n in ("fw_in", "fw_amax", "fw_small", "fw_limit", "fq_step", "fqT_mm", "fqT_out"))
        bank_mm, bank_hi, bank_lo = sem("bank_mm1"), sem("bank_hi1"), sem("bank_lo1")
        w1_uses = [("w1", yg, dc, c) for yg in range(2) for c in range(0, HCH, XPOSE4) for dc in range(DC)]
        uses = [("gate",)] + w1_uses + [("w2", c) for c in range(0, HCH, 2)]

        def moved(use, n, i):
            b = bank[n % 8]
            if use[0] == "gate":
                return b[:, 0:DC * E].rearrange("p (c e) -> p c e", e=E), g["gateT"][i][:, :, :]
            if use[0] == "w1":
                _, yg, dc, c = use
                k = min(XPOSE4, HCH - c)
                return b[:, 0:k * P].rearrange("p (c h) -> p c h", h=P), g["w1T"][i][:, dc, yg, c:c + k, :]
            c = use[1]
            k = min(2, HCH - c)
            return b[:, 0:k * D].rearrange("p (c d) -> p c d", d=D), g["w2T"][i][:, c:c + k, :]

        with nc.Block() as block:
            @block.sync
            def _(sp):
                sp.dma_start(fw[:, :, :], w["L1_ffn_weight"].rearrange("(c p) d -> p c d", p=P)).then_inc(fw_in, 16)
                sp.dma_start(gates[:, :], w["L0_ffn_gate_w"]).then_inc(gate_in, 16)
                w1 = w["L0_ffn_W1"].rearrange("(q e) (s r) d -> s e r q d", e=2, s=2)
                ws1 = w["L0_ffn_Ws1"].rearrange("(s c p) d -> s p c d", s=2, p=P)
                half = P // 2
                for yg, s in ((0, y_in), (1, g_in)):
                    sp.dma_start(w1s[:, yg, SHARED::3, :], w1[yg, 0, 0:P]).then_inc(s, 16)
                    sp.dma_start(w1s[0:half, yg, SHARED + 1::3, :], w1[yg, 0, P:H2]).then_inc(s, 16)
                    sp.dma_start(w1s[half:P, yg, SHARED + 1::3, :], w1[yg, 1, 0:half]).then_inc(s, 16)
                    sp.dma_start(w1s[:, yg, SHARED + 2::3, :], w1[yg, 1, half:H2]).then_inc(s, 16)
                    sp.dma_start(w1s[:, yg, 0:SHARED, :], ws1[yg]).then_inc(s, 16)
                w2s_routed = w2s[:, :, SHARED * P:].rearrange("p c (e h) -> p c e h", h=H2)
                for dc in range(DC):
                    sp.dma_start(w2s_routed[:, dc, :, :], w["L0_ffn_W2"][:, dc * P:(dc + 1) * P, :].rearrange("e p h -> p e h")).then_inc(w2_in, 16)
                sp.dma_start(w2s[:, :, 0:SHARED * P], w["L0_ffn_Ws2"].rearrange("(c p) h -> p c h", p=P)).then_inc(w2_in, 16)

            @block.gpsimd
            def _(gp):
                gp.memset(g["before"][:, :, :], 1.0).then_inc(ones_done, 1)
                gp.wait_ge(ones_done, 1)
                gp.affine_select(out=g["before"][:, :, :], in_=g["before"][:, :, :], compare_op=ALU.is_gt, fill=0.0,
                                 base=0, pattern=[[1, E], [-1, E]], channel_multiplier=0)

            @block.tensor
            def _(pe):
                pe.wait_ge(fw_amax, 1)
                ffn_transpose_amax(pe, g, bank[7], amax, fw_small)
                pe.wait_ge(fw_limit, 6)
                ffn_spread_scales(pe, g, bank[7], scale_row, fw_small)
                pe.wait_ge(fq_step, 5)
                for c in range(DC):
                    for r in range(DC):
                        last = pe.transpose(bank[6][:, c * D + r * P:c * D + (r + 1) * P], fq[:, r, c * P:(c + 1) * P], g["ident"][:, :])
                last.then_inc(fqT_mm, 1)
                for n, use in enumerate(uses):
                    b = bank[n % 8]
                    if n == 6:
                        pe.wait_ge(fqT_out, 1)
                    if n >= 8:
                        pe.wait_ge(bank_lo, n - 7)
                    if use[0] == "gate":
                        pe.wait_ge(gate_in, 16)
                        for dc in range(DC):
                            last = pe.transpose(b[:, dc * E:(dc + 1) * E], gates[:, dc * P:(dc + 1) * P], g["ident"][0:E, 0:E])
                    elif use[0] == "w1":
                        _, yg, dc, c0 = use
                        pe.wait_ge((y_in, g_in)[yg], 5 * 16)
                        for c in range(c0, min(c0 + XPOSE4, HCH)):
                            last = pe.transpose(b[:, (c - c0) * P:(c - c0 + 1) * P], w1s[:, yg, c, dc * P:(dc + 1) * P], g["ident"][:, :])
                    else:
                        pe.wait_ge(w2_in, 3 * 16)
                        for c in range(use[1], min(use[1] + 2, HCH)):
                            for dc in range(DC):
                                at = (c - use[1]) * D + dc * P
                                last = pe.transpose(b[:, at:at + P], w2s[:, dc, c * P:(c + 1) * P], g["ident"][:, :])
                    last.then_inc(bank_mm, 1)

            @block.scalar
            def _(act):
                act.wait_ge(fqT_mm, 1)
                act.activation(g["ffn_wqT"][:, :, :], bank[6][:, :].rearrange("p (c d) -> p c d", d=D), ACT.Copy).then_inc(fqT_out, 1)
                for n, use in enumerate(uses):
                    src, hi = moved(use, n, 0)
                    act.wait_ge(bank_mm, n + 1)
                    act.activation(hi, src, ACT.Copy).then_inc(bank_hi, 1)

            @block.vector
            def _(dve):
                dve.wait_ge(fw_in, 16)
                dve.tensor_reduce(amax[:, :], fw[:, :, :].rearrange("p c d -> p (c d)"), AX_X, ALU.max,
                                  apply_absolute_value=True).then_inc(fw_amax, 1)
                dve.wait_ge(fw_small, 1)
                ffn_scales(dve, limit, scale_row, bank[7][0:1, 0:P], fw_limit)
                dve.wait_ge(fw_small, 2)
                dve.tensor_copy(g["ffn_w_scales"][:, :], bank[7][:, P:P + 2]).then_inc(fw_limit, 1)
                dve.wait_ge(fw_limit, 7)
                dve.tensor_scalar(fq[:, :, :], fw[:, :, :], g["ffn_w_scales"][:, 0:1], FP8_MAX, ALU.mult, ALU.min).then_inc(fq_step, 1)
                dve.wait_ge(fq_step, 1)
                dve.tensor_scalar(fe[:, :, :].bitcast(I32), fq[:, :, :].bitcast(I32), EXPONENT_BITS, None, ALU.bitwise_and).then_inc(fq_step, 1)
                dve.wait_ge(fq_step, 2)
                dve.tensor_scalar(fe[:, :, :], fe[:, :, :], FP8_MIN_NORMAL, ROUND_AT, ALU.max, ALU.mult).then_inc(fq_step, 1)
                dve.wait_ge(fq_step, 3)
                dve.scalar_tensor_tensor(fq[:, :, :], fq[:, :, :], -FP8_MAX, fe[:, :, :], ALU.max, ALU.add).then_inc(fq_step, 1)
                dve.wait_ge(fq_step, 4)
                dve.tensor_tensor(fq[:, :, :], fq[:, :, :], fe[:, :, :], ALU.subtract).then_inc(fq_step, 1)
                for n, use in enumerate(uses):
                    src, hi = moved(use, n, 0)
                    _, lo = moved(use, n, 1)
                    dve.wait_ge(bank_hi, n + 1)
                    dve.tensor_tensor(lo, src, f32(hi), ALU.subtract).then_inc(bank_lo, 1)


def experts(nc, g, scratch):
    with ExitStack() as ctx:
        sb = lambda name, shape, dt: ctx.enter_context(nc.sbuf_tensor(name, shape, dt))
        pb = lambda name: ctx.enter_context(nc.psum_tensor(name, [P, 512], F32))
        xn = sb("xn1", [P, TJ, D], F32)
        xnT = [[sb(f"xnT1_{s}_{i}", [P, DC, TB], F32R) for i in range(2)] for s in range(2)]
        stats, mean_var, rstd = sb("stats1", [P, TJ, 6], F32), sb("mean_var1", [P, TJ, 2], F32), sb("rstd1", [P, TJ], F32)
        logit, expv, route = (sb(n, [P, TJ, E], F32) for n in ("logit", "expv", "route"))
        gmax, gsum, ginv = (sb(n, [P, TJ], F32) for n in ("gmax", "gsum", "ginv"))
        above, tie = sb("above", [P, TJ, E, E], F32), sb("tie", [P, TJ, E, E], F32)
        rank, weight = sb("rank", [P, TJ, E], F32), sb("weight", [P, TJ, E], F32)
        weightT = sb("weightT", [E, TB], F32)
        weight_all = sb("weight_all", [P, ROUTED, TB], F32)
        gated = [sb(f"gated{s}", [P, TB], F32) for s in range(2)]
        hid = [sb(f"hid{s}", [P, TB], F32) for s in range(3)]
        hidT = [[sb(f"hidT{s}_{i}", [P, TB], F32R) for i in range(2)] for s in range(3)]
        py, pg = [pb(f"py{s}") for s in range(2)], [pb(f"pg{s}") for s in range(2)]
        acc = [pb(f"acc1_{s}") for s in range(2)]
        tr, pgate = pb("tr1"), pb("pgate")
        names = ("mv_ready", "eps_done", "rstd_ready", "xn_ready", "tr_mm", "tr_hi", "tr_lo", "gate_mm", "gmax_done", "logit_ready",
                 "expv_ready", "route_step",
                 "weight_ready", "wT_mm", "wT_ready", "wT_out", "w_all_in", "up_mm", "silu_done", "silu_weighted", "hid_done", "hid_hi",
                 "hid_lo", "down_mm", "acc_free")
        s = {n: ctx.enter_context(nc.semaphore(n + "1")) for n in names}

        ROUTE_STEPS = 8
        PE_STEPS = (3, 5, 7, 8, 12)
        ACT_STEPS = (5, 7, 10, 13)
        DVE_STEPS = (1, 3, 5, 7, 9, 11)

        def pe_next(pe, n, par, part):
            if part < DC:
                if part == 0:
                    pe.wait_ge(s["xn_ready"], n + 1)
                    pe.wait_ge(s["wT_ready"], n + 1)
                pe.wait_ge(s["tr_lo"], DC * n + part + 1)
                for j in range(TJ):
                    last = pe.transpose(tr[:, j * P:(j + 1) * P], xn[:, j, part * P:(part + 1) * P], g["ident"][:, :])
                last.then_inc(s["tr_mm"], 1)
            elif part < 4:
                pe.wait_ge(s["tr_lo"], DC * n + DC + 1)
                for j in range(2 * (part - 2), 2 * (part - 1)):
                    for q, (i, k) in enumerate(HI_LO_PASSES):
                        for dc in range(DC):
                            last = pe.matmul(pgate[:, j * E:(j + 1) * E], xnT[par][i][:, dc, j * P:(j + 1) * P], g["gateT"][k][:, dc, :],
                                             start=(q == 0 and dc == 0), stop=(q == 2 and dc == DC - 1))
                last.then_inc(s["gate_mm"], 1)
            else:
                pe.wait_ge(s["weight_ready"], n + 1)
                for j in range(TJ):
                    last = pe.transpose(tr[0:E, j * P:(j + 1) * P], weight[:, j, :], g["ident"][:, :])
                last.then_inc(s["wT_mm"], 1)

        def pe_up(pe, n, par, c):
            if c >= 2 or not (isinstance(n, int) and n == 0):
                pe.wait_ge(s["hid_done"], HCH * n + c - 1)
            bank = (HCH * par + c) % 2
            for yg, out in ((0, py), (1, pg)):
                for q, (i, k) in enumerate(HI_LO_PASSES):
                    for dc in range(DC):
                        last = pe.matmul(out[bank][:, :], g["w1T"][i][:, dc, yg, c, :], xnT[par][k][:, dc, :],
                                         start=(q == 0 and dc == 0), stop=(q == 2 and dc == DC - 1))
            last.then_inc(s["up_mm"], 1)

        def pe_down(pe, n, c):
            pe.wait_ge(s["hid_lo"], HCH * n + c + 1)
            if c == 0:
                pe.wait_ge(s["acc_free"], n + 1)
            for j in range(TJ):
                for q, (i, k) in enumerate(HI_LO_PASSES):
                    last = pe.matmul(acc[j // 2][:, (j % 2) * D:(j % 2 + 1) * D], hidT[c % 3][i][:, j * P:(j + 1) * P], g["w2T"][k][:, c, :],
                                     start=(c == 0 and q == 0 and j % 2 == 0), stop=(c == HCH - 1 and q == 2), skip_group_check=True)
            last.then_inc(s["down_mm"], 1)

        def pe_block(pe, n, par, nxt):
            for c in range(HCH):
                if c + 2 < HCH:
                    pe_up(pe, n, par, c + 2)
                elif nxt:
                    pe_up(pe, n + 1, 1 - par, c + 2 - HCH)
                pe_down(pe, n, c)
                if nxt and c in PE_STEPS:
                    pe_next(pe, n + 1, 1 - par, PE_STEPS.index(c))

        def act_next(act, n, par, part):
            if part < DC:
                act.wait_ge(s["tr_mm"], DC * n + part + 1)
                act.activation(xnT[par][0][:, part, :], tr[:, :], ACT.Copy).then_inc(s["tr_hi"], 1)
            elif part == 2:
                act.wait_ge(s["logit_ready"], n + 1)
                act.activation(expv[:, :, :], logit[:, :, :], ACT.Exp).then_inc(s["expv_ready"], 1)
            else:
                act.wait_ge(s["wT_mm"], n + 1)
                act.activation(weightT[:, :], tr[0:E, :], ACT.Copy).then_inc(s["wT_ready"], 1)

        def act_silu(act, n, par, c):
            bank = (HCH * par + c) % 2
            act.wait_ge(s["up_mm"], HCH * n + c + 1)
            act.activation(gated[bank][:, :], pg[bank][:, :], ACT.Silu).then_inc(s["silu_done"], 1)

        def act_block(act, n, par, nxt):
            for c in range(HCH):
                if c + 1 < HCH:
                    act_silu(act, n, par, c + 1)
                elif nxt:
                    act_silu(act, n + 1, 1 - par, 0)
                act.wait_ge(s["hid_done"], HCH * n + c + 1)
                act.activation(hidT[c % 3][0][:, :], hid[c % 3][:, :], ACT.Copy).then_inc(s["hid_hi"], 1)
                if nxt and c in ACT_STEPS:
                    act_next(act, n + 1, 1 - par, ACT_STEPS.index(c))

        def gp_next(gp, n):
            gp.wait_ge(s["mv_ready"], n + 1)
            inverse_std(gp, g, rstd, mean_var[:, :, 1], s["eps_done"], n + 1, s["rstd_ready"])

        def gp_block(gp, n, par, nxt):
            if nxt:
                gp_next(gp, n + 1)
            gp.wait_ge(s["w_all_in"], 4 * 16 * (n + 1))
            for c in range(SHARED, HCH):
                gp.wait_ge(s["silu_done"], HCH * n + c + 1)
                bank = (HCH * par + c) % 2
                gp.tensor_tensor(gated[bank][:, :], gated[bank][:, :], weight_all[:, c - SHARED, :], ALU.mult).then_inc(s["silu_weighted"], 1)

        def x_tile(n):
            return lambda j: g["x"][:, ds(n, 1), j, :].rearrange("p a d -> p (a d)")

        def dve_next(dve, n, par, part):
            if part == 0:
                layer_norm_stats(dve, x_tile(n), stats, mean_var, s["mv_ready"])
            elif part == 1:
                dve.wait_ge(s["rstd_ready"], n + 1)
                for j in range(TJ):
                    last = dve.tensor_scalar(xn[:, j, :], x_tile(n)(j), mean_var[:, j, 0:1], rstd[:, j:j + 1], ALU.subtract, ALU.mult)
                last.then_inc(s["xn_ready"], 1)
            elif part < 2 + DC:
                dc = part - 2
                dve.wait_ge(s["tr_hi"], DC * n + dc + 1)
                dve.tensor_tensor(xnT[par][1][:, dc, :], tr[:, :], f32(xnT[par][0][:, dc, :]), ALU.subtract).then_inc(s["tr_lo"], 1)
            elif part == 2 + DC:
                dve.wait_ge(s["gate_mm"], 2 * (n + 1))
                logits = pgate[:, 0:TJ * E].rearrange("p (j e) -> p j e", e=E)
                dve.tensor_reduce(gmax[:, :], logits, AX_X, ALU.max).then_inc(s["gmax_done"], 1)
                dve.wait_ge(s["gmax_done"], n + 1)
                dve.tensor_tensor(logit[:, :, :], logits, gmax[:, :].unsqueeze(2).to_broadcast([P, TJ, E]),
                                  ALU.subtract).then_inc(s["logit_ready"], 1)
            else:
                dve.wait_ge(s["expv_ready"], n + 1)
                dve.tensor_reduce(gsum[:, :], expv[:, :, :], AX_X, ALU.add).then_inc(s["route_step"], 1)
                dve.wait_ge(s["route_step"], ROUTE_STEPS * n + 1)
                dve.reciprocal(ginv[:, :], gsum[:, :]).then_inc(s["route_step"], 1)
                dve.wait_ge(s["route_step"], ROUTE_STEPS * n + 2)
                dve.tensor_tensor(route[:, :, :], expv[:, :, :], ginv[:, :].unsqueeze(2).to_broadcast([P, TJ, E]),
                                  ALU.mult).then_inc(s["route_step"], 1)
                dve.wait_ge(s["route_step"], ROUTE_STEPS * n + 3)
                other = route[:, :, :].unsqueeze(2).to_broadcast([P, TJ, E, E])
                own = route[:, :, :].unsqueeze(3).to_broadcast([P, TJ, E, E])
                dve.tensor_tensor(above[:, :, :, :], other, own, ALU.is_gt).then_inc(s["route_step"], 1)
                dve.tensor_tensor(tie[:, :, :, :], other, own, ALU.is_equal).then_inc(s["route_step"], 1)
                dve.wait_ge(s["route_step"], ROUTE_STEPS * n + 5)
                dve.tensor_tensor(tie[:, :, :, :], tie[:, :, :, :], g["before"][:, :, :].unsqueeze(1).to_broadcast([P, TJ, E, E]),
                                  ALU.mult).then_inc(s["route_step"], 1)
                dve.wait_ge(s["route_step"], ROUTE_STEPS * n + 6)
                dve.tensor_tensor(above[:, :, :, :], above[:, :, :, :], tie[:, :, :, :], ALU.add).then_inc(s["route_step"], 1)
                dve.wait_ge(s["route_step"], ROUTE_STEPS * n + 7)
                dve.tensor_reduce(rank[:, :, :], above[:, :, :, :], AX_X, ALU.add).then_inc(s["route_step"], 1)
                dve.wait_ge(s["route_step"], ROUTE_STEPS * n + 8)
                dve.scalar_tensor_tensor(weight[:, :, :], rank[:, :, :], float(TOP_K), route[:, :, :], ALU.is_lt, ALU.mult).then_inc(s["weight_ready"], 1)

        def dve_hidden(dve, n, par, c):
            bank = (HCH * par + c) % 2
            if c >= SHARED:
                dve.wait_ge(s["silu_weighted"], ROUTED * n + c - SHARED + 1)
            else:
                dve.wait_ge(s["silu_done"], HCH * n + c + 1)
            dve.tensor_tensor(hid[c % 3][:, :], py[bank][:, :], gated[bank][:, :], ALU.mult).then_inc(s["hid_done"], 1)

        def dve_block(dve, n, par, nxt):
            for c in range(HCH):
                if c + 1 < HCH:
                    dve_hidden(dve, n, par, c + 1)
                elif nxt:
                    dve_hidden(dve, n + 1, 1 - par, 0)
                dve.wait_ge(s["hid_hi"], HCH * n + c + 1)
                dve.tensor_tensor(hidT[c % 3][1][:, :], hid[c % 3][:, :], f32(hidT[c % 3][0][:, :]), ALU.subtract).then_inc(s["hid_lo"], 1)
                if nxt and c in DVE_STEPS:
                    dve_next(dve, n + 1, 1 - par, DVE_STEPS.index(c))
            dve.wait_ge(s["down_mm"], HCH * (n + 1))
            for a in range(2):
                xa = g["x"][:, ds(n, 1), 2 * a:2 * a + 2, :].rearrange("p a j d -> p (a j d)")
                last = dve.tensor_tensor(xa, acc[a][:, :], xa, ALU.add)
            last.then_inc(s["acc_free"], 1)

        def sp_next(sp, n, first):
            transposed, written, used = (v if isinstance(v, int) else sp.to_reg(v) for v in (n + 2, 16 * (n + 1), ROUTED * n))
            sp.wait_ge(s["wT_ready"], transposed)
            sp.dma_start(scratch, weightT[:, :]).then_inc(s["wT_out"], 16)
            sp.wait_ge(s["wT_out"], written)
            if not first:
                sp.wait_ge(s["silu_weighted"], used)
            row, half = scratch.rearrange("(q e) t -> e q t", e=2), P // 2
            for dst, e in ((weight_all[:, 0:ROUTED:3, :], 0), (weight_all[0:half, 1:ROUTED:3, :], 0),
                           (weight_all[half:P, 1:ROUTED:3, :], 1), (weight_all[:, 2:ROUTED:3, :], 1)):
                sp.dma_start(dst, row[e].partition_broadcast(dst.shape[0])).then_inc(s["w_all_in"], 16)

        LOOPS = NBLK // 2 - 1

        with nc.Block() as block:
            @block.sync
            def _(sp):
                sp_next(sp, 0, True)
                with sp.Fori(0, LOOPS) as it:
                    for a in range(2):
                        sp_next(sp, 2 * it + a + 1, False)
                sp_next(sp, NBLK - 1, False)

            @block.gpsimd
            def _(gp):
                gp_next(gp, 0)
                with gp.Fori(0, LOOPS) as it:
                    for a in range(2):
                        gp_block(gp, 2 * it + a, a, True)
                gp_block(gp, NBLK - 2, 0, True)
                gp_block(gp, NBLK - 1, 1, False)

            @block.scalar
            def _(act):
                for part in range(len(ACT_STEPS)):
                    act_next(act, 0, 0, part)
                act_silu(act, 0, 0, 0)
                with act.Fori(0, LOOPS) as it:
                    for a in range(2):
                        act_block(act, 2 * it + a, a, True)
                act_block(act, NBLK - 2, 0, True)
                act_block(act, NBLK - 1, 1, False)

            @block.vector
            def _(dve):
                dve.sem_inc(s["acc_free"], 1)
                dve.sem_inc(s["tr_lo"], 1)
                dve.sem_inc(s["wT_ready"], 1)
                for part in range(len(DVE_STEPS)):
                    dve_next(dve, 0, 0, part)
                dve_hidden(dve, 0, 0, 0)
                with dve.Fori(0, LOOPS) as it:
                    for a in range(2):
                        dve_block(dve, 2 * it + a, a, True)
                dve_block(dve, NBLK - 2, 0, True)
                dve_block(dve, NBLK - 1, 1, False)

            @block.tensor
            def _(pe):
                for part in range(len(PE_STEPS)):
                    pe_next(pe, 0, 0, part)
                for c in range(2):
                    pe_up(pe, 0, 0, c)
                with pe.Fori(0, LOOPS) as it:
                    for a in range(2):
                        pe_block(pe, 2 * it + a, a, True)
                pe_block(pe, NBLK - 2, 0, True)
                pe_block(pe, NBLK - 1, 1, False)


H3 = HEADS
DH3 = D // H3
HH = H3 // DC
HALF = HH * KEYS
C3 = -(-HALF // P)
SLOT = DH3 + 2
C3_HEADS = [(P * c // KEYS, min(HH, -(-P * (c + 1) // KEYS))) for c in range(C3)]
CMAX = max(b - a for a, b in C3_HEADS)
NORM_EPS = 1e-12
NC3 = DC * C3
PROB_BUFFERS = 4


def attention1_weights(nc, g, w, ctx):
    sb = lambda name, shape, dt: ctx.enter_context(nc.sbuf_tensor(name, shape, dt))
    g["wq1"] = [sb(f"wq1_{i}", [P, DC, D], F32R) for i in range(2)]
    g["wo1"] = [sb(f"wo1_{i}", [P, DC, D], F32R) for i in range(2)]
    g["k1T"] = [sb(f"k1T_{i}", [P, DC, CK], F32R) for i in range(2)]
    g["vbd"] = [sb(f"vbd{i}", [P, B, DC, C3, CMAX, SLOT], F32R) for i in range(2)]
    g["head_rows"] = sb("head_rows", [P, HH, KEYS], F32)
    g["bq1"], g["bo1"], g["gamma"], g["beta"] = (sb(n, [P, D], F32) for n in ("bq1", "bo1", "gamma", "beta"))
    with ExitStack() as tmp:
        t = lambda name, shape, dt: tmp.enter_context(nc.sbuf_tensor(name, shape, dt))
        sem = lambda name: tmp.enter_context(nc.semaphore(name + "3w"))
        ctxs = t("ctxs1", [KEYS, B, CTX], F32)
        ctxT = [t(f"ctxT1_{i}", [CP, CC, CK], F32R) for i in range(2)]
        wqs, wos = t("wq1s", [P, DC, D], F32), t("wo1s", [P, DC, D], F32)
        wks, wvs = t("wk1s", [CP, CC, D], F32), t("wv1s", [CP, CC, D], F32)
        wk, wv = ([t(f"{n}_{i}", [CP, CC, D], F32R) for i in range(2)] for n in ("wk1", "wv1"))
        bk, bv = t("bk1", [P, D], F32), t("bv1", [P, D], F32)
        k, ksq, v = (t(n, [KEYS, B, D], F32) for n in ("k1", "k1sq", "v1"))
        vh = [t(f"v1_{i}", [KEYS, B, D], F32R) for i in range(2)]
        knorm, kinv = t("knorm", [KEYS, B], F32), t("kinv", [KEYS, B], F32)
        spread_f = t("spread_f", [KEYS, C3 * P], F32)
        spread = t("spread", [KEYS, C3 * P], F32R)
        row_head = t("row_head", [P, C3, HH], F32)
        bank = [tmp.enter_context(nc.psum_tensor(f"w3_bank{i}", [P, 512], F32)) for i in range(8)]
        ctx_in, wk_in, wv_in, wq_in, wo_in, bias_in, row_in = (
            sem(n) for n in ("ctx_in", "wk_in", "wv_in", "wq_in", "wo_in", "bias_in", "row_in"))
        fill, shaped, w_hi, w_lo, mm, hi, lo, k_out, sq_out, norm_out, norm_pow, norm_max, inv_out, kn_out, v_out, vh_hi, vh_lo, v_zero, spread_out, vbd_out = (
            sem(n) for n in ("fill", "shaped", "w_hi", "w_lo", "mm", "hi", "lo", "k_out", "sq_out", "norm_out", "norm_pow", "norm_max",
                             "inv_out", "kn_out", "v_out", "vh_hi", "vh_lo", "v_zero", "spread_out", "vbd_out"))
        SPREAD = [(b, c) for b in range(B) for c in range(C3)]

        def ones_where(gp, tile, pattern_base_cm, n):
            for m, (base, cm, pattern) in enumerate(pattern_base_cm):
                gp.wait_ge(fill if m == 0 else shaped, 4 if m == 0 else n + m)
                gp.affine_select(out=tile, in_=tile, compare_op=ALU.is_ge, fill=0.0, base=base, pattern=pattern,
                                 channel_multiplier=cm).then_inc(shaped, 1)
            return n + len(pattern_base_cm)

        with nc.Block() as block:
            @block.sync
            def _(sp):
                sp.dma_start(ctxs[:, :, :], w["ctx_768"].rearrange("b k c -> k b c")).then_inc(ctx_in, 16)
                for dst, src, p, s in ((wks, w["L1_xattn_Wk"], CP, wk_in), (wvs, w["L1_xattn_Wv"], CP, wv_in),
                                       (wqs, w["L1_xattn_Wq"], P, wq_in), (wos, w["L1_xattn_Wo"], P, wo_in)):
                    sp.dma_start(dst[:, :, :], src.rearrange("(c p) n -> p c n", p=p)).then_inc(s, 16)
                for dst, src in ((bk, w["L1_xattn_bk"]), (bv, w["L1_xattn_bv"])):
                    sp.dma_start(dst[:, :], src.partition_broadcast(P)).then_inc(bias_in, 16)
                rows = ((g["bq1"], w["L1_xattn_bq"]), (g["bo1"], w["L1_xattn_bo"]), (g["gamma"], w["L1_xattn_ln_gamma"]), (g["beta"], w["L1_xattn_ln_beta"]))
                for dst, src in rows:
                    sp.dma_start(dst[:, :], src.partition_broadcast(P)).then_inc(row_in, 16)
                sp.wait_ge(row_in, 16 * len(rows))

            @block.gpsimd
            def _(gp):
                gp.memset(g["head_rows"][:, :, :], 1.0).then_inc(fill, 1)
                gp.memset(row_head[:, :, :], 1.0).then_inc(fill, 1)
                gp.memset(spread_f[:, HALF:], 0.0).then_inc(fill, 1)
                gp.memset(spread_f[:, 0:HALF], 1.0).then_inc(fill, 1)
                n = ones_where(gp, g["head_rows"][:, :, :], ((0, 1, [[-DH3, HH], [0, KEYS]]), (DH3 - 1, -1, [[DH3, HH], [0, KEYS]])), 0)
                n = ones_where(gp, row_head[:, :, :], ((0, 1, [[P, C3], [-KEYS, HH]]), (KEYS - 1, -1, [[-P, C3], [KEYS, HH]])), n)
                n = ones_where(gp, spread_f[:, 0:HALF], ((0, 1, [[0, HH], [-1, KEYS]]), (0, -1, [[0, HH], [1, KEYS]])), n)
                for i in range(2):
                    gp.memset(f32(g["vbd"][i][:, :, :, :, :, :]), 0.0).then_inc(v_zero, 1)
                gp.wait_ge(norm_out, 1)
                gp.tensor_tensor(knorm[:, :], knorm[:, :], g["half"][0:KEYS, 0:B], ALU.pow).then_inc(norm_pow, 1)

            @block.scalar
            def _(act):
                for n, (dst, src, s) in enumerate(((wk, wks, wk_in), (wv, wvs, wv_in), (g["wq1"], wqs, wq_in), (g["wo1"], wos, wo_in))):
                    act.wait_ge(s, 16)
                    act.activation(dst[0][:, :, :], src[:, :, :], ACT.Copy).then_inc(w_hi, 1)
                for c in range(CC):
                    act.wait_ge(mm, c + 1)
                    act.activation(ctxT[0][:, c, :], bank[c][0:CP, 0:CK], ACT.Copy).then_inc(hi, 1)
                act.wait_ge(shaped, 6)
                act.activation(spread[:, :], spread_f[:, :], ACT.Copy).then_inc(spread_out, 1)
                act.wait_ge(v_out, 2)
                act.activation(vh[0][:, :, :], v[:, :, :], ACT.Copy).then_inc(vh_hi, 1)
                for f in range(DC):
                    act.wait_ge(mm, 7 + f)
                    act.activation(g["k1T"][0][:, f, :], bank[6 + f][:, 0:CK], ACT.Copy).then_inc(hi, 1)

            @block.vector
            def _(dve):
                for n, (dst, src) in enumerate(((wk, wks), (wv, wvs), (g["wq1"], wqs), (g["wo1"], wos))):
                    dve.wait_ge(w_hi, n + 1)
                    dve.tensor_tensor(dst[1][:, :, :], src[:, :, :], f32(dst[0][:, :, :]), ALU.subtract).then_inc(w_lo, 1)
                for c in range(CC):
                    dve.wait_ge(hi, c + 1)
                    dve.tensor_tensor(ctxT[1][:, c, :], bank[c][0:CP, 0:CK], f32(ctxT[0][:, c, :]), ALU.subtract).then_inc(lo, 1)
                dve.wait_ge(bias_in, 32)
                two = lambda ap: ap[0:KEYS, :].unsqueeze(1).to_broadcast([KEYS, 2, D])
                for n, (dst, bias, s) in enumerate(((k, bk, k_out), (k, bk, k_out), (v, bv, v_out), (v, bv, v_out))):
                    dve.wait_ge(mm, 2 + n + 1)
                    a = n % 2
                    dve.tensor_tensor(dst[:, 2 * a:2 * a + 2, :], bank[2 + n][0:KEYS, :].rearrange("p (b d) -> p b d", d=D), two(bias),
                                      ALU.add).then_inc(s, 1)
                dve.wait_ge(k_out, 2)
                dve.tensor_tensor(ksq[:, :, :], k[:, :, :], k[:, :, :], ALU.mult).then_inc(sq_out, 1)
                dve.wait_ge(sq_out, 1)
                dve.tensor_reduce(knorm[:, :], ksq[:, :, :], AX_X, ALU.add).then_inc(norm_out, 1)
                dve.wait_ge(norm_pow, 1)
                dve.tensor_scalar(knorm[:, :], knorm[:, :], NORM_EPS, None, ALU.max).then_inc(norm_max, 1)
                dve.wait_ge(norm_max, 1)
                dve.reciprocal(kinv[:, :], knorm[:, :]).then_inc(inv_out, 1)
                dve.wait_ge(inv_out, 1)
                dve.tensor_tensor(k[:, :, :], k[:, :, :], kinv[:, :].unsqueeze(2).to_broadcast([KEYS, B, D]), ALU.mult).then_inc(kn_out, 1)
                dve.wait_ge(vh_hi, 1)
                dve.tensor_tensor(vh[1][:, :, :], v[:, :, :], f32(vh[0][:, :, :]), ALU.subtract).then_inc(vh_lo, 1)
                for f in range(DC):
                    dve.wait_ge(hi, CC + f + 1)
                    dve.tensor_tensor(g["k1T"][1][:, f, :], bank[6 + f][:, 0:CK], f32(g["k1T"][0][:, f, :]), ALU.subtract).then_inc(lo, 1)
                dve.wait_ge(shaped, 6)
                dve.wait_ge(v_zero, 2)
                for c, (h0, h1) in enumerate(C3_HEADS):
                    dve.tensor_copy(g["vbd"][0][:, :, :, c, 0:h1 - h0, DH3],
                                    row_head[:, c, h0:h1].unsqueeze(1).unsqueeze(1).to_broadcast([P, B, DC, h1 - h0]))
                for n, (b, c) in enumerate(SPREAD):
                    h0, h1 = C3_HEADS[c]
                    dve.wait_ge(mm, 8 + n + 1)
                    for i in range(2):
                        src = bank[n % 8][:, i * D:(i + 1) * D].rearrange("p (f h d) -> p f h d", f=DC, d=DH3)[:, :, h0:h1, :]
                        keep = row_head[:, c, h0:h1].unsqueeze(1).unsqueeze(3).to_broadcast([P, DC, h1 - h0, DH3])
                        last = dve.tensor_tensor(g["vbd"][i][:, b, :, c, 0:h1 - h0, 0:DH3], src, keep, ALU.mult)
                    last.then_inc(vbd_out, 1)

            @block.tensor
            def _(pe):
                pe.wait_ge(ctx_in, 16)
                for c in range(CC):
                    for b in range(B):
                        last = pe.transpose(bank[c][0:CP, b * KEYS:(b + 1) * KEYS], ctxs[:, b, c * CP:(c + 1) * CP], g["ident"][0:KEYS, 0:KEYS])
                    last.then_inc(mm, 1)
                pe.wait_ge(lo, CC)
                for n, weight in enumerate((wk, wk, wv, wv)):
                    pe.wait_ge(w_lo, 1 + n // 2)
                    for a in range(2):
                        b = 2 * (n % 2) + a
                        for q, (i, j) in enumerate(HI_LO_PASSES):
                            for c in range(CC):
                                last = pe.matmul(bank[2 + n][0:KEYS, a * D:(a + 1) * D], ctxT[i][:, c, b * KEYS:(b + 1) * KEYS], weight[j][:, c, :],
                                                 start=(q == 0 and c == 0), stop=(q == 2 and c == CC - 1))
                    last.then_inc(mm, 1)
                pe.wait_ge(kn_out, 1)
                for f in range(DC):
                    for b in range(B):
                        last = pe.transpose(bank[6 + f][:, b * KEYS:(b + 1) * KEYS], k[:, b, f * P:(f + 1) * P], g["ident"][0:KEYS, 0:KEYS])
                    last.then_inc(mm, 1)
                pe.wait_ge(spread_out, 1)
                pe.wait_ge(vh_lo, 1)
                pe.wait_ge(lo, CC + DC)
                for n, (b, c) in enumerate(SPREAD):
                    if n >= 8:
                        pe.wait_ge(vbd_out, n - 7)
                    for i in range(2):
                        last = pe.matmul(bank[n % 8][:, i * D:(i + 1) * D], spread[:, c * P:(c + 1) * P], vh[i][:, b, :], start=True, stop=True)
                    last.then_inc(mm, 1)


def attention1(nc, g):
    with ExitStack() as ctx:
        sb = lambda name, shape, dt: ctx.enter_context(nc.sbuf_tensor(name, shape, dt))
        pb = lambda name: ctx.enter_context(nc.psum_tensor(name, [P, 512], F32))
        kbd = [sb(f"kbd1_{i}", [P, DC, HH, KEYS], F32R) for i in range(2)]
        xn = sb("xn3", [P, TJ, D], F32)
        xnT = [sb(f"xnT3_{i}", [P, DC, TB], F32R) for i in range(2)]
        stats, mean_var, rstd = sb("stats3", [P, TJ, 6], F32), sb("mean_var3", [P, TJ, 2], F32), sb("rstd3", [P, TJ], F32)
        y_stats, y_mean_var, y_rstd = sb("stats_y", [P, TJ, 6], F32), sb("mean_var_y", [P, TJ, 2], F32), sb("rstd_y", [P, TJ], F32)
        f_stats, f_mean_var = sb("stats_f", [P, TJ, 6], F32), sb("mean_var_f", [P, TJ, 2], F32)
        f_rstd, f_shift = sb("rstd_f", [P, TJ], F32), sb("shift_f", [P, TJ], F32)
        qp, qres = [sb(f"qp{s}", [P, TJ, D], F32) for s in range(2)], [sb(f"qres{s}", [P, TJ, D], F32) for s in range(2)]
        qn, sq = sb("qn", [P, TJ, D], F32), sb("sq", [P, TJ, D], F32)
        ssq, qinv = sb("ssq", [P, TJ], F32), sb("qinv", [P, TJ], F32)
        qT = [[sb(f"qT{s}_{i}", [P, DC, TB], F32R) for i in range(2)] for s in range(2)]
        prob = [sb(f"prob3_{s}", [P, TB], F32) for s in range(PROB_BUFFERS)]
        probT = [[sb(f"probT3_{s}_{i}", [P, TB], F32R) for i in range(2)] for s in range(PROB_BUFFERS)]
        sums, o = sb("sums3", [P, TJ, H3], F32), sb("o3", [P, TJ, D], F32)
        oT = [sb(f"oT{i}", [P, DC, TB], F32R) for i in range(2)]
        y = sb("y3", [P, TJ, D], F32)
        score = [pb(f"score3_{s}") for s in range(2)]
        acc = [pb(f"acc3_{j}") for j in range(TJ)]
        tr, proj = pb("tr3"), pb("proj3")
        names = ("mv_ready", "eps_done", "rstd_ready", "xn_ready", "tr_mm", "tr_hi", "tr_lo", "proj_mm", "proj_out", "ssq_done", "root_done",
                 "qinv_done", "qn_ready", "qres_ready", "kbd_ready", "score_mm", "exp_done", "prob_hi", "prob_lo", "pv_mm",
                 "sums_done", "o_ready", "y_mv", "y_eps", "y_rstd", "y_gamma", "beta_added",
                 "f_mv", "f_eps", "f_rstd", "f_shift", "f_seen", "f_ready", "x_done")
        s = {n: ctx.enter_context(nc.semaphore(n + "3")) for n in names}
        two_tiles = lambda ap: ap[:, :].unsqueeze(1).to_broadcast([P, 2, D])
        four_tiles = lambda ap: ap[:, :].unsqueeze(1).to_broadcast([P, TJ, D])
        pair = lambda tile, a: tile[:, 2 * a:2 * a + 2, :]
        banked = lambda bank: bank[:, :].rearrange("p (j d) -> p j d", d=D)

        def is_block(n, *blocks):
            return isinstance(n, int) and n in blocks

        def tr_use(n, kind, dc):
            if kind == 0:
                return (0 if is_block(n, 0) else 6 * n - 2) + dc
            if kind == 1:
                return (2 if is_block(n, 0) else 6 * n) + dc
            return 6 * n + (4 if is_block(n, NBLK - 1) else 8) + dc

        def proj_use(n, kind, a):
            if kind == 0:
                return (0 if is_block(n, 0) else 4 * n - 2) + a
            return 4 * n + (2 if is_block(n, NBLK - 1) else 4) + a

        def chunk(c):
            f, cc = divmod(c, C3)
            return f, cc, min(P, HALF - cc * P)

        def slot(par, c):
            return (NC3 * par + c) % PROB_BUFFERS

        def x_tile(n):
            return lambda j: g["x"][:, ds(n, 1), j, :].rearrange("p a d -> p (a d)")

        def x_block(n):
            return g["x"][:, ds(n, 1), :, :].rearrange("p a j d -> p (a j) d")

        def pe_transpose(pe, n, kind, dc, src):
            use = tr_use(n, kind, dc)
            if not is_block(use, 0):
                pe.wait_ge(s["tr_lo"], use)
            for j in range(TJ):
                last = pe.transpose(tr[:, j * P:(j + 1) * P], src[:, j, dc * P:(dc + 1) * P], g["ident"][:, :])
            last.then_inc(s["tr_mm"], 1)

        def pe_project(pe, n, kind, a, xT, weight):
            use = proj_use(n, kind, a)
            if not is_block(use, 0):
                pe.wait_ge(s["proj_out"], use)
            if a == 0:
                pe.wait_ge(s["tr_lo"], tr_use(n, 2 * kind, DC - 1) + 1)
            for b in range(2):
                j = 2 * a + b
                for q, (i, k) in enumerate(HI_LO_PASSES):
                    for dc in range(DC):
                        last = pe.matmul(proj[:, b * D:(b + 1) * D], xT[i][:, dc, j * P:(j + 1) * P], weight[k][:, dc, :],
                                         start=(q == 0 and dc == 0), stop=(q == 2 and dc == DC - 1))
            last.then_inc(s["proj_mm"], 1)

        def pe_front(pe, n, part):
            if part < 2:
                if part == 0:
                    pe.wait_ge(s["xn_ready"], n + 1)
                pe_transpose(pe, n, 0, part, xn)
            elif part < 4:
                pe_project(pe, n, 0, part - 2, xnT, g["wq1"])
            else:
                if part == 4:
                    pe.wait_ge(s["qn_ready"], n + 1)
                pe_transpose(pe, n, 1, part - 4, qn)

        def pe_back(pe, n, part):
            if part < 2:
                if part == 0:
                    pe.wait_ge(s["o_ready"], n + 2)
                pe_transpose(pe, n, 2, part, o)
            else:
                pe_project(pe, n, 1, part - 2, oT, g["wo1"])

        def pe_scores(pe, n, par, batch, c):
            f, cc, rows = chunk(c)
            if cc == 0:
                pe.wait_ge(s["kbd_ready"], DC * batch + f + 1)
                pe.wait_ge(s["tr_lo"], tr_use(n, 1, f) + 1)
            if c >= 2 or not is_block(n, 0):
                pe.wait_ge(s["exp_done"], NC3 * n + c - 1)
            for q, (i, k) in enumerate(HI_LO_PASSES):
                keys = kbd[i][:, f, :, :].rearrange("p h k -> p (h k)")[:, cc * P:cc * P + rows]
                last = pe.matmul(score[c % 2][0:rows, :], keys, qT[par][k][:, f, :], start=(q == 0), stop=(q == 2))
            last.then_inc(s["score_mm"], 1)

        def pe_values(pe, n, par, batch, c):
            f, cc, rows = chunk(c)
            h0, h1 = C3_HEADS[cc]
            pe.wait_ge(s["prob_lo"], NC3 * n + c + 1)
            if c == 0:
                pe.wait_ge(s["o_ready"], n + 1)
            for j in range(TJ):
                out = acc[j][:, (f * HH + h0) * SLOT:(f * HH + h1) * SLOT]
                for q, (i, k) in enumerate(HI_LO_PASSES):
                    v = g["vbd"][k][0:rows, ds(batch, 1), f, cc, 0:h1 - h0, :].rearrange("p a h d -> p (a h d)")
                    last = pe.matmul(out, probT[slot(par, c)][i][0:rows, j * P:(j + 1) * P], v, start=(c == 0 and q == 0),
                                     stop=(c == NC3 - 1 and q == 2), skip_group_check=True)
            last.then_inc(s["pv_mm"], 1)

        PE_FRONT = {2: 0, 3: 1, 4: 2, 5: 3, 8: 4, 9: 5}
        PE_BACK = {0: 0, 1: 1, 2: 2, 3: 3}

        def pe_block(pe, n, par, batch, next_batch, prv, nxt, prv2):
            for c in range(NC3):
                if c + 2 < NC3:
                    pe_scores(pe, n, par, batch, c + 2)
                pe_values(pe, n, par, batch, c)
                if nxt and c + 1 == NC3:
                    for first in range(2):
                        pe_scores(pe, n + 1, 1 - par, next_batch, first)
                if prv and c in PE_BACK:
                    pe_back(pe, n - 1, PE_BACK[c])
                if nxt and c in PE_FRONT:
                    pe_front(pe, n + 1, PE_FRONT[c])

        def act_split(act, n, kind, dc, dst):
            act.wait_ge(s["tr_mm"], tr_use(n, kind, dc) + 1)
            act.activation(dst[0][:, dc, :], tr[:, :], ACT.Copy).then_inc(s["tr_hi"], 1)

        def act_squares(act, n, par, a):
            act.wait_ge(s["proj_out"], proj_use(n, 0, a) + 1)
            for j in (2 * a, 2 * a + 1):
                last = act.activation(sq[:, j, :], qp[par][:, j, :], ACT.Square, accum_out=ssq[:, j:j + 1])
            last.then_inc(s["ssq_done"], 1)

        def act_exp(act, n, par, c):
            rows = chunk(c)[2]
            act.wait_ge(s["score_mm"], NC3 * n + c + 1)
            if c >= PROB_BUFFERS or not is_block(n, 0):
                act.wait_ge(s["prob_lo"], NC3 * n + c - PROB_BUFFERS + 1)
            act.activation(prob[slot(par, c)][0:rows, :], score[c % 2][0:rows, :], ACT.Exp, scale=DH3 ** -0.5).then_inc(s["exp_done"], 1)

        def act_hi(act, n, par, c):
            rows = chunk(c)[2]
            act.wait_ge(s["exp_done"], NC3 * n + c + 1)
            if c >= PROB_BUFFERS or not is_block(n, 0):
                act.wait_ge(s["pv_mm"], NC3 * n + c - PROB_BUFFERS + 1)
            act.activation(probT[slot(par, c)][0][0:rows, :], prob[slot(par, c)][0:rows, :], ACT.Copy).then_inc(s["prob_hi"], 1)

        def act_block(act, n, par, batch, next_batch, prv, nxt, prv2):
            for c in range(NC3):
                if c + 1 < NC3:
                    act_exp(act, n, par, c + 1)
                act_hi(act, n, par, c)
                if prv and c in (1, 2):
                    act_split(act, n - 1, 2, c - 1, oT)
                if nxt and c in (3, 4):
                    act_split(act, n + 1, 0, c - 3, xnT)
                if nxt and c in (6, 7):
                    act_squares(act, n + 1, 1 - par, c - 6)
                if nxt and c == 9:
                    act_split(act, n + 1, 1, 0, qT[1 - par])
                if prv and c == 0:
                    act_split(act, n, 1, 1, qT[par])
                if prv2 and c == 4:
                    act_last_norm(act, n - 2)
            if nxt:
                act_exp(act, n + 1, 1 - par, 0)

        def act_last_norm(act, n):
            act.wait_ge(s["f_shift"], n + 1)
            act.sem_inc(s["f_seen"], 1)
            for j in range(TJ):
                last = act.activation(g["xf"][:, ds(n, 1), j, :].rearrange("p a d -> p (a d)"), x_tile(n)(j), ACT.Identity,
                                      scale=f_rstd[:, j:j + 1], bias=f_shift[:, j:j + 1])
            last.then_inc(s["f_ready"], 1)

        def dve_split(dve, n, kind, dc, dst):
            dve.wait_ge(s["tr_hi"], tr_use(n, kind, dc) + 1)
            dve.tensor_tensor(dst[1][:, dc, :], tr[:, :], f32(dst[0][:, dc, :]), ALU.subtract).then_inc(s["tr_lo"], 1)

        def dve_stats(dve, n):
            layer_norm_stats(dve, x_tile(n), stats, mean_var, s["mv_ready"])

        def dve_normalize(dve, n):
            dve.wait_ge(s["rstd_ready"], n + 1)
            for j in range(TJ):
                last = dve.tensor_scalar(xn[:, j, :], x_tile(n)(j), mean_var[:, j, 0:1], rstd[:, j:j + 1], ALU.subtract, ALU.mult)
            last.then_inc(s["xn_ready"], 1)

        def dve_queries(dve, n, par, a):
            dve.wait_ge(s["proj_mm"], proj_use(n, 0, a) + 1)
            dve.tensor_tensor(pair(qp[par], a), banked(proj), two_tiles(g["bq1"]), ALU.add).then_inc(s["proj_out"], 1)

        def dve_unit_queries(dve, n, par):
            dve.wait_ge(s["root_done"], n + 1)
            dve.tensor_scalar(qinv[:, :], qinv[:, :], 1.0 / NORM_EPS, None, ALU.min).then_inc(s["qinv_done"], 1)
            dve.wait_ge(s["qinv_done"], n + 1)
            for j in range(TJ):
                last = dve.tensor_scalar(qn[:, j, :], qp[par][:, j, :], qinv[:, j:j + 1], None, ALU.mult)
            last.then_inc(s["qn_ready"], 1)

        def dve_outputs(dve, n):
            dve.wait_ge(s["pv_mm"], NC3 * (n + 1))
            slots = [acc[j][:, 0:H3 * SLOT].rearrange("p (h d) -> p h d", d=SLOT) for j in range(TJ)]
            for j in range(TJ):
                last = dve.reciprocal(sums[:, j, :], slots[j][:, :, DH3])
            last.then_inc(s["sums_done"], 1)
            dve.wait_ge(s["sums_done"], n + 1)
            for j in range(TJ):
                last = dve.tensor_tensor(o[:, j, :].rearrange("p (h d) -> p h d", d=DH3), slots[j][:, :, 0:DH3],
                                         sums[:, j, :].unsqueeze(2).to_broadcast([P, H3, DH3]), ALU.mult)
            last.then_inc(s["o_ready"], 1)

        def dve_residual(dve, n, par, a):
            if a == 0:
                dve.wait_ge(s["qres_ready"], n + 1)
            dve.wait_ge(s["proj_mm"], proj_use(n, 1, a) + 1)
            dve.tensor_tensor(pair(y, a), banked(proj), pair(qres[par], a), ALU.add).then_inc(s["proj_out"], 1)

        def dve_y_stats(dve, n):
            dve.wait_ge(s["proj_out"], proj_use(n, 1, 1) + 1)
            layer_norm_stats(dve, lambda j: y[:, j, :], y_stats, y_mean_var, s["y_mv"])

        def dve_gamma(dve, n):
            dve.wait_ge(s["y_rstd"], n + 1)
            for j in range(TJ):
                last = dve.scalar_tensor_tensor(y[:, j, :], y[:, j, :], y_mean_var[:, j, 0:1], g["gamma"][:, :], ALU.subtract, ALU.mult)
            last.then_inc(s["y_gamma"], 1)

        def dve_update(dve, n):
            dve.wait_ge(s["y_gamma"], n + 1)
            dve.wait_ge(s["beta_added"], n + 1)
            for j in range(TJ):
                last = dve.scalar_tensor_tensor(x_tile(n)(j), y[:, j, :], y_rstd[:, j:j + 1], x_tile(n)(j), ALU.mult, ALU.add)
            if is_block(n, NBLK - 1):
                last.then_inc(s["x_done"], 1)

        def dve_block(dve, n, par, batch, next_batch, prv, nxt, prv2):
            if prv:
                dve_outputs(dve, n - 1)
            for c in range(NC3):
                rows = chunk(c)[2]
                dve.wait_ge(s["prob_hi"], NC3 * n + c + 1)
                dve.tensor_tensor(probT[slot(par, c)][1][0:rows, :], prob[slot(par, c)][0:rows, :], f32(probT[slot(par, c)][0][0:rows, :]),
                                  ALU.subtract).then_inc(s["prob_lo"], 1)
                if prv and c == 0:
                    dve_split(dve, n, 1, 1, qT[par])
                if nxt and c == 0:
                    dve_stats(dve, n + 1)
                if prv and c in (1, 2):
                    dve_split(dve, n - 1, 2, c - 1, oT)
                if nxt and c == 1:
                    dve_normalize(dve, n + 1)
                if prv2 and c == 2:
                    dve_last_stats(dve, n - 2)
                if prv2 and c == 3:
                    dve_last_shift(dve, n - 2)
                if nxt and c in (3, 4):
                    dve_split(dve, n + 1, 0, c - 3, xnT)
                if prv and c in (3, 4):
                    dve_residual(dve, n - 1, 1 - par, c - 3)
                if nxt and c in (5, 6):
                    dve_queries(dve, n + 1, 1 - par, c - 5)
                if prv and c == 5:
                    dve_y_stats(dve, n - 1)
                if prv and c == 6:
                    dve_gamma(dve, n - 1)
                if nxt and c == 8:
                    dve_unit_queries(dve, n + 1, 1 - par)
                if nxt and c == 9:
                    dve_split(dve, n + 1, 1, 0, qT[1 - par])
                if prv and c == 9:
                    dve_update(dve, n - 1)
                if prv2 and c == 9:
                    dve_last_max(dve, n - 2)

        def dve_last_stats(dve, n):
            layer_norm_stats(dve, x_tile(n), f_stats, f_mean_var, s["f_mv"])

        def dve_last_shift(dve, n):
            dve.wait_ge(s["f_rstd"], n + 1)
            dve.scalar_tensor_tensor(f_shift[:, :], f_mean_var[:, :, 0], -1.0, f_rstd[:, :], ALU.mult, ALU.mult).then_inc(s["f_shift"], 1)

        def dve_last_max(dve, n):
            dve.wait_ge(s["f_ready"], n + 1)
            dve.tensor_reduce(g["xf_max"][:, ds(n, 1)], g["xf"][:, ds(n, 1), :, :].rearrange("p a j d -> p a (j d)"), AX_X, ALU.max,
                              apply_absolute_value=True)

        def gp_ln(gp, n):
            gp.wait_ge(s["mv_ready"], n + 1)
            inverse_std(gp, g, rstd, mean_var[:, :, 1], s["eps_done"], n + 1, s["rstd_ready"])

        def gp_root(gp, n):
            gp.wait_ge(s["ssq_done"], 2 * (n + 1))
            gp.tensor_tensor(qinv[:, :], ssq[:, :], g["minus_half"][:, :], ALU.pow).then_inc(s["root_done"], 1)

        def gp_residual(gp, n, par):
            gp.tensor_tensor(qres[par][:, :, :], qp[par][:, :, :], four_tiles(g["bo1"]), ALU.add).then_inc(s["qres_ready"], 1)

        def gp_beta(gp, n):
            gp.wait_ge(s["xn_ready"], n + 1)
            gp.tensor_tensor(x_block(n), x_block(n), four_tiles(g["beta"]), ALU.add).then_inc(s["beta_added"], 1)

        def gp_y(gp, n):
            gp.wait_ge(s["y_mv"], n + 1)
            inverse_std(gp, g, y_rstd, y_mean_var[:, :, 1], s["y_eps"], n + 1, s["y_rstd"])

        def gp_keys(gp, batch, f):
            for i in range(2):
                keys = f32(g["k1T"][i][:, f, ds(batch * KEYS, KEYS)]).unsqueeze(1).to_broadcast([P, HH, KEYS])
                last = gp.tensor_tensor(kbd[i][:, f, :, :], keys, g["head_rows"][:, :, :], ALU.mult)
            last.then_inc(s["kbd_ready"], 1)

        def gp_last_rstd(gp, n):
            gp.wait_ge(s["f_mv"], n + 1)
            inverse_std(gp, g, f_rstd, f_mean_var[:, :, 1], s["f_eps"], n + 1, s["f_rstd"])

        def gp_block(gp, n, par, batch, next_batch, prv, nxt, prv2):
            if nxt:
                gp_ln(gp, n + 1)
            if par == 0:
                if prv:
                    gp.wait_ge(s["score_mm"], NC3 * n)
                gp_keys(gp, batch, 1)
            if prv:
                gp_beta(gp, n - 1)
            if prv2:
                gp_last_rstd(gp, n - 2)
            if prv:
                gp_y(gp, n - 1)
            if nxt and par == 1:
                gp.wait_ge(s["score_mm"], NC3 * n + C3)
                gp_keys(gp, next_batch, 0)
            if nxt:
                gp_root(gp, n + 1)
                gp_residual(gp, n + 1, 1 - par)

        LOOPS = (NBLK - 4) // 2

        def each_block(eng, body):
            body(eng, 0, 0, 0, 0, False, True, False)
            body(eng, 1, 1, 0, 1, True, True, False)
            body(eng, 2, 0, 1, 1, True, True, True)
            with eng.Fori(0, LOOPS) as it:
                body(eng, 2 * it + 3, 1, it + 1, it + 2, True, True, True)
                body(eng, 2 * it + 4, 0, it + 2, it + 2, True, True, True)
            body(eng, NBLK - 1, 1, B - 1, B - 1, True, False, True)

        with nc.Block() as block:
            @block.gpsimd
            def _(gp):
                gp_ln(gp, 0)
                gp_keys(gp, 0, 0)
                gp_root(gp, 0)
                gp_residual(gp, 0, 0)
                each_block(gp, gp_block)
                gp_beta(gp, NBLK - 1)
                gp_last_rstd(gp, NBLK - 2)
                gp_y(gp, NBLK - 1)
                gp.wait_ge(s["f_ready"], NBLK - 1)
                gp_last_rstd(gp, NBLK - 1)

            @block.scalar
            def _(act):
                for dc in range(DC):
                    act_split(act, 0, 0, dc, xnT)
                for a in range(2):
                    act_squares(act, 0, 0, a)
                for dc in range(DC):
                    act_split(act, 0, 1, dc, qT[0])
                act_exp(act, 0, 0, 0)
                each_block(act, act_block)
                for dc in range(DC):
                    act_split(act, NBLK - 1, 2, dc, oT)
                for n in (NBLK - 2, NBLK - 1):
                    act_last_norm(act, n)

            @block.vector
            def _(dve):
                dve.sem_inc(s["o_ready"], 1)
                dve_stats(dve, 0)
                dve_normalize(dve, 0)
                for dc in range(DC):
                    dve_split(dve, 0, 0, dc, xnT)
                for a in range(2):
                    dve_queries(dve, 0, 0, a)
                dve_unit_queries(dve, 0, 0)
                for dc in range(DC):
                    dve_split(dve, 0, 1, dc, qT[0])
                each_block(dve, dve_block)
                dve_outputs(dve, NBLK - 1)
                for dc in range(DC):
                    dve_split(dve, NBLK - 1, 2, dc, oT)
                dve_last_stats(dve, NBLK - 2)
                dve_last_shift(dve, NBLK - 2)
                for a in range(2):
                    dve_residual(dve, NBLK - 1, 1, a)
                dve_y_stats(dve, NBLK - 1)
                dve_gamma(dve, NBLK - 1)
                dve_update(dve, NBLK - 1)
                dve.wait_ge(s["x_done"], 1)
                dve_last_stats(dve, NBLK - 1)
                dve_last_shift(dve, NBLK - 1)
                for n in (NBLK - 2, NBLK - 1):
                    dve_last_max(dve, n)

            @block.tensor
            def _(pe):
                for part in range(6):
                    pe_front(pe, 0, part)
                for c in range(2):
                    pe_scores(pe, 0, 0, 0, c)
                each_block(pe, pe_block)
                for part in range(4):
                    pe_back(pe, NBLK - 1, part)


def quantized_ffn(nc, g, w, out):
    with ExitStack() as ctx:
        sb = lambda name, shape, dt: ctx.enter_context(nc.sbuf_tensor(name, shape, dt))
        pb = lambda name: ctx.enter_context(nc.psum_tensor(name, [P, 512], F32))
        bias = sb("ffn_bias", [P, D], F32)
        amax, limit, scale_row = ffn_scale_buffers(sb, "x")
        scales, dequant = sb("scales", [P, 2], F32), sb("dequant", [P, 1], F32)
        floor = sb("floor", [P, 1], F32)
        v = [sb(f"ffn_v{s}", [P, TJ, D], F32) for s in range(3)]
        e = [sb(f"ffn_e{s}", [P, TJ, D], F32) for s in range(2)]
        qT = [sb(f"ffn_qT{s}", [P, DC, TB], BF16) for s in range(2)]
        z = [sb(f"ffn_z{s}", [P, TJ, D], BF16) for s in range(2)]
        tr = [pb(f"ffn_tr{s}") for s in range(2)]
        acc = [pb(f"ffn_acc{s}") for s in range(4)]
        small = pb("ffn_small")
        names = ("bias_in", "amax_done", "small_mm", "limit_done", "v_ready", "e_ready", "m_ready", "t_done", "q_ready",
                 "tr_mm", "qT_out", "mm", "z_out", "x_done", "stored")
        s = {n: ctx.enter_context(nc.semaphore(n + "4")) for n in names}

        def x_values(tile, n):
            return tile[:, n, :, :].rearrange("p j d -> p (j d)")

        def values(tile):
            return tile[:, :, :].rearrange("p j d -> p (j d)")

        with nc.Block() as block:
            @block.sync
            def _(sp):
                sp.dma_start(bias[:, :], w["L1_ffn_bias"].partition_broadcast(P)).then_inc(s["bias_in"], 16)
                out_blocks = out.rearrange("b (n p j) d -> p (b n) j d", p=P, j=TJ)
                for n in range(NBLK):
                    sp.wait_ge(s["x_done"], n + 1)
                    sp.dma_start(out_blocks[:, n, :, :], g["x"][:, n, :, :]).then_inc(s["stored"], 16)
                sp.wait_ge(s["stored"], 16 * NBLK)

            @block.scalar
            def _(act):
                def scaled(n):
                    if n >= 3:
                        act.wait_ge(s["tr_mm"], DC * (n - 2))
                    act.activation(values(v[n % 3]), x_values(g["xf"], n), ACT.Copy, scale=scales[:, 0:1]).then_inc(s["v_ready"], 1)

                def round_at(n):
                    act.wait_ge(s["e_ready"], n + 1)
                    act.activation(values(e[n % 2]), values(e[n % 2]), ACT.Relu, scale=ROUND_AT, bias=floor[:, 0:1]).then_inc(s["m_ready"], 1)

                def copy_qT(n):
                    if n >= 2:
                        act.wait_ge(s["mm"], 2 * n - 2)
                    for dc in range(DC):
                        act.wait_ge(s["tr_mm"], DC * n + dc + 1)
                        act.activation(qT[n % 2][:, dc, :], tr[dc][:, :], ACT.Copy).then_inc(s["qT_out"], 1)

                act.wait_ge(s["limit_done"], 8)
                scaled(0)
                round_at(0)
                scaled(1)
                for n in range(NBLK):
                    if n + 1 < NBLK:
                        round_at(n + 1)
                    if n + 2 < NBLK:
                        scaled(n + 2)
                    copy_qT(n)

            @block.vector
            def _(dve):
                dve.tensor_reduce(amax[:, 0:1], g["xf_max"][:, :], AX_X, ALU.max).then_inc(s["amax_done"], 1)
                dve.memset(floor[:, :], -ROUND_AT * FP8_MIN_NORMAL)
                dve.wait_ge(s["small_mm"], 1)
                ffn_scales(dve, limit, scale_row, small[0:1, 0:P], s["limit_done"])
                dve.wait_ge(s["small_mm"], 2)
                dve.tensor_copy(scales[:, :], small[:, P:P + 2]).then_inc(s["limit_done"], 1)
                dve.wait_ge(s["limit_done"], 7)
                dve.scalar_tensor_tensor(dequant[:, :], scales[:, 1:2], -1.0, g["ffn_w_scales"][:, 1:2], ALU.mult, ALU.mult).then_inc(s["limit_done"], 1)
                dve.wait_ge(s["bias_in"], 16)

                def power(n):
                    dve.wait_ge(s["v_ready"], n + 1)
                    if n >= 2:
                        dve.wait_ge(s["q_ready"], n - 1)
                    dve.tensor_scalar(values(e[n % 2]).bitcast(I32), values(v[n % 3]).bitcast(I32), EXPONENT_BITS, None,
                                      ALU.bitwise_and).then_inc(s["e_ready"], 1)

                def rounded(n):
                    dve.wait_ge(s["m_ready"], n + 1)
                    dve.scalar_tensor_tensor(values(v[n % 3]), values(e[n % 2]), ROUND_AT * FP8_MIN_NORMAL, values(v[n % 3]),
                                             ALU.add, ALU.add).then_inc(s["t_done"], 1)
                    dve.wait_ge(s["t_done"], n + 1)
                    dve.scalar_tensor_tensor(values(v[n % 3]), values(e[n % 2]), ROUND_AT * FP8_MIN_NORMAL, values(v[n % 3]),
                                             ALU.add, ALU.subtract).then_inc(s["q_ready"], 1)

                def finish(n):
                    if n >= 2:
                        dve.wait_ge(s["x_done"], n - 1)
                    for a in range(2):
                        dve.wait_ge(s["mm"], 2 * n + a + 1)
                        for b in range(2):
                            last = dve.scalar_tensor_tensor(z[n % 2][:, 2 * a + b, :], acc[2 * (n % 2) + a][:, b * D:(b + 1) * D],
                                                            dequant[:, 0:1], bias[:, :], ALU.mult, ALU.add)
                        last.then_inc(s["z_out"], 1)

                power(0)
                for n in range(NBLK + 1):
                    if n + 1 < NBLK:
                        power(n + 1)
                    if n < NBLK:
                        rounded(n)
                    if n >= 1:
                        finish(n - 1)

            @block.gpsimd
            def _(gp):
                for n in range(NBLK):
                    gp.wait_ge(s["z_out"], 2 * n + 2)
                    gp.tensor_tensor(g["x"][:, n, :, :], g["x"][:, n, :, :], z[n % 2][:, :, :], ALU.add).then_inc(s["x_done"], 1)

            @block.tensor
            def _(pe):
                pe.wait_ge(s["amax_done"], 1)
                ffn_transpose_amax(pe, g, small, amax, s["small_mm"])
                pe.wait_ge(s["limit_done"], 6)
                ffn_spread_scales(pe, g, small, scale_row, s["small_mm"])

                def transposes(n):
                    pe.wait_ge(s["q_ready"], n + 1)
                    for dc in range(DC):
                        if n >= 1:
                            pe.wait_ge(s["qT_out"], DC * (n - 1) + dc + 1)
                        for j in range(TJ):
                            last = pe.transpose(tr[dc][:, j * P:(j + 1) * P], v[n % 3][:, j, dc * P:(dc + 1) * P], g["ident"][:, :])
                        last.then_inc(s["tr_mm"], 1)

                def products(n):
                    pe.wait_ge(s["qT_out"], DC * (n + 1))
                    if n >= 2:
                        pe.wait_ge(s["z_out"], 2 * n - 2)
                    for a in range(2):
                        for b in range(2):
                            j = 2 * a + b
                            for dc in range(DC):
                                last = pe.matmul(acc[2 * (n % 2) + a][:, b * D:(b + 1) * D], qT[n % 2][:, dc, j * P:(j + 1) * P],
                                                 g["ffn_wqT"][:, dc, :], start=(dc == 0), stop=(dc == DC - 1))
                        last.then_inc(s["mm"], 1)

                for n in range(NBLK + 1):
                    if n >= 1:
                        products(n - 1)
                    if n < NBLK:
                        transposes(n)


def program(nc, w, out):
    with ExitStack() as ctx:
        g = {}
        sb = lambda name, shape, dt: ctx.enter_context(nc.sbuf_tensor(name, shape, dt))
        g["x"] = sb("x_res", [P, NBLK, TJ, D], F32)
        g["ident"] = sb("ident", [P, P], F32)
        g["minus_half"] = sb("minus_half", [P, TJ], F32)
        g["eps"] = sb("eps", [P, TJ], F32)
        g["half"] = sb("half", [P, TJ], F32)
        g["ffn_wqT"], g["ffn_w_scales"] = sb("ffn_wqT", [P, DC, D], BF16), sb("ffn_w_scales", [P, 2], F32)
        with ExitStack() as weights0:
            attention0_weights(nc, g, w, weights0)
            attention0(nc, g)
        weight_rows = nc.dram_tensor("weight_rows", (E, TB), F32, kind="Internal").ap()
        with ExitStack() as weights1:
            experts_weights(nc, g, w, weights1)
            experts(nc, g, weight_rows)
        g["xf"] = sb("xf", [P, NBLK, TJ, D], F32)
        g["xf_max"] = sb("xf_max", [P, NBLK], F32)
        with ExitStack() as weights3:
            attention1_weights(nc, g, w, weights3)
            attention1(nc, g)
        quantized_ffn(nc, g, w, out)


INPUTS = ['x', 'ctx_768', 'L0_xattn_Wq', 'L0_xattn_Wk', 'L0_xattn_Wv', 'L0_xattn_Wo', 'L0_xattn_bo', 'L0_ffn_gate_w',
          'L0_ffn_W1', 'L0_ffn_W2', 'L0_ffn_Ws1', 'L0_ffn_Ws2', 'L1_xattn_Wq', 'L1_xattn_bq', 'L1_xattn_Wk', 'L1_xattn_bk',
          'L1_xattn_Wv', 'L1_xattn_bv', 'L1_xattn_Wo', 'L1_xattn_bo', 'L1_xattn_ln_gamma', 'L1_xattn_ln_beta',
          'L1_ffn_weight', 'L1_ffn_bias']


def kernel(**inputs):
    import numpy as np
    import concourse.bacc as bacc
    from concourse.bass_utils import run_bass_kernel_spmd

    nc = bacc.Bacc("TRN2", target_bir_lowering=False, num_devices=1)
    arrays, views = {}, {}
    for name in INPUTS:
        a = np.ascontiguousarray(inputs[name])
        arrays["in_" + name] = a
        views[name] = nc.dram_tensor("in_" + name, a.shape, mybir.dt.from_np(a.dtype), kind="ExternalInput").ap()
    out = nc.dram_tensor("out", (B, N, D), F32, kind="ExternalOutput").ap()
    program(nc, views, out)
    r = run_bass_kernel_spmd(nc, [arrays], core_ids=[0])
    return r.results[0]["out"]
```
